# Optimizing a Trainium2 kernel written in Bass

```python
import numpy as np
import jax
import jax.numpy as jnp

def _softmax(x, axis=-1):
    return jax.nn.softmax(x, axis=axis)

def _gelu(x):
    return jax.nn.gelu(x, approximate=True)

def _silu(x):
    return jax.nn.silu(x)

def _sigmoid(x):
    return jax.nn.sigmoid(x)

def _layernorm(x, axis=-1, eps=1e-05):
    m = jnp.mean(x, axis=axis, keepdims=True)
    v = jnp.var(x, axis=axis, keepdims=True)
    return (x - m) / jnp.sqrt(v + eps)

def _scatter_add(tgt, idx, src, axis=0):
    return tgt.at[idx].add(src)

def _segment_sum(src, seg, n):
    return jax.ops.segment_sum(src, seg, n)
kernel_name = 'mk_seq_postln_d2_jaxref_r4_3b41f1'

def setup_inputs(seed: int=0):
    np.random.seed(seed)
    _w = jnp.asarray

    def _L0_attn_setup():
        import jax, jax.numpy as jnp
        import numpy as np
        B, S, H, HS, BLK = (4, 1024, 16, 256, 64)
        D = HS // H
        key = jax.random.key(seed)
        ks = jax.random.split(key, 7)
        s = np.float32(1.0 / np.sqrt(HS))
        return {'hidden_states': jax.random.normal(ks[0], (B, S, HS), jnp.float32), 'Wq': jax.random.normal(ks[1], (HS, HS), jnp.float32) * s, 'bq': jax.random.normal(ks[2], (HS,), jnp.float32) * s, 'Wk': jax.random.normal(ks[3], (HS, HS), jnp.float32) * s, 'bk': jax.random.normal(ks[4], (HS,), jnp.float32) * s, 'Wv': jax.random.normal(ks[5], (HS, HS), jnp.float32) * s, 'bv': jax.random.normal(ks[6], (HS,), jnp.float32) * s}
    _L0_attn_in = _L0_attn_setup()

    def _L0_ffn_setup():
        import jax, jax.numpy as jnp
        import numpy as np
        TOP_K = 2

        def _gelu(x):
            return jax.nn.gelu(x, approximate=False)
        key = jax.random.key(seed)
        ks = jax.random.split(key, 6)
        B, S, D, F, E = (2, 512, 256, 512, 8)
        sc_g = 1.0 / np.sqrt(D)

        def xav(k, shape, fan_in, fan_out):
            lim = np.sqrt(6.0 / (fan_in + fan_out))
            return jax.random.uniform(k, shape, jnp.float32, -lim, lim)
        return {'x': jax.random.normal(ks[0], (B, S, D), jnp.float32), 'Wg': xav(ks[1], (D, E), D, E), 'Wu': xav(ks[2], (E, D, F), D, F), 'Wd': xav(ks[3], (E, F, D), F, D), 'W1': xav(ks[4], (D, F), D, F), 'W2': xav(ks[5], (F, D), F, D)}
    _L0_ffn_in = _L0_ffn_setup()

    def _L1_attn_setup():
        import jax, jax.numpy as jnp
        import numpy as np
        EPS = 1e-06

        def _rms(x):
            return x * jax.lax.rsqrt(jnp.mean(x * x, axis=-1, keepdims=True) + EPS)
        key = jax.random.key(seed)
        ks = jax.random.split(key, 10)
        B, S, D, MULT = (4, 1024, 256, 4)
        H = MULT * D

        def w(k, shape, s=0.02):
            return jax.random.normal(k, shape, jnp.float32) * s
        return {'x': jax.random.normal(ks[0], (B, S, D), jnp.float32), 'Wk': w(ks[1], (D, D)), 'Wv': w(ks[2], (D, D)), 'Wr': w(ks[3], (D, D)), 'Wo': w(ks[4], (D, D)), 'time_decay': jax.random.normal(ks[5], (D,), jnp.float32) * 0.01 - 5.0, 'time_first': jax.random.normal(ks[6], (D,), jnp.float32) * 0.01, 'mixer_scale': jnp.ones((D,), jnp.float32), 'Wfc': w(ks[7], (H, D)), 'Wmlp': w(ks[8], (D, H)), 'mlp_scale': jnp.ones((D,), jnp.float32)}
    _L1_attn_in = _L1_attn_setup()

    def _L1_ffn_setup():
        import jax, jax.numpy as jnp
        import numpy as np
        D = 256
        H = 1024
        E = 8
        TOPK = 2
        CAP_F = 1.25
        key = jax.random.key(seed)
        ks = jax.random.split(key, 6)
        sc = 0.02
        return {'x': jax.random.normal(ks[0], (4, 512, D), jnp.float32), 'Wg': jax.random.normal(ks[1], (D, E), jnp.float32) * sc, 'bg': jnp.zeros((E,), jnp.float32), 'W1': jax.random.normal(ks[2], (E, D, H), jnp.float32) * sc, 'W2': jax.random.normal(ks[3], (E, D, H), jnp.float32) * sc, 'W3': jax.random.normal(ks[4], (E, H, D), jnp.float32) * sc}
    _L1_ffn_in = _L1_ffn_setup()
    _d = {'L0_attn_hidden_states': _L0_attn_in['hidden_states'], 'L0_attn_Wq': _L0_attn_in['Wq'], 'L0_attn_bq': _L0_attn_in['bq'], 'L0_attn_Wk': _L0_attn_in['Wk'], 'L0_attn_bk': _L0_attn_in['bk'], 'L0_attn_Wv': _L0_attn_in['Wv'], 'L0_attn_bv': _L0_attn_in['bv'], 'L0_ffn_Wg': _L0_ffn_in['Wg'], 'L0_ffn_Wu': _L0_ffn_in['Wu'], 'L0_ffn_Wd': _L0_ffn_in['Wd'], 'L0_ffn_W1': _L0_ffn_in['W1'], 'L0_ffn_W2': _L0_ffn_in['W2'], 'L1_attn_Wk': _L1_attn_in['Wk'], 'L1_attn_Wv': _L1_attn_in['Wv'], 'L1_attn_Wr': _L1_attn_in['Wr'], 'L1_attn_Wo': _L1_attn_in['Wo'], 'L1_attn_time_decay': _L1_attn_in['time_decay'], 'L1_attn_time_first': _L1_attn_in['time_first'], 'L1_attn_mixer_scale': _L1_attn_in['mixer_scale'], 'L1_attn_Wfc': _L1_attn_in['Wfc'], 'L1_attn_Wmlp': _L1_attn_in['Wmlp'], 'L1_attn_mlp_scale': _L1_attn_in['mlp_scale'], 'L1_ffn_Wg': _L1_ffn_in['Wg'], 'L1_ffn_bg': _L1_ffn_in['bg'], 'L1_ffn_W1': _L1_ffn_in['W1'], 'L1_ffn_W2': _L1_ffn_in['W2'], 'L1_ffn_W3': _L1_ffn_in['W3']}
    _x0 = _d['L0_attn_hidden_states']
    _d['L0_attn_hidden_states'] = jax.random.normal(jax.random.fold_in(jax.random.key(seed), 1), (1, 4096, 256), dtype=_x0.dtype)
    del _x0
    return _d

def reference(L0_attn_hidden_states, L0_attn_Wq, L0_attn_bq, L0_attn_Wk, L0_attn_bk, L0_attn_Wv, L0_attn_bv, L0_ffn_Wg, L0_ffn_Wu, L0_ffn_Wd, L0_ffn_W1, L0_ffn_W2, L1_attn_Wk, L1_attn_Wv, L1_attn_Wr, L1_attn_Wo, L1_attn_time_decay, L1_attn_time_first, L1_attn_mixer_scale, L1_attn_Wfc, L1_attn_Wmlp, L1_attn_mlp_scale, L1_ffn_Wg, L1_ffn_bg, L1_ffn_W1, L1_ffn_W2, L1_ffn_W3):

    def _L0_attn_ref(hidden_states, Wq, bq, Wk, bk, Wv, bv):
        import jax, jax.numpy as jnp
        import numpy as np
        B, S, H, HS, BLK = (4, 1024, 16, 256, 64)
        D = HS // H
        b, m, _ = hidden_states.shape
        h, d, wm = (H, D, BLK)
        wn = wm
        nb = m // wm
        scale = np.float32(1.0 / np.sqrt(d))

        def heads(x):
            return x.reshape(b, m, h, d).transpose(0, 2, 1, 3)
        q = heads(hidden_states @ Wq.T + bq)
        k = heads(hidden_states @ Wk.T + bk)
        v = heads(hidden_states @ Wv.T + bv)
        qb = q.reshape(b, h, nb, wm, d)
        kb = k.reshape(b, h, nb, wn, d)
        vb = v.reshape(b, h, nb, wn, d)

        def attend(qx, kx, vx):
            scores = jnp.einsum('bhqd,bhkd->bhqk', qx, kx) * scale
            return jnp.einsum('bhqk,bhkd->bhqd', jax.nn.softmax(scores, axis=-1), vx)
        first_ctx = attend(qb[:, :, 0], k, v)[:, :, None]
        k2 = jnp.concatenate([kb[:, :, 0], kb[:, :, 1], kb[:, :, 2], kb[:, :, -1]], axis=2)
        v2 = jnp.concatenate([vb[:, :, 0], vb[:, :, 1], vb[:, :, 2], vb[:, :, -1]], axis=2)
        second_ctx = attend(qb[:, :, 1], k2, v2)[:, :, None]
        exp_k = jnp.concatenate([kb[:, :, 1:-3], kb[:, :, 2:-2], kb[:, :, 3:-1]], axis=3)
        exp_v = jnp.concatenate([vb[:, :, 1:-3], vb[:, :, 2:-2], vb[:, :, 3:-1]], axis=3)
        mq = qb[:, :, 2:-2]
        inner = jnp.einsum('bhlqd,bhlkd->bhlqk', mq, exp_k) * scale
        first_band = jnp.einsum('bhlqd,bhkd->bhlqk', mq, kb[:, :, 0]) * scale
        last_band = jnp.einsum('bhlqd,bhkd->bhlqk', mq, kb[:, :, -1]) * scale
        band = jnp.concatenate([first_band, inner, last_band], axis=-1)
        aw = jax.nn.softmax(band, axis=-1)
        mid_ctx = jnp.einsum('bhlqk,bhlkd->bhlqd', aw[..., wn:4 * wn], exp_v)
        mid_ctx = mid_ctx + jnp.einsum('bhlqk,bhkd->bhlqd', aw[..., :wn], vb[:, :, 0])
        mid_ctx = mid_ctx + jnp.einsum('bhlqk,bhkd->bhlqd', aw[..., -wn:], vb[:, :, -1])
        k3 = jnp.concatenate([kb[:, :, 0], kb[:, :, -3], kb[:, :, -2], kb[:, :, -1]], axis=2)
        v3 = jnp.concatenate([vb[:, :, 0], vb[:, :, -3], vb[:, :, -2], vb[:, :, -1]], axis=2)
        second_last_ctx = attend(qb[:, :, -2], k3, v3)[:, :, None]
        last_ctx = attend(qb[:, :, -1], k, v)[:, :, None]
        ctx = jnp.concatenate([first_ctx, second_ctx, mid_ctx, second_last_ctx, last_ctx], axis=2)
        return ctx.reshape(b, h, m, d).transpose(0, 2, 1, 3).reshape(b, m, h * d)

    def _L0_ffn_ref(x, Wg, Wu, Wd, W1, W2):
        import jax, jax.numpy as jnp
        import numpy as np
        TOP_K = 2

        def _gelu(x):
            return jax.nn.gelu(x, approximate=False)
        B, S, D = x.shape
        E = Wu.shape[0]
        T = B * S
        xt = x.reshape(T, D)
        probs = jax.nn.softmax(xt @ Wg, axis=-1)
        topv, topi = jax.lax.top_k(probs, TOP_K)
        topv = topv / jnp.sum(topv, axis=-1, keepdims=True)
        cw = jnp.zeros((T, E), x.dtype).at[jnp.arange(T)[:, None], topi].set(topv)
        h = _gelu(jnp.einsum('td,edf->tef', xt, Wu))
        y = jnp.einsum('tef,efd->ted', h, Wd)
        moe = jnp.einsum('ted,te->td', y, cw)
        shared = _gelu(xt @ W1) @ W2
        return (shared + moe).reshape(B, S, D)

    def _L1_attn_ref(x, Wk, Wv, Wr, Wo, time_decay, time_first, mixer_scale, Wfc, Wmlp, mlp_scale):
        import jax, jax.numpy as jnp
        import numpy as np
        EPS = 1e-06

        def _rms(x):
            return x * jax.lax.rsqrt(jnp.mean(x * x, axis=-1, keepdims=True) + EPS)
        normed = _rms(x)
        k = normed @ Wk.T
        v = normed @ Wv.T
        r = jax.nn.sigmoid(normed @ Wr.T)
        ew = jnp.exp(-jnp.exp(time_decay))
        eu = jnp.exp(time_first)
        kv = (k * v).transpose(1, 0, 2)
        state0 = jnp.zeros((x.shape[0], x.shape[2]), x.dtype)

        def step(state, kvt):
            wkv = state + eu * kvt
            return (ew * state + kvt, wkv)
        _, wkv = jax.lax.scan(step, state0, kv)
        mixer_out = r * wkv.transpose(1, 0, 2) @ Wo.T
        x = x + mixer_scale[None, None, :] * mixer_out
        h = jax.nn.leaky_relu(_rms(x) @ Wfc.T, negative_slope=0.5)
        x = x + mlp_scale[None, None, :] * (h * h @ Wmlp.T)
        return x

    def _L1_ffn_ref(x, Wg, bg, W1, W2, W3):
        import jax, jax.numpy as jnp
        import numpy as np
        D = 256
        H = 1024
        E = 8
        TOPK = 2
        CAP_F = 1.25
        b, s, d = x.shape
        xt = x.reshape(-1, d)
        T = xt.shape[0]
        capacity = int(T / E * CAP_F)
        gate_logits = xt @ Wg + bg
        top_v, top_i = jax.lax.top_k(gate_logits, TOPK)
        expert_label = jax.nn.one_hot(top_i, E, dtype=xt.dtype).sum(axis=1)
        seq = jnp.cumsum(expert_label, axis=0) * expert_label
        valid = (seq > 0) & (seq <= capacity)
        slot = (seq - 1.0).astype(jnp.int32)
        flat_idx = jnp.where(valid, jnp.arange(E, dtype=jnp.int32)[None, :] * capacity + slot, E * capacity)
        src = jnp.broadcast_to(xt[:, None, :], (T, E, d)).reshape(-1, d)
        buf = jnp.zeros((E * capacity + 1, d), xt.dtype).at[flat_idx.reshape(-1)].set(src)
        disp = buf[:-1].reshape(E, capacity, d)
        h = jax.nn.silu(jnp.einsum('ecd,edh->ech', disp, W1)) * jnp.einsum('ecd,edh->ech', disp, W2)
        out = jnp.einsum('ech,ehd->ecd', h, W3)
        out_flat = jnp.concatenate([out.reshape(E * capacity, d), jnp.zeros((1, d), xt.dtype)], axis=0)
        all_expert_output = out_flat[flat_idx]
        sel = jnp.take_along_axis(all_expert_output, top_i[:, :, None], axis=1)
        routing_w = jax.nn.softmax(top_v, axis=-1)
        y = (routing_w[:, :, None] * sel).sum(axis=1)
        return y.reshape(b, s, d)
    x = L0_attn_hidden_states
    x = _layernorm(x + _L0_attn_ref(x, L0_attn_Wq, L0_attn_bq, L0_attn_Wk, L0_attn_bk, L0_attn_Wv, L0_attn_bv), axis=-1)
    x = _layernorm(x + _L0_ffn_ref(x, L0_ffn_Wg, L0_ffn_Wu, L0_ffn_Wd, L0_ffn_W1, L0_ffn_W2), axis=-1)
    x = _layernorm(x + _L1_attn_ref(x, L1_attn_Wk, L1_attn_Wv, L1_attn_Wr, L1_attn_Wo, L1_attn_time_decay, L1_attn_time_first, L1_attn_mixer_scale, L1_attn_Wfc, L1_attn_Wmlp, L1_attn_mlp_scale), axis=-1)
    x = _layernorm(x + _L1_ffn_ref(x, L1_ffn_Wg, L1_ffn_bg, L1_ffn_W1, L1_ffn_W2, L1_ffn_W3), axis=-1)
    return x

_drawn_inputs = setup_inputs


def setup_inputs(seed=0):
    import zlib

    import numpy as np

    out = dict(_drawn_inputs(seed))
    spreads = {'L1_attn_mixer_scale': (1.0, 0.563),
     'L1_attn_mlp_scale': (1.0, 0.6),
     'L1_ffn_bg': (0.0, 0.637)}
    factors = {'L0_attn_bq': 2.963,
     'L0_attn_bk': 200.0,
     'L1_attn_Wr': 2.693,
     'L1_attn_time_decay': 8.0,
     'L1_attn_time_first': 130.571,
     'L1_ffn_Wg': 3.488,
     'L1_ffn_W1': 3.21,
     'L1_ffn_W2': 3.179,
     'L1_ffn_W3': 3.174}
    for name, (base, spread) in spreads.items():
        noise = np.random.default_rng([zlib.crc32(name.encode()), seed]).standard_normal(out[name].shape)
        drawn = base * np.exp(spread * noise) if base else spread * noise
        out[name] = jnp.asarray(drawn.astype(out[name].dtype))
    for name, factor in factors.items():
        out[name] = (out[name] * factor).astype(out[name].dtype)
    return out
```

```python
from contextlib import ExitStack

import concourse.bass as bass
from concourse import mybir

F32 = mybir.dt.float32
F32R = mybir.dt.float32r
I32 = mybir.dt.int32
U32 = mybir.dt.uint32
ALU = mybir.AluOpType
ACT = mybir.ActivationFunctionType
AX = mybir.AxisListType

P = 128
T = 4096
D = 256
KD = D // P
TT = T // P
GRP = 512
NGRP = T // GRP
GT = GRP // P
H, HD = 16, 16
BLK = 64
NBLK = T // BLK
PAIRS = H // 2
VW = HD + 1
E = 8
LN_EPS = 1e-5
RMS_EPS = 1e-6



taken = []


class Mem:

    def __init__(self, nc, ctx, tag):
        self.nc, self.ctx, self.tag = nc, ctx, tag

    def sb(self, name, shape, dt=F32):
        return self.ctx.enter_context(self.nc.sbuf_tensor(f"{self.tag}_{name}", shape, dt))

    def ps(self, name, shape, dt=F32):
        return self.ctx.enter_context(self.nc.psum_tensor(f"{self.tag}_{name}", shape, dt))

    def sem(self, name):
        sem = self.nc.alloc_semaphore(f"{self.tag}_{name}")
        taken.append(sem)
        return sem


def row(ap):
    return ap.rearrange("(a d) -> a d", a=1)


def token_rows(a, g):
    return a[bass.ds(g * GRP, GRP), :].rearrange("(j p) d -> p j d", p=P)


def project_qkv(nc, hsT, WqT, bq, WkT, bk, WvT, bv, qk_d, v_d):
    with ExitStack() as ctx:
        m = Mem(nc, ctx, "qkv")
        w = m.sb("w", [P, 3, KD, D])
        b_col = m.sb("b_col", [P, 2, KD])
        b_colq = m.sb("b_colq", [P, 2, KD])
        bv_row = m.sb("bv_row", [P, D])
        x = [m.sb(f"x{i}", [P, KD, GRP]) for i in range(2)]
        whole = m.sb("whole", [P, 2, GRP])
        part = [m.sb(f"part{i}", [P, 2, GRP], F32R) for i in range(2)]
        v = m.sb("v", [P, PAIRS, TT, 2, VW])
        qk_ps = [m.ps(f"qk_ps{i}", [P, GRP]) for i in range(2)]
        v_ps = [m.ps(f"v_ps{i}", [P, D]) for i in range(2)]
        weights_in, ones_set, scaled = m.sem("weights_in"), m.sem("ones_set"), m.sem("scaled")
        x_in = [m.sem(f"x_in{i}") for i in range(2)]
        qk_done, whole_done, high_done = (m.sem("qk_done"),
                                                  m.sem("whole_done"), m.sem("high_done"))
        low_done, v_done, v_copied = m.sem("low_done"), m.sem("v_done"), m.sem("v_copied")
        part_out = [m.sem(f"part_out{i}") for i in range(2)]
        v_out = m.sem("v_out")
        NW = 8 * 16
        block = ctx.enter_context(nc.Block())

        @block.sync
        def _(sp):
            for i, a in enumerate((WqT, WkT, WvT)):
                sp.dma_start(w[:, i], a.rearrange("(k p) n -> p k n", p=P)).then_inc(weights_in, 16)
            for i, a in enumerate((bq, bk)):
                for k in range(KD):
                    sp.dma_start(b_col[:, i, k:k + 1],
                                 a[k * P:(k + 1) * P].rearrange("(p a) -> p a", a=1)).then_inc(weights_in, 16)
            sp.dma_start(bv_row[:, :], row(bv).broadcast_to([P, D])).then_inc(weights_in, 16)
            src = hsT.rearrange("(k p) t -> p k t", p=P)
            with sp.Fori(0, NGRP // 2) as i:
                for s in range(2):
                    sp.wait_ge(v_done, 8 * i)
                    sp.dma_start(x[s][:, :, :], src[:, :, bass.ds(i * 2 * GRP + s * GRP, GRP)]).then_inc(x_in[s], 16)

        @block.scalar
        def _(act):
            act.wait_ge(weights_in, NW)
            act.wait_ge(scaled, 1)
            with act.Fori(0, NGRP) as i:
                for j in range(4):
                    t, g = j // 2, j % 2
                    act.wait_ge(qk_done, 4 * i + j + 1)
                    act.wait_ge(low_done, 4 * i + max(j - 1, 0))
                    nc.scalar.activation(whole[:, j % 2, :], qk_ps[j % 2][:, :], ACT.Identity,
                                         bias=b_colq[:, t, g:g + 1],
                                         scale=0.25 if t == 0 else 1.0).then_inc(whole_done, 1)

        @block.vector
        def _(dve):
            nc.vector.memset(v[:, :, :, :, HD:VW], 1.0).then_inc(ones_set, 1)
            dve.wait_ge(weights_in, NW)
            nc.vector.tensor_scalar(b_colq[:, 0, :], b_col[:, 0, :], 0.25, None, ALU.mult)
            nc.vector.tensor_copy(b_colq[:, 1, :], b_col[:, 1, :]).then_inc(scaled, 1)
            with dve.Fori(0, NGRP) as i:
                for j in range(4):
                    s = j % 2
                    dve.wait_ge(whole_done, 4 * i + j + 1)
                    dve.wait_ge(part_out[s], 32 * 2 * i + 32 * (j // 2))
                    nc.vector.tensor_copy(part[s][:, 0, :], whole[:, s, :]).then_inc(high_done, 1)
                    dve.wait_ge(high_done, 4 * i + j + 1)
                    nc.vector.tensor_tensor(part[s][:, 1, :], whole[:, s, :], part[s][:, 0, :].bitcast(F32),
                                            ALU.subtract).then_inc(low_done, 1)
                    dve.wait_ge(v_done, 4 * i + j + 1)
                    nc.vector.tensor_tensor(
                        v[:, :, bass.ds(4 * i + j, 1), :, 0:HD].rearrange("p h t a d -> p (h t) a d"),
                        v_ps[s][:, :].rearrange("p (a h d) -> p h a d", a=2, d=HD),
                        bv_row[:, :].rearrange("p (a h d) -> p h a d", a=2, d=HD), ALU.add).then_inc(v_copied, 1)

        @block.tensor
        def _(pe):
            pe.wait_ge(weights_in, NW)
            with pe.Fori(0, NGRP // 2) as i2:
                for s in range(2):
                    i = 2 * i2 + s
                    pe.wait_ge(x_in[s], 16 * i2 + 16)
                    for j in range(4):
                        t, g = j // 2, j % 2
                        pe.wait_ge(whole_done, 4 * i + max(j - 1, 0))
                        for k in range(KD):
                            mm = nc.tensor.matmul(qk_ps[j % 2][:, :], w[:, t, k, g * P:(g + 1) * P], x[s][:, k, :],
                                                  start=(k == 0), stop=(k == KD - 1))
                        mm.then_inc(qk_done, 1)
                        pe.wait_ge(v_copied, 4 * i + max(j - 1, 0))
                        for k in range(KD):
                            mm = nc.tensor.matmul(v_ps[j % 2][:, :], x[s][:, k, j * P:(j + 1) * P], w[:, 2, k, :],
                                                  start=(k == 0), stop=(k == KD - 1))
                        mm.then_inc(v_done, 1)


        @block.gpsimd
        def _(pool):
            dst = qk_d.rearrange("t h (g p) n -> p t h g n", p=P)
            with pool.Fori(0, NGRP) as i:
                for j in range(4):
                    t, g = j // 2, j % 2
                    pool.wait_ge(low_done, 4 * i + j + 1)
                    for h in range(2):
                        pool.dma_start(dst[:, t, h, g, bass.ds(i * GRP, GRP)], part[j % 2][:, h, :].bitcast(F32)).then_inc(part_out[j % 2], 16)
            pool.wait_ge(v_copied, TT)
            pool.wait_ge(ones_set, 1)
            pool.dma_start(v_d.rearrange("h p t v -> p h t v"),
                           v[:, :, :, :, :].rearrange("p h t a v -> p h t (a v)")).then_inc(v_out, 16)
            pool.wait_ge(v_out, 16)
            for s in range(2):
                pool.wait_ge(part_out[s], 32 * 2 * NGRP)


def attend(nc, qk_d, v_d, ident, ctx_d, sums_d):
    FULL = 16
    BAND = (NBLK - 2) // 2
    STEPS = FULL + BAND
    UNITS = FULL + 2 * BAND
    LEAD = 3
    WARM = 12
    ROWS, MROW = 97, 96
    CHUNKS = 4
    CB = NBLK // CHUNKS
    CT = T // CHUNKS
    LOCAL = 3 * BLK
    with ExitStack() as ctx:
        m = Mem(nc, ctx, "att")
        q = [m.sb(f"q{i}", [P, NBLK, 2 * BLK], F32R) for i in range(2)]
        k = [m.sb(f"k{i}", [P, T + BLK], F32R) for i in range(2)]
        kgm = [m.sb(f"kgm{i}", [P, 2 * BLK], F32R) for i in range(2)]
        kg = [m.sb(f"kg{i}", [P, 2 * BLK], F32R) for i in range(2)]
        ve = [m.sb(f"ve{i}", [P, TT, 2 * VW]) for i in range(2)]
        vo = [m.sb(f"vo{i}", [P, TT, 2 * VW]) for i in range(2)]
        vg = [m.sb(f"vg{i}", [P, 3, 2 * VW]) for i in range(2)]
        neg_max = m.sb("neg_max", [P, NBLK])
        chunk_max = m.sb("chunk_max", [P, 2, FULL // 2])
        max_row = m.sb("max_row", [NBLK, P], F32R)
        prob = [m.sb(f"prob{i}", [P, 4 * P]) for i in range(2)]
        prob_c = [m.sb(f"prob_c{i}", [BLK, 2 * P]) for i in range(2)]
        raw = [m.sb(f"raw{i}", [2 * VW, NBLK, 2 * BLK]) for i in range(2)]
        m_ps = [m.ps(f"m_ps{i}", [P, 512]) for i in range(2)]
        s_ps = [m.ps(f"s_ps{i}", [P, 512]) for i in range(2)]
        c_ps = [m.ps(f"c_ps{i}", [P, 2 * P]) for i in range(2)]
        o_ps = [m.ps(f"o_ps{i}", [P, 512]) for i in range(2)]
        qk_in = [m.sem(f"qk_in{c}") for c in range(CHUNKS)]
        kg_in, v_in, cleared = m.sem("kg_in"), m.sem("v_in"), m.sem("cleared")
        globals_ready = m.sem("globals_ready")
        m_done, m_reduced, max_ready = m.sem("m_done"), m.sem("m_reduced"), m.sem("max_ready")
        row_turned, row_ready, row_in = m.sem("row_turned"), m.sem("row_ready"), m.sem("row_in")
        s_done, exp_done, pv_done, o_out = m.sem("s_done"), m.sem("exp_done"), m.sem("pv_done"), m.sem("o_out")
        raw_out = [m.sem(f"raw_out{i}") for i in range(2)]
        passed = m.sem("passed")
        block = ctx.enter_context(nc.Block())

        def rounds(eng, one):
            one(0, None, 0)
            with eng.Fori(0, PAIRS // 2 - 1) as j:
                one(2 * j + 1, 2 * j, 1)
                one(2 * j + 2, 2 * j + 1, 0)
            one(PAIRS - 1, PAIRS - 2, 1)
            one(None, PAIRS - 1, 0)

        def m_units(s):
            return [2 * s, 2 * s + 1] if s < BAND else [BAND + s]

        def m_stream(p, b):
            steps = [] if p is None else [(p, b, s) for s in range(LEAD, STEPS)]
            if p is not None and b_next(p):
                steps += [(p + 1, 1 - b, s) for s in range(LEAD)]
            return steps

        def b_next(p):
            return not (isinstance(p, int) and p == PAIRS - 1)

        @block.sync
        def _(sp):
            qk = qk_d.rearrange("t h (a f) n -> t h a f n", a=2)

            def head(p, t, h, a):
                return qk[t, h, a, bass.ds(p * HD, HD), :]

            def load_globals(p, b):
                for a in range(2):
                    for i, h in enumerate((0, 1, 0)):
                        r = 48 * a + 16 * i
                        sp.dma_start(kgm[b][r:r + HD, :].rearrange("f (g t) -> f g t", g=2).bitcast(F32),
                                     head(p, 1, h, a).rearrange("f (l t) -> f l t", t=BLK)[:, 0:NBLK:NBLK - 1, :]
                                     ).then_inc(kg_in, 16)

            def load_chunk(p, b, c):
                for a in range(2):
                    for i, (hq, hk) in enumerate(((0, 0), (0, 1), (1, 0))):
                        r = 48 * a + 16 * i
                        sp.dma_start(q[b][r:r + HD, c * CB:(c + 1) * CB, a * BLK:(a + 1) * BLK].bitcast(F32),
                                     head(p, 0, hq, a)[:, c * CT:(c + 1) * CT].rearrange("f (l t) -> f l t", t=BLK)
                                     ).then_inc(qk_in[c], 16)
                        sp.dma_start(k[b][r:r + HD, c * CT:(c + 1) * CT].bitcast(F32),
                                     head(p, 1, hk, a)[:, c * CT:(c + 1) * CT]).then_inc(qk_in[c], 16)

            def load_values(p, b):
                vp = v_d[bass.ds(p, 1)].rearrange("h p t v -> (h p) t v")
                sp.dma_start(ve[b][:, :, :], vp).then_inc(v_in, 16)
                sp.dma_start(vo[b][0:BLK, :, :], vp[BLK:P]).then_inc(v_in, 16)
                sp.dma_start(vo[b][BLK:P, 0:TT - 1, :], vp[0:BLK, 1:TT]).then_inc(v_in, 16)

            sp.wait_ge(cleared, 1)
            for p in range(2):
                load_globals(p, p)
                for c in range(CHUNKS):
                    load_chunk(p, p, c)
                    sp.wait_ge(qk_in[c], 192 * (p + 1))
                load_values(p, p)
                sp.wait_ge(kg_in, 96 * (p + 1))
                sp.wait_ge(v_in, 48 * (p + 1))

            def refill(p, b):
                load_globals(p + 1, 1 - b)
                for c in range(CHUNKS):
                    sp.wait_ge(s_done, (p - 1) * STEPS + FULL + min(CB // 2 * (c + 1), BAND))
                    sp.sem_inc(passed, 1)
                    load_chunk(p + 1, 1 - b, c)
                sp.wait_ge(pv_done, p * STEPS)
                load_values(p + 1, 1 - b)

            with sp.Fori(0, PAIRS // 2 - 1) as j:
                for r in range(2):
                    sp.wait_ge(globals_ready, 2 * j + 1 + r)
                    refill(2 * j + 1 + r, (1 + r) % 2)

        @block.tensor
        def _(pe):
            def maxima(p, b, s):
                if s == 0:
                    pe.wait_ge(kg_in, 96 * (p + 1))
                    pe.wait_ge(row_ready, p)
                for c in range(CHUNKS):
                    if s < BAND and (2 * s + 3) // CB == c and (s == 0 or (2 * s + 1) // CB < c):
                        pe.wait_ge(qk_in[c], 192 * (p + 1))
                for u in m_units(s):
                    pe.wait_ge(m_reduced, p * UNITS + max(u - 1, 0))
                    bank = m_ps[u % 2]
                    if u < 2 * BAND:
                        l = 1 + u
                        nc.tensor.matmul(bank[:, 0:LOCAL], q[b][0:MROW, l, :],
                                         k[b][0:MROW, (l - 1) * BLK:(l + 2) * BLK], start=True, stop=True)
                        nc.tensor.matmul(bank[:, LOCAL:LOCAL + 2 * BLK], q[b][0:MROW, l, :], kgm[b][0:MROW, :],
                                         start=True, stop=True).then_inc(m_done, 1)
                    else:
                        f = u - 2 * BAND
                        l, chunk = (0 if f < FULL // 2 else NBLK - 1), f % (FULL // 2)
                        nc.tensor.matmul(bank[:, :], q[b][0:MROW, l, :], k[b][0:MROW, chunk * 512:(chunk + 1) * 512],
                                         start=True, stop=True).then_inc(m_done, 1)

            def turn(p):
                pe.wait_ge(max_ready, p + 1)
                pe.sem_inc(passed, 1)
                nc.tensor.transpose(m_ps[0][0:NBLK, 0:P], neg_max[:, :], ident[:, :]).then_inc(row_turned, 1)

            def scores(e, c, s):
                if s == 0:
                    pe.wait_ge(row_in, 16 * (e + 1))
                if s == FULL:
                    pe.wait_ge(globals_ready, e + 1)
                pe.wait_ge(exp_done, e * STEPS + max(s - 1, 0))
                bank = s_ps[s % 2]
                if s < FULL:
                    for i in range(2):
                        t = 2 * s + i
                        for j, l in enumerate((0, NBLK - 1)):
                            o = (2 * i + j) * P
                            mm = nc.tensor.matmul(bank[:, o:o + P], k[c][0:ROWS, t * P:(t + 1) * P],
                                                  q[c][0:ROWS, l, :], start=True, stop=True)
                else:
                    l0 = 1 + 2 * (s - FULL)
                    nc.tensor.matmul(bank[:, 2 * P:4 * P], kg[c][0:ROWS, :],
                                     q[c][0:ROWS, l0:l0 + 2, :].rearrange("p l t -> p (l t)"), start=True, stop=True)
                    for j in range(2):
                        l = l0 + j
                        nc.tensor.matmul(bank[:, j * P:(j + 1) * P], k[c][0:ROWS, (l - 1) * BLK:(l + 1) * BLK],
                                         q[c][0:ROWS, l, :], start=True, stop=True)
                        mm = nc.tensor.matmul(c_ps[s % 2][:, j * P:(j + 1) * P],
                                              k[c][0:ROWS, (l + 1) * BLK:(l + 3) * BLK],
                                              q[c][0:ROWS, l, :], start=True, stop=True)
                mm.then_inc(s_done, 1)

            def values(e, c, s):
                pe.wait_ge(exp_done, e * STEPS + s + 1)
                pr, prc = prob[s % 2], prob_c[s % 2]
                if s < FULL:
                    if s == 0:
                        pe.wait_ge(v_in, 48 * (e + 1))
                        pe.wait_ge(o_out, e * (BAND + 1))
                        for _ in range(WARM):
                            nc.tensor.matmul(o_ps[0][:, :], k[c][0:MROW, 0:P], k[c][0:MROW, 0:512], start=True, stop=True)
                    for i in range(2):
                        t = 2 * s + i
                        mm = nc.tensor.matmul(o_ps[1][0:2 * VW, 0:2 * P], ve[c][:, t, :],
                                              pr[:, 2 * i * P:2 * (i + 1) * P], start=(t == 0), stop=(t == TT - 1))
                else:
                    n = s - FULL
                    pe.wait_ge(o_out, e * (BAND + 1) + max(n, 1))
                    out = o_ps[n % 2]
                    l0 = 1 + 2 * n
                    if l0 == 1:
                        parts = ((1, 0, P), (0, P, 2 * P))
                    elif l0 == NBLK - 3:
                        parts = ((0, 0, P), (2, P, 2 * P))
                    else:
                        parts = ((0, 0, 2 * P),)
                    for i, (g, x0, x1) in enumerate(parts):
                        nc.tensor.matmul(out[0:2 * VW, x0:x1], vg[c][:, g, :], pr[:, 2 * P + x0:2 * P + x1],
                                         start=(i == 0), stop=False, skip_group_check=True)
                    for j in range(2):
                        l = l0 + j
                        vl, t = (vo[c], l // 2 - 1) if l % 2 == 0 else (ve[c], (l - 1) // 2)
                        o = out[0:2 * VW, j * P:(j + 1) * P]
                        nc.tensor.matmul(o, vl[:, t, :], pr[:, j * P:(j + 1) * P], start=False, stop=False,
                                         skip_group_check=True)
                        mm = nc.tensor.matmul(o, vl[0:BLK, t + 1, :], prc[:, j * P:(j + 1) * P],
                                              start=False, stop=True, skip_group_check=True)
                mm.then_inc(pv_done, 1)

            def one(p, e, b):
                ms = m_stream(p, b)
                for s in range(STEPS):
                    if e is not None:
                        scores(e, 1 - b, s)
                    if p is not None and s == STEPS - LEAD:
                        if e is not None:
                            values(e, 1 - b, s - 1)
                        turn(p)
                    if s < len(ms):
                        maxima(*ms[s])
                    if e is not None and s > 0 and (p is None or s != STEPS - LEAD):
                        values(e, 1 - b, s - 1)
                if e is not None:
                    values(e, 1 - b, STEPS - 1)

            pe.wait_ge(cleared, 1)
            for s in range(LEAD):
                maxima(0, 0, s)
            rounds(pe, one)

        @block.scalar
        def _(act):
            def one(p, e, b):
                if e is None:
                    return
                for s in range(STEPS):
                    act.wait_ge(s_done, e * STEPS + s + 1)
                    act.wait_ge(pv_done, e * STEPS + max(s - 1, 0))
                    ins = nc.scalar.activation(prob[s % 2][:, :], s_ps[s % 2][:, :], ACT.Exp)
                    if s >= FULL:
                        ins = nc.scalar.activation(prob_c[s % 2][:, :], c_ps[s % 2][0:BLK, :], ACT.Exp)
                    ins.then_inc(exp_done, 1)
                    out(e, 1 - b, s - 2)
                out(e, 1 - b, STEPS - 2)
                out(e, 1 - b, STEPS - 1)

            def out(e, c, s):
                if s < FULL - 1:
                    return
                act.wait_ge(pv_done, e * STEPS + s + 1)
                if s == FULL - 1:
                    if not isinstance(e, int) or e > 0:
                        act.wait_ge(raw_out[c], 64 * (e // 2))
                    for j, l in enumerate((0, NBLK - 1)):
                        ins = nc.scalar.copy(raw[c][:, l, :], o_ps[1][0:2 * VW, j * P:(j + 1) * P])
                else:
                    n = s - FULL
                    ins = nc.scalar.copy(raw[c][:, 1 + 2 * n:3 + 2 * n, :].rearrange("p l t -> p (l t)"),
                                         o_ps[n % 2][0:2 * VW, 0:2 * P])
                ins.then_inc(o_out, 1)

            rounds(act, one)

        @block.vector
        def _(dve):
            for b in range(2):
                nc.vector.memset(vg[b][:, :, :].bitcast(U32), 0)
                nc.vector.memset(q[b][:, :, :].bitcast(U32), 0)
                nc.vector.memset(k[b][0:MROW, T:T + BLK].bitcast(U32), 0)
                nc.vector.memset(kgm[b][MROW:ROWS, :].bitcast(F32), 1.0)
                ins = nc.vector.memset(k[b][MROW:ROWS, :].bitcast(F32), 1.0)
            ins.then_inc(cleared, 1)

            def maximum(p, s):
                if s == 0:
                    dve.wait_ge(row_turned, p)
                for u in m_units(s):
                    dve.wait_ge(m_done, p * UNITS + u + 1)
                    if u < 2 * BAND:
                        l = 1 + u
                        ins = nc.vector.tensor_reduce(neg_max[:, l:l + 1], m_ps[u % 2][:, 0:LOCAL + 2 * BLK], AX.X,
                                                      ALU.max, negate=True)
                    else:
                        f = u - 2 * BAND
                        ins = nc.vector.tensor_reduce(chunk_max[:, f // 8, f % 8:f % 8 + 1], m_ps[u % 2][:, :],
                                                      AX.X, ALU.max)
                    ins.then_inc(m_reduced, 1)

            def close(p, b):
                dve.wait_ge(m_reduced, (p + 1) * UNITS)
                for i, l in enumerate((0, NBLK - 1)):
                    ins = nc.vector.tensor_reduce(neg_max[:, l:l + 1], chunk_max[:, i, :], AX.X, ALU.max, negate=True)
                ins.then_inc(max_ready, 1)
                dve.wait_ge(row_turned, p + 1)
                dve.wait_ge(row_in, 16 * p)
                nc.vector.tensor_copy(max_row[:, :], m_ps[0][0:NBLK, 0:P]).then_inc(row_ready, 1)
                if not isinstance(p, int) or p > 0:
                    dve.wait_ge(pv_done, (p - 1) * STEPS)
                nc.vector.tensor_copy(kg[b][0:ROWS, :], kgm[b][0:ROWS, :].bitcast(F32))
                dve.wait_ge(v_in, 48 * (p + 1))
                nc.vector.tensor_copy(vg[b][0:BLK, 0, :], ve[b][0:BLK, 0, :])
                nc.vector.tensor_copy(vg[b][0:BLK, 2, :], ve[b][0:BLK, 0, :])
                nc.vector.tensor_copy(vg[b][BLK:P, 0, :], ve[b][BLK:P, TT - 1, :])
                nc.vector.tensor_copy(vg[b][BLK:P, 1, :], ve[b][BLK:P, TT - 1, :]).then_inc(globals_ready, 1)

            def one(p, e, b):
                for pm, bm, s in m_stream(p, b):
                    maximum(pm, s)
                    if s == STEPS - 1:
                        close(pm, bm)

            for s in range(LEAD):
                maximum(0, s)
            rounds(dve, one)

        @block.gpsimd
        def _(pool):
            def one(p, e, b):
                if p is not None:
                    pool.wait_ge(row_ready, p + 1)
                    pool.sem_inc(passed, 1)
                    pool.dma_start(q[b][MROW:MROW + 1, :, :].rearrange("p l t -> p (l t)").bitcast(F32),
                                   max_row[:, :].bitcast(F32)).then_inc(row_in, 16)
                if e is not None:
                    pool.wait_ge(o_out, (e + 1) * (BAND + 1))
                    for a in range(2):
                        cols = raw[1 - b][a * VW:(a + 1) * VW, :, a * BLK:(a + 1) * BLK]
                        pool.dma_start(heads[a, bass.ds(e * HD, HD)].rearrange("f (l t) -> f l t", t=BLK),
                                       cols[0:HD]).then_inc(raw_out[1 - b], 16)
                        pool.dma_start(sums[a, bass.ds(e, 1)].rearrange("f (l t) -> f l t", t=BLK),
                                       cols[HD:VW]).then_inc(raw_out[1 - b], 16)

            heads = ctx_d.rearrange("(a f) n -> a f n", a=2)
            sums = sums_d.rearrange("(a f) n -> a f n", a=2)
            rounds(pool, one)
            for c in range(2):
                pool.wait_ge(raw_out[c], 64 * PAIRS // 2)


def merge_heads(nc, hs, ctx_d, sums_d, ident, sum_d):
    with ExitStack() as ctx:
        m = Mem(nc, ctx, "merge")
        c = [m.sb(f"c{i}", [P, KD, GRP]) for i in range(2)]
        z = [m.sb(f"z{i}", [H, GRP]) for i in range(2)]
        x = [m.sb(f"x{i}", [P, GT, D]) for i in range(2)]
        out = [m.sb(f"out{i}", [P, GT, D]) for i in range(2)]
        inv = [m.sb(f"inv{i}", [P, H]) for i in range(2)]
        scaled = [m.sb(f"scaled{i}", [P, D]) for i in range(2)]
        ps = [m.ps(f"ps{i}", [P, 512]) for i in range(2)]
        in_ = [m.sem(f"in{i}") for i in range(2)]
        out_sem = [m.sem(f"out{i}") for i in range(2)]
        turned, inverted, multiplied, added = m.sem("turned"), m.sem("inverted"), m.sem("multiplied"), m.sem("added")
        block = ctx.enter_context(nc.Block())

        @block.sync
        def _(sp):
            with sp.Fori(0, NGRP // 2) as i:
                for s in range(2):
                    g = 2 * i + s
                    sp.wait_ge(added, GT * 2 * i)
                    toks = bass.ds(g * GRP, GRP)
                    sp.dma_start(c[s][:, :, :], ctx_d.rearrange("(k p) t -> p k t", p=P)[:, :, toks]).then_inc(in_[s], 16)
                    sp.dma_start(z[s][:, :], sums_d[:, toks]).then_inc(in_[s], 16)
                    sp.dma_start(x[s][:, :, :], token_rows(hs, g)).then_inc(in_[s], 16)

        @block.tensor
        def _(pe):
            with pe.Fori(0, NGRP // 2) as i:
                for s in range(2):
                    pe.wait_ge(in_[s], 48 * (i + 1))
                    for j in range(GT):
                        n = GT * (2 * i + s) + j
                        pe.wait_ge(multiplied, GT * 2 * i + max(GT * s + j - 1, 0))
                        cols = slice(j * P, (j + 1) * P)
                        for k in range(KD):
                            nc.tensor.transpose(ps[j % 2][:, k * P:(k + 1) * P], c[s][:, k, cols], ident[:, :])
                        nc.tensor.transpose(ps[j % 2][:, D:D + H], z[s][:, cols], ident[0:H, 0:H]).then_inc(turned, 1)

        @block.vector
        def _(dve):
            with dve.Fori(0, NGRP // 2) as i:
                for s in range(2):
                    dve.wait_ge(out_sem[s], 16 * i)
                    for j in range(GT):
                        n = GT * (2 * i + s) + j
                        dve.wait_ge(turned, n + 1)
                        nc.vector.reciprocal(inv[j % 2][:, :], ps[j % 2][:, D:D + H]).then_inc(inverted, 1)
                        dve.wait_ge(inverted, n + 1)
                        nc.vector.tensor_tensor(
                            scaled[j % 2][:, :].rearrange("p (h d) -> p h d", h=H),
                            ps[j % 2][:, 0:D].rearrange("p (h d) -> p h d", h=H),
                            inv[j % 2][:, :].rearrange("p (h a) -> p h a", a=1).broadcast_to([P, H, HD]),
                            ALU.mult).then_inc(multiplied, 1)
                        dve.wait_ge(multiplied, n + 1)
                        nc.vector.tensor_tensor(out[s][:, j, :], scaled[j % 2][:, :], x[s][:, j, :], ALU.add).then_inc(added, 1)

        @block.gpsimd
        def _(pool):
            with pool.Fori(0, NGRP // 2) as i:
                for s in range(2):
                    pool.wait_ge(added, GT * (2 * i + s + 1))
                    pool.dma_start(token_rows(sum_d, 2 * i + s), out[s][:, :, :]).then_inc(out_sem[s], 16)
            for s in range(2):
                pool.wait_ge(out_sem[s], 16 * NGRP // 2)


def normalise(nc, tag, sum_d, out_d, ident, xT, layer_norm, rms_norm):
    with ExitStack() as ctx:
        m = Mem(nc, ctx, tag)
        x = [m.sb(f"x{i}", [P, GT, D]) for i in range(2)]
        y = [m.sb(f"y{i}", [P, GT, D]) for i in range(2)]
        r = [m.sb(f"r{i}", [P, GT, D]) for i in range(2)]
        stats = [m.sb(f"stats{i}", [P, GT, 6]) for i in range(2)]
        mean_var = [m.sb(f"mean_var{i}", [P, GT, 2]) for i in range(2)]
        std = [m.sb(f"std{i}", [P, GT]) for i in range(2)]
        inv = [m.sb(f"inv{i}", [P, GT]) for i in range(2)]
        square = [m.sb(f"square{i}", [P, D]) for i in range(2)]
        total = [m.sb(f"total{i}", [P, GT]) for i in range(2)]
        root = [m.sb(f"root{i}", [P, GT]) for i in range(2)]
        inv_root = [m.sb(f"inv_root{i}", [P, GT]) for i in range(2)]
        eps = m.sb("eps", [P, 2])
        ps = [[m.ps(f"ps{i}{k}", [P, GRP]) for k in range(KD)] for i in range(2)]
        in_ = [m.sem(f"in{i}") for i in range(2)]
        out_sem = [m.sem(f"out{i}") for i in range(2)]
        eps_set, stats_done, aggregated, std_done, inv_done, normed = (
            m.sem("eps_set"), m.sem("stats_done"), m.sem("aggregated"), m.sem("std_done"), m.sem("inv_done"), m.sem("normed"))
        squared, root_done, inv_root_done, scaled = m.sem("squared"), m.sem("root_done"), m.sem("inv_root_done"), m.sem("scaled")
        turned, copied = m.sem("turned"), m.sem("copied")
        passed = m.sem("passed")
        block = ctx.enter_context(nc.Block())
        rows_in = y if layer_norm else x
        last = r if rms_norm else y

        @block.sync
        def _(sp):
            with sp.Fori(0, NGRP // 2) as i:
                for s in range(2):
                    sp.wait_ge(normed if layer_norm else scaled, GT * 2 * i)
                    sp.dma_start(x[s][:, :, :], token_rows(sum_d, 2 * i + s)).then_inc(in_[s], 16)

        @block.vector
        def _(dve):
            nc.vector.memset(eps[:, 0:1], LN_EPS)
            nc.vector.memset(eps[:, 1:2], RMS_EPS).then_inc(eps_set, 1)
            with dve.Fori(0, NGRP // 2) as i:
                for s in range(2):
                    g = 2 * i + s
                    if layer_norm:
                        dve.wait_ge(in_[s], 16 * (i + 1))
                        for j in range(GT):
                            nc.vector.bn_stats(stats[s][:, j, :], x[s][:, j, :]).then_inc(stats_done, 1)
                        dve.wait_ge(stats_done, GT * (g + 1))
                        dve.sem_inc(passed, 1)
                        for j in range(GT):
                            nc.vector.bn_aggr(mean_var[s][:, j, :], stats[s][:, j, :]).then_inc(aggregated, 1)
                        dve.wait_ge(std_done, g + 1)
                        nc.vector.reciprocal(inv[s][:, :], std[s][:, :]).then_inc(inv_done, 1)
                        dve.wait_ge(inv_done, g + 1)
                        if out_d is not None:
                            dve.wait_ge(out_sem[s], 16 * i)
                        if xT is not None:
                            dve.wait_ge(turned, KD * 2 * i)
                        for j in range(GT):
                            nc.vector.tensor_scalar(y[s][:, j, :], x[s][:, j, :], mean_var[s][:, j, 0:1], inv[s][:, j:j + 1],
                                                    ALU.subtract, ALU.mult).then_inc(normed, 1)
                    if rms_norm:
                        dve.wait_ge(root_done, g + 1)
                        nc.vector.reciprocal(inv_root[s][:, :], root[s][:, :]).then_inc(inv_root_done, 1)
                        dve.wait_ge(inv_root_done, g + 1)
                        dve.wait_ge(turned, KD * 2 * i)
                        for j in range(GT):
                            nc.vector.tensor_scalar(r[s][:, j, :], rows_in[s][:, j, :], inv_root[s][:, j:j + 1], None,
                                                    ALU.mult).then_inc(scaled, 1)

        @block.scalar
        def _(act):
            act.wait_ge(eps_set, 1)
            with act.Fori(0, NGRP // 2) as i:
                for s in range(2):
                    g = 2 * i + s
                    if layer_norm:
                        act.wait_ge(aggregated, GT * (g + 1))
                        act.wait_ge(inv_done, 2 * i)
                        nc.scalar.activation(std[s][:, :], mean_var[s][:, :, 1:2].rearrange("p g a -> p (g a)"), ACT.Sqrt,
                                             bias=eps[:, 0:1]).then_inc(std_done, 1)
                    if rms_norm:
                        if layer_norm:
                            act.wait_ge(normed, GT * (g + 1))
                        else:
                            act.wait_ge(in_[s], 16 * (i + 1))
                        act.wait_ge(root_done, g)
                        for j in range(GT):
                            act.wait_ge(squared, GT * g + max(j - 1, 0))
                            nc.scalar.activation(square[j % 2][:, :], rows_in[s][:, j, :], ACT.Square,
                                                 accum_out=total[s][:, j:j + 1]).then_inc(squared, 1)
                        act.wait_ge(squared, GT * (g + 1))
                        act.wait_ge(inv_root_done, 2 * i)
                        nc.scalar.activation(root[s][:, :], total[s][:, :], ACT.Sqrt, bias=eps[:, 1:2],
                                             scale=1.0 / D).then_inc(root_done, 1)
                    if xT is not None:
                        for k in range(KD):
                            act.wait_ge(turned, KD * g + k + 1)
                            nc.scalar.copy(xT[:, k, bass.ds(g * GRP, GRP)], ps[s][k][:, :]).then_inc(copied, 1)

        if xT is not None:
            @block.tensor
            def _(pe):
                with pe.Fori(0, NGRP // 2) as i:
                    for s in range(2):
                        g = 2 * i + s
                        pe.wait_ge(scaled if rms_norm else normed, GT * (g + 1))
                        pe.wait_ge(copied, KD * 2 * i)
                        for k in range(KD):
                            for j in range(GT):
                                mm = nc.tensor.transpose(ps[s][k][:, j * P:(j + 1) * P], last[s][:, j, k * P:(k + 1) * P],
                                                         ident[:, :])
                            mm.then_inc(turned, 1)

        if out_d is not None:
            @block.gpsimd
            def _(pool):
                with pool.Fori(0, NGRP // 2) as i:
                    for s in range(2):
                        pool.wait_ge(normed, GT * (2 * i + s + 1))
                        pool.dma_start(token_rows(out_d, 2 * i + s), y[s][:, :, :]).then_inc(out_sem[s], 16)
                for s in range(2):
                    pool.wait_ge(out_sem[s], 16 * NGRP // 2)


def route(nc, tag, xT, Wg, bg, ident, upto, capacity, weight, pos, table, tile_expert):
    NT = table.shape[1]
    BIG = 3.0e38
    with ExitStack() as ctx:
        m = Mem(nc, ctx, tag)
        wg = m.sb("wg", [P, KD, E])
        bias = m.sb("bias", [E, 1])
        logit_row = [m.sb(f"logit_row{i}", [E, GRP]) for i in range(2)]
        S = [P, E, TT]
        value, low, hit, cand, expo = (m.sb(a, S) for a in ("value", "low", "hit", "cand", "expo"))
        one = [m.sb(f"one{a}", S) for a in range(2)]
        labels, tile_sum, upto_tile, place, carry = (m.sb(a, S) for a in ("labels", "tile_sum", "upto_tile", "place", "carry"))
        number = m.sb("number", S)
        top = [m.sb(f"top{a}", [P, TT]) for a in range(2)]
        pick = m.sb("pick", [P, TT])
        total, inv = m.sb("total", [P, TT]), m.sb("inv", [P, TT])
        tiles, end, base = m.sb("tiles", [P, E]), m.sb("end", [P, E]), m.sb("base", [P, E])
        ones_e = m.sb("ones_e", [P, E])
        at_tile = m.sb("at_tile", [P, NT, E])
        tile_no = m.sb("tile_no", [P, NT])
        where = m.sb("where", [P, 2, TT])
        bits = m.sb("bits", [P, 2, TT], I32)
        slot, tile_of = m.sb("slot", [P, 2, TT]), m.sb("tile_of", [P, 2, TT])
        counts_i, tokens_i = m.sb("counts_i", [P, P], I32), m.sb("tokens_i", [P, TT], I32)
        counts, tokens = m.sb("counts", [P, P]), m.sb("tokens", [P, TT])
        ones = m.sb("ones", [P, P])
        in_slot = [m.sb(f"in_slot{i}", [P, P], F32R) for i in range(2)]
        in_tile = [m.sb(f"in_tile{i}", [P, NT], F32R) for i in range(2)]
        row_ps = [m.ps(f"row_ps{i}", [E, GRP]) for i in range(2)]
        col_ps = [m.ps(f"col_ps{i}", [P, GT, E]) for i in range(2)]
        cum_ps, sum_ps, table_ps = m.ps("cum_ps", S), m.ps("sum_ps", S), m.ps("table_ps", [P, NT])
        wg_in, row_done, row_copied, turned, logits_in = (m.sem("wg_in"), m.sem("row_done"), m.sem("row_copied"),
                                                          m.sem("turned"), m.sem("logits_in"))
        step, exp_in, exp_done, labels_in, counted = m.sem("step"), m.sem("exp_in"), m.sem("exp_done"), m.sem("labels_in"), m.sem("counted")
        iotas, made, placed = m.sem("iotas"), m.sem("made"), m.sem("placed")
        NW = 16 * (1 + (bg is not None))
        passed = m.sem("passed")
        block = ctx.enter_context(nc.Block())

        @block.sync
        def _(sp):
            sp.dma_start(wg[:, :, :], Wg.rearrange("(k p) e -> p k e", p=P)).then_inc(wg_in, 16)
            if bg is not None:
                sp.dma_start(bias[:, :], bg.rearrange("(e a) -> e a", a=1)).then_inc(wg_in, 16)

        @block.tensor
        def _(pe):
            pe.wait_ge(wg_in, NW)
            with pe.Fori(0, NGRP // 2) as i:
                for s in range(2):
                    g = 2 * i + s
                    pe.wait_ge(row_copied, 2 * i)
                    for k in range(KD):
                        mm = nc.tensor.matmul(row_ps[s][:, :], wg[:, k, :], xT[:, k, bass.ds(g * GRP, GRP)],
                                              start=(k == 0), stop=(k == KD - 1))
                    mm.then_inc(row_done, 1)
                for s in range(2):
                    g = 2 * i + s
                    pe.wait_ge(row_copied, g + 1)
                    pe.wait_ge(logits_in, 2 * i)
                    pe.sem_inc(passed, 1)
                    for j in range(GT):
                        mm = nc.tensor.transpose(col_ps[s][:, j, :], logit_row[s][:, j * P:(j + 1) * P], ident[0:E, 0:E])
                    mm.then_inc(turned, 1)
            pe.wait_ge(labels_in, 1)
            flat = labels[:, :, :].rearrange("p e t -> p (e t)")
            nc.tensor.matmul(sum_ps[:, :, :].rearrange("p e t -> p (e t)"), ones[:, :], flat, start=True, stop=True)
            nc.tensor.matmul(cum_ps[:, :, :].rearrange("p e t -> p (e t)"), upto[:, :], flat, start=True, stop=True).then_inc(counted, 1)

            def place_tile(t, first, last):
                for a in range(2):
                    pe.wait_ge(made, 2 * t + a + 1)
                    nc.tensor.matmul(table_ps[:, :], in_slot[a][:, :], in_tile[a][:, :], start=(first and a == 0),
                                     stop=(last and a == 1)).then_inc(placed, 1)

            place_tile(0, True, False)
            with pe.Fori(1, TT - 1) as t:
                place_tile(t, False, False)
            place_tile(TT - 1, False, True)

        @block.scalar
        def _(act):
            act.wait_ge(wg_in, NW)
            with act.Fori(0, NGRP // 2) as i:
                for s in range(2):
                    act.wait_ge(row_done, 2 * i + s + 1)
                    act.wait_ge(turned, 2 * i)
                    if bg is None:
                        nc.scalar.copy(logit_row[s][:, :], row_ps[s][:, :]).then_inc(row_copied, 1)
                    else:
                        nc.scalar.activation(logit_row[s][:, :], row_ps[s][:, :], ACT.Identity,
                                             bias=bias[:, 0:1]).then_inc(row_copied, 1)
            act.wait_ge(exp_in, 1)
            if capacity is None:
                nc.scalar.activation(expo[:, :, :], low[:, :, :], ACT.Exp).then_inc(exp_done, 1)
            else:
                nc.scalar.activation(total[:, :], pick[:, :], ACT.Exp).then_inc(exp_done, 1)

        @block.gpsimd
        def _(pool):
            nc.gpsimd.iota(counts_i[:, :], pattern=[[1, P]], base=0, channel_multiplier=0).then_inc(iotas, 1)
            nc.gpsimd.iota(tokens_i[:, :], pattern=[[P, TT]], base=0, channel_multiplier=1).then_inc(iotas, 1)

        @block.vector
        def _(dve):
            count = [0]

            def settle(ins):
                ins.then_inc(step, 1)
                count[0] += 1
                dve.wait_ge(step, count[0])

            def over_experts(a):
                return a[:, :, :].rearrange("p e t -> p t e")

            def to_experts(a):
                return a.rearrange("p (a t) -> p a t", a=1).broadcast_to(S)

            def to_tiles(a):
                return a.rearrange("p (e a) -> p e a", a=1).broadcast_to(S)

            dve.wait_ge(iotas, 2)
            for e in range(E):
                nc.vector.memset(number[:, e, :], float(e - E))
            nc.vector.memset(ones_e[:, :], 1.0)
            nc.vector.memset(ones[:, :], 1.0)
            nc.vector.memset(carry[:, :, 1:TT], 1.0)
            nc.vector.memset(carry[:, :, 0:1], 0.0)
            nc.vector.tensor_copy(tokens[:, :], tokens_i[:, :])
            settle(nc.vector.tensor_copy(counts[:, :], counts_i[:, :]))
            with dve.Fori(0, NGRP // 2) as i:
                for s in range(2):
                    g = 2 * i + s
                    dve.wait_ge(turned, g + 1)
                    nc.vector.tensor_copy(value[:, :, bass.ds(g * GT, GT)].rearrange("p e j -> p j e"),
                                          col_ps[s][:, :, :]).then_inc(logits_in, 1)
            dve.wait_ge(logits_in, NGRP)
            if capacity is None:
                settle(nc.vector.tensor_reduce(top[0][:, :], over_experts(value), AX.X, ALU.max))
                nc.vector.tensor_tensor(low[:, :, :], value[:, :, :], to_experts(top[0][:, :]), ALU.subtract).then_inc(exp_in, 1)
                dve.wait_ge(exp_done, 1)
                settle(nc.vector.tensor_reduce(total[:, :], over_experts(expo), AX.X, ALU.add))
                settle(nc.vector.reciprocal(inv[:, :], total[:, :]))
                settle(nc.vector.tensor_tensor(value[:, :, :], expo[:, :, :], to_experts(inv[:, :]), ALU.mult))
            for a in range(2):
                src = value if a == 0 else low
                settle(nc.vector.tensor_reduce(top[a][:, :], over_experts(src), AX.X, ALU.max))
                settle(nc.vector.tensor_tensor(hit[:, :, :], src[:, :, :], to_experts(top[a][:, :]), ALU.is_equal))
                settle(nc.vector.scalar_tensor_tensor(cand[:, :, :], hit[:, :, :], float(-E), number[:, :, :], ALU.mult, ALU.add))
                settle(nc.vector.tensor_reduce(pick[:, :], over_experts(cand), AX.X, ALU.min))
                settle(nc.vector.tensor_scalar(pick[:, :], pick[:, :], float(E), None, ALU.add))
                settle(nc.vector.tensor_tensor(one[a][:, :, :], number[:, :, :], to_experts(pick[:, :]), ALU.is_equal))
                if a == 0:
                    settle(nc.vector.scalar_tensor_tensor(low[:, :, :], one[0][:, :, :], -BIG, value[:, :, :], ALU.mult, ALU.add))
            if capacity is None:
                settle(nc.vector.tensor_tensor(total[:, :], top[0][:, :], top[1][:, :], ALU.add))
                settle(nc.vector.reciprocal(inv[:, :], total[:, :]))
                for a in range(2):
                    nc.vector.tensor_tensor(weight[:, a, :], top[a][:, :], inv[:, :], ALU.mult)
            else:
                nc.vector.tensor_tensor(pick[:, :], top[1][:, :], top[0][:, :], ALU.subtract).then_inc(exp_in, 1)
                dve.wait_ge(exp_done, 1)
                settle(nc.vector.tensor_scalar(inv[:, :], total[:, :], 1.0, None, ALU.add))
                settle(nc.vector.reciprocal(weight[:, 0, :], inv[:, :]))
                settle(nc.vector.tensor_tensor(weight[:, 1, :], total[:, :], weight[:, 0, :], ALU.mult))
            nc.vector.tensor_tensor(labels[:, :, :], one[0][:, :, :], one[1][:, :, :], ALU.add).then_inc(labels_in, 1)
            dve.wait_ge(counted, 1)
            settle(nc.vector.tensor_copy(tile_sum[:, :, :], sum_ps[:, :, :]))
            settle(nc.vector.tensor_tensor_scan(upto_tile[:, :, :].rearrange("p e t -> p (e t)"),
                                                carry[:, :, :].rearrange("p e t -> p (e t)"),
                                                tile_sum[:, :, :].rearrange("p e t -> p (e t)"), 0.0, ALU.mult, ALU.add))
            settle(nc.vector.tensor_tensor(place[:, :, :], upto_tile[:, :, :], tile_sum[:, :, :], ALU.subtract))
            settle(nc.vector.tensor_tensor(place[:, :, :], cum_ps[:, :, :], place[:, :, :], ALU.add))
            if capacity is None:
                settle(nc.vector.tensor_scalar(hit[:, 0, :], counts[:, 0:TT], float(P), None, ALU.mult))
                settle(nc.vector.tensor_tensor(cand[:, :, :], upto_tile[:, :, TT - 1:TT].broadcast_to(S),
                                               hit[:, 0:1, :].broadcast_to(S), ALU.is_gt))
                settle(nc.vector.tensor_reduce(tiles[:, :], cand[:, :, :], AX.X, ALU.add))
                settle(nc.vector.tensor_tensor_scan(end[:, :], ones_e[:, :], tiles[:, :], 0.0, ALU.mult, ALU.add))
                settle(nc.vector.tensor_tensor(base[:, :], end[:, :], tiles[:, :], ALU.subtract))
                settle(nc.vector.tensor_scalar(base[:, :], base[:, :], float(P), -1.0, ALU.mult, ALU.add))
                settle(nc.vector.tensor_tensor(place[:, :, :], place[:, :, :], to_tiles(base[:, :]), ALU.add))
                settle(nc.vector.tensor_tensor(at_tile[:, :, :],
                                               end[:, :].rearrange("p (a e) -> p a e", a=1).broadcast_to([P, NT, E]),
                                               counts[:, 0:NT].rearrange("p (t a) -> p t a", a=1).broadcast_to([P, NT, E]),
                                               ALU.is_le))
                settle(nc.vector.tensor_reduce(tile_no[:, :], at_tile[:, :, :], AX.X, ALU.add))
                settle(nc.vector.tensor_scalar(tile_expert[:, :], tile_no[:, :], float(E - 1), None, ALU.min))
            else:
                settle(nc.vector.tensor_scalar(hit[:, :, :], place[:, :, :], float(capacity), None, ALU.is_le))
                settle(nc.vector.tensor_scalar(cand[:, :, :], number[:, :, :], float(capacity), -1.0, ALU.mult, ALU.add))
                settle(nc.vector.tensor_tensor(place[:, :, :], place[:, :, :], cand[:, :, :], ALU.add))
                settle(nc.vector.tensor_tensor(place[:, :, :], place[:, :, :], hit[:, :, :], ALU.mult))
                settle(nc.vector.tensor_scalar(place[:, :, :], place[:, :, :], float(E * capacity), None, ALU.add))
            for a in range(2):
                settle(nc.vector.tensor_tensor(hit[:, :, :], one[a][:, :, :], place[:, :, :], ALU.mult))
                settle(nc.vector.tensor_reduce(where[:, a, :], over_experts(hit), AX.X, ALU.add))
            settle(nc.vector.tensor_copy(pos[:, :, :], where[:, :, :]))
            settle(nc.vector.tensor_scalar(bits[:, :, :], pos[:, :, :], P - 1, None, ALU.bitwise_and))
            settle(nc.vector.tensor_copy(slot[:, :, :], bits[:, :, :]))
            settle(nc.vector.tensor_scalar(bits[:, :, :], pos[:, :, :], 7, None, ALU.arith_shift_right))
            settle(nc.vector.tensor_copy(tile_of[:, :, :], bits[:, :, :]))
            with dve.Fori(0, TT) as t:
                for a in range(2):
                    dve.wait_ge(placed, 2 * t)
                    nc.vector.tensor_scalar(in_slot[a][:, :], counts[:, :], slot[:, a, bass.ds(t, 1)], None, ALU.is_equal)
                    nc.vector.tensor_scalar(in_tile[a][:, :], counts[:, 0:NT], tile_of[:, a, bass.ds(t, 1)],
                                            tokens[:, bass.ds(t, 1)], ALU.is_equal, ALU.mult).then_inc(made, 1)
            dve.wait_ge(placed, 2 * TT)
            settle(nc.vector.tensor_copy(table[:, :], table_ps[:, :]))


def experts_gelu(nc, x_d, Wu, Wd, ident, table, tile_expert, y_d):
    NT = table.shape[1]
    F = Wu.shape[2]
    KF = F // P
    XS = 4
    with ExitStack() as ctx:
        m = Mem(nc, ctx, "gelu")
        wu, wd = m.sb("wu", [P, KD, E, F]), m.sb("wd", [P, KF, E, D])
        row_no = [m.sb(f"row_no{i}", [P, 1], I32) for i in range(XS)]
        x = [m.sb(f"x{i}", [P, D]) for i in range(XS)]
        xT = [m.sb(f"xT{i}", [P, D]) for i in range(2)]
        h = [m.sb(f"h{i}", [P, F]) for i in range(2)]
        hT = [m.sb(f"hT{i}", [P, F]) for i in range(2)]
        y = [m.sb(f"y{i}", [P, D]) for i in range(2)]
        x_ps = m.ps("x_ps", [P, D])
        h_ps, t_ps, y_ps = ([m.ps(f"{a}_ps{i}", [P, n]) for i in range(2)] for a, n in (("h", F), ("t", F), ("y", D)))
        w_in, x_turned, xT_ready, h_done, h_ready, h_turned, hT_ready, y_done, y_ready, numbered = (m.sem(a) for a in (
            "w_in", "x_turned", "xT_ready", "h_done", "h_ready", "h_turned", "hT_ready", "y_done", "y_ready", "numbered"))
        x_in = [m.sem(f"x_in{i}") for i in range(XS)]
        y_out = [m.sem(f"y_out{i}") for i in range(2)]
        passed = m.sem("passed")
        block = ctx.enter_context(nc.Block())

        @block.sync
        def _(sp):
            for k in range(KD):
                sp.dma_start(wu[:, k, :, :], Wu[:, k * P:(k + 1) * P, :].rearrange("e p f -> p e f")).then_inc(w_in, 16)
            for k in range(KF):
                sp.dma_start(wd[:, k, :, :], Wd[:, k * P:(k + 1) * P, :].rearrange("e p f -> p e f")).then_inc(w_in, 16)
            with sp.Fori(0, NT // 2) as i:
                for s in range(2):
                    n = 2 * i + s
                    sp.wait_ge(y_ready, n + 1)
                    sp.dma_start(y_d[bass.ds(n * P, P), :], y[s][:, :]).then_inc(y_out[s], 16)
            for s in range(2):
                sp.wait_ge(y_out[s], 16 * NT // 2)

        @block.gpsimd
        def _(pool):
            with pool.Fori(0, NT // XS) as i:
                for s in range(XS):
                    n = XS * i + s
                    pool.wait_ge(x_in[s], 16 * i)
                    nc.gpsimd.tensor_copy(row_no[s][:, :], table[:, bass.ds(n, 1)]).then_inc(numbered, 1)
                for s in range(XS):
                    n = XS * i + s
                    pool.wait_ge(numbered, n + 1)
                    pool.wait_ge(x_turned, XS * i)
                    pool.sem_inc(passed, 1)
                    nc.gpsimd.indirect_dma_start(out=x[s][:, :], out_offset=None, in_=x_d,
                                                 in_offset=bass.IndirectOffsetOnAxis(ap=row_no[s][:, 0:1], axis=0)
                                                 ).then_inc(x_in[s], 16)

        @block.tensor
        def _(pe):
            def turn_x(n, s):
                pe.wait_ge(x_in[s], 16 * (n // XS + 1))
                pe.wait_ge(xT_ready, n)
                for k in range(KD):
                    mm = nc.tensor.transpose(x_ps[:, k * P:(k + 1) * P], x[s][:, k * P:(k + 1) * P], ident[:, :])
                mm.then_inc(x_turned, 1)

            def up(n, s):
                e = pe.value_load(tile_expert[0:1, bass.ds(n, 1)], min_val=0, max_val=E - 1)
                pe.wait_ge(xT_ready, n + 1)
                if not isinstance(n, int) or n > 1:
                    pe.wait_ge(h_ready, n - 1)
                for k in range(KD):
                    mm = nc.tensor.matmul(h_ps[s][:, :], xT[s][:, k * P:(k + 1) * P],
                                          wu[:, k, bass.ds(e, 1), :].rearrange("p e f -> p (e f)"),
                                          start=(k == 0), stop=(k == KD - 1))
                mm.then_inc(h_done, 1)

            def turn_h(n, s):
                pe.wait_ge(h_ready, n + 1)
                for k in range(KF):
                    mm = nc.tensor.transpose(t_ps[s][:, k * P:(k + 1) * P], h[s][:, k * P:(k + 1) * P], ident[:, :])
                mm.then_inc(h_turned, 1)

            def down(n, s):
                e = pe.value_load(tile_expert[0:1, bass.ds(n, 1)], min_val=0, max_val=E - 1)
                pe.wait_ge(hT_ready, n + 1)
                if not isinstance(n, int) or n > 1:
                    pe.wait_ge(y_ready, n - 1)
                for k in range(KF):
                    mm = nc.tensor.matmul(y_ps[s][:, :], hT[s][:, k * P:(k + 1) * P],
                                          wd[:, k, bass.ds(e, 1), :].rearrange("p e f -> p (e f)"),
                                          start=(k == 0), stop=(k == KF - 1))
                mm.then_inc(y_done, 1)

            def one(n, s):
                turn_h(n, s % 2)
                if not (isinstance(n, int) and n + 1 >= NT):
                    up(n + 1, (s + 1) % 2)
                down(n, s % 2)
                if not (isinstance(n, int) and n + 2 >= NT):
                    turn_x(n + 2, (s + 2) % XS)

            pe.wait_ge(w_in, 16 * (KD + KF))
            turn_x(0, 0)
            turn_x(1, 1)
            up(0, 0)
            one(0, 0)
            one(1, 1)
            one(2, 2)
            one(3, 3)
            with pe.Fori(1, NT // XS - 1) as i:
                for s in range(XS):
                    one(XS * i + s, s)
            for s in range(XS):
                one(NT - XS + s, s)

        @block.scalar
        def _(act):
            with act.Fori(0, NT // 2) as i:
                for s in range(2):
                    n = 2 * i + s
                    act.wait_ge(h_done, n + 1)
                    act.wait_ge(h_turned, 2 * i)
                    nc.scalar.activation(h[s][:, :], h_ps[s][:, :], ACT.Gelu).then_inc(h_ready, 1)
                    act.wait_ge(h_turned, n + 1)
                    act.wait_ge(y_done, 2 * i)
                    nc.scalar.copy(hT[s][:, :], t_ps[s][:, :]).then_inc(hT_ready, 1)

        @block.vector
        def _(dve):
            def take_x(n, s):
                dve.wait_ge(x_turned, n + 1)
                if not isinstance(n, int) or n > 1:
                    dve.wait_ge(h_done, n - 1)
                nc.vector.tensor_copy(xT[s][:, :], x_ps[:, :]).then_inc(xT_ready, 1)

            def take_y(n, s):
                dve.wait_ge(y_done, n + 1)
                dve.wait_ge(y_out[s], 16 * (n // 2))
                nc.vector.tensor_copy(y[s][:, :], y_ps[s][:, :]).then_inc(y_ready, 1)

            take_x(0, 0)
            take_x(1, 1)
            with dve.Fori(0, NT // 2 - 1) as i:
                for s in range(2):
                    take_y(2 * i + s, s)
                    take_x(2 * i + s + 2, s)
            for s in range(2):
                take_y(NT - 2 + s, s)


def experts_silu(nc, x_d, W1, W2, W3, ident, table, capacity, y_d):
    NT = table.shape[1]
    F = W1.shape[2]
    KF = F // P
    CT = capacity // P
    HALF = capacity // 2
    with ExitStack() as ctx:
        m = Mem(nc, ctx, "silu")
        w12 = [m.sb(f"w12{i}", [P, 2, KD, F]) for i in range(2)]
        w3 = [m.sb(f"w3{i}", [P, KF, D]) for i in range(2)]
        row_no = m.sb("row_no", [P, CT], I32)
        x = [m.sb(f"x{i}", [P, CT, D]) for i in range(2)]
        xT = [m.sb(f"xT{i}", [P, KD, capacity]) for i in range(2)]
        gate = [m.sb(f"gate{i}", [P, HALF]) for i in range(2)]
        h = m.sb("h", [P, KF, capacity])
        y = [m.sb(f"y{i}", [P, D]) for i in range(2)]
        zero = m.sb("zero", [1, D])
        x_ps = [m.ps(f"x_ps{i}", [P, KD, P]) for i in range(2)]
        h_ps = [[m.ps(f"h_ps{i}{a}", [P, HALF]) for a in range(2)] for i in range(2)]
        y_ps = [m.ps(f"y_ps{i}", [P, D]) for i in range(2)]
        x_turned, xT_ready, h_done, gated, h_ready, y_done, y_ready, numbered, zeroed = (m.sem(a) for a in (
            "x_turned", "xT_ready", "h_done", "gated", "h_ready", "y_done", "y_ready", "numbered", "zeroed"))
        w_in = [m.sem(f"w_in{i}") for i in range(2)]
        x_in = [m.sem(f"x_in{i}") for i in range(2)]
        y_out, zero_out = [m.sem(f"y_out{i}") for i in range(2)], m.sem("zero_out")
        UNITS = 2 * KF
        passed = m.sem("passed")
        block = ctx.enter_context(nc.Block())

        @block.sync
        def _(sp):
            def load(e, s):
                ex = bass.ds(e, 1)
                for a, W in enumerate((W1, W2)):
                    sp.dma_start(w12[s][:, a, :, :], W[ex].rearrange("e (k p) f -> p (e k) f", p=P)).then_inc(w_in[s], 16)
                sp.dma_start(w3[s][:, :, :], W3[ex].rearrange("e (k p) f -> p (e k) f", p=P)).then_inc(w_in[s], 16)

            def store(e, s):
                for j in range(CT):
                    sp.wait_ge(y_ready, CT * e + j + 1)
                    b = (s + j) % 2
                    sp.dma_start(y_d[bass.ds((CT * e + j) * P, P), :], y[b][:, :]).then_inc(y_out[b], 16)

            load(0, 0)
            load(1, 1)
            with sp.Fori(0, E // 2 - 1) as i:
                for s in range(2):
                    store(2 * i + s, s)
                    load(2 * i + s + 2, s)
            for s in range(2):
                store(E - 2 + s, s)
            for b in range(2):
                sp.wait_ge(y_out[b], 16 * NT // 2)

        @block.gpsimd
        def _(pool):
            nc.gpsimd.memset(zero[:, :], 0.0).then_inc(zeroed, 1)
            pool.wait_ge(zeroed, 1)
            pool.dma_start(y_d[NT * P:NT * P + 1, :], zero[:, :]).then_inc(zero_out, 16)
            with pool.Fori(0, E // 2) as i:
                for s in range(2):
                    e = 2 * i + s
                    pool.wait_ge(x_in[1 - s], 16 * CT * (i + s))
                    nc.gpsimd.tensor_copy(row_no[:, :], table[:, bass.ds(e * CT, CT)]).then_inc(numbered, 1)
                    pool.wait_ge(numbered, e + 1)
                    pool.wait_ge(x_turned, CT * 2 * i)
                    pool.sem_inc(passed, 1)
                    for j in range(CT):
                        nc.gpsimd.indirect_dma_start(out=x[s][:, j, :], out_offset=None, in_=x_d,
                                                     in_offset=bass.IndirectOffsetOnAxis(ap=row_no[:, j:j + 1], axis=0)
                                                     ).then_inc(x_in[s], 16)
            pool.wait_ge(zero_out, 16)

        @block.tensor
        def _(pe):
            def turn(e, s):
                pe.wait_ge(x_in[s], 16 * CT * (e // 2 + 1))
                for j in range(CT):
                    if not isinstance(e, int) or CT * e + j > 1:
                        pe.wait_ge(xT_ready, CT * e + j - 1)
                    for k in range(KD):
                        mm = nc.tensor.transpose(x_ps[(s + j) % 2][:, k, :], x[s][:, j, k * P:(k + 1) * P], ident[:, :])
                    mm.then_inc(x_turned, 1)

            def work(e, s, more):
                pe.wait_ge(w_in[s], 48 * (e // 2 + 1))
                pe.wait_ge(xT_ready, CT * (e + 1))
                for u in range(UNITS):
                    f, half = u // 2, u % 2
                    if not isinstance(e, int) or UNITS * e + u > 1:
                        pe.wait_ge(h_ready, UNITS * e + u - 1)
                    for a in range(2):
                        for k in range(KD):
                            mm = nc.tensor.matmul(h_ps[u % 2][a][:, :], w12[s][:, a, k, f * P:(f + 1) * P],
                                                  xT[s][:, k, half * HALF:(half + 1) * HALF],
                                                  start=(k == 0), stop=(k == KD - 1))
                    mm.then_inc(h_done, 1)
                if more:
                    turn(e + 1, 1 - s)
                pe.wait_ge(h_ready, UNITS * (e + 1))
                for j in range(CT):
                    if not isinstance(e, int) or CT * e + j > 1:
                        pe.wait_ge(y_ready, CT * e + j - 1)
                    for f in range(KF):
                        mm = nc.tensor.matmul(y_ps[(s + j) % 2][:, :], h[:, f, j * P:(j + 1) * P], w3[s][:, f, :],
                                              start=(f == 0), stop=(f == KF - 1))
                    mm.then_inc(y_done, 1)

            turn(0, 0)
            work(0, 0, True)
            with pe.Fori(0, E // 2 - 1) as i:
                work(2 * i + 1, 1, True)
                work(2 * i + 2, 0, True)
            work(E - 1, 1, False)

        @block.scalar
        def _(act):
            def one(e):
                for u in range(UNITS):
                    act.wait_ge(h_done, UNITS * e + u + 1)
                    if not isinstance(e, int) or UNITS * e + u > 1:
                        act.wait_ge(h_ready, UNITS * e + u - 1)
                    nc.scalar.activation(gate[u % 2][:, :], h_ps[u % 2][0][:, :], ACT.Silu).then_inc(gated, 1)

            one(0)
            with act.Fori(1, E) as e:
                one(e)

        @block.vector
        def _(dve):
            def take_x(e, s):
                if not isinstance(e, int) or e > 1:
                    dve.wait_ge(h_done, UNITS * (e - 1))
                for j in range(CT):
                    dve.wait_ge(x_turned, CT * e + j + 1)
                    nc.vector.tensor_copy(xT[s][:, :, j * P:(j + 1) * P], x_ps[(s + j) % 2][:, :, :]).then_inc(xT_ready, 1)

            def work(e, s, more):
                dve.wait_ge(y_done, CT * e)
                for u in range(UNITS):
                    dve.wait_ge(gated, UNITS * e + u + 1)
                    nc.vector.tensor_tensor(h[:, u // 2, (u % 2) * HALF:(u % 2 + 1) * HALF], gate[u % 2][:, :],
                                            h_ps[u % 2][1][:, :], ALU.mult).then_inc(h_ready, 1)
                if more:
                    take_x(e + 1, 1 - s)
                for j in range(CT):
                    b = (s + j) % 2
                    dve.wait_ge(y_done, CT * e + j + 1)
                    if not isinstance(e, int) or CT * e + j > 1:
                        dve.wait_ge(y_out[b], 16 * ((CT * e + j) // 2))
                    nc.vector.tensor_copy(y[b][:, :], y_ps[b][:, :]).then_inc(y_ready, 1)

            take_x(0, 0)
            work(0, 0, True)
            with dve.Fori(0, E // 2 - 1) as i:
                work(2 * i + 1, 1, True)
                work(2 * i + 2, 0, True)
            work(E - 1, 1, False)


def combine(nc, tag, x_d, y_d, pos, weight, sum_d, xT=None, W1=None, W2=None):
    shared = W1 is not None
    F = W1.shape[1] if shared else P
    KF = F // P
    with ExitStack() as ctx:
        m = Mem(nc, ctx, tag)
        w1, w2 = m.sb("w1", [P, KD, F]), m.sb("w2", [P, KF, D])
        x = [m.sb(f"x{i}", [P, GT, D]) for i in range(2)]
        y = [m.sb(f"y{i}", [P, GT, 2, D]) for i in range(2)]
        row_no = [m.sb(f"row_no{i}", [P, 2, GT], I32) for i in range(2)]
        part = [m.sb(f"part{i}", [P, GT, 2, D]) for i in range(2)]
        out = [m.sb(f"out{i}", [P, GT, D]) for i in range(2)]
        h = [m.sb(f"h{i}", [P, KF, GRP]) for i in range(2)]
        h_ps = [m.ps(f"h_ps{i}", [P, GRP]) for i in range(2)]
        y_ps = [m.ps(f"y_ps{i}", [P, D]) for i in range(2)]
        w_in, h_done, h_ready, y_done, numbered, first, second, summed = (m.sem(a) for a in (
            "w_in", "h_done", "h_ready", "y_done", "numbered", "first", "second", "summed"))
        x_in, y_in, out_sem = ([m.sem(f"{a}{i}") for i in range(2)] for a in ("x_in", "y_in", "out_sem"))
        passed = m.sem("passed")
        block = ctx.enter_context(nc.Block())

        @block.sync
        def _(sp):
            if shared:
                sp.dma_start(w1[:, :, :], W1.rearrange("(k p) f -> p k f", p=P)).then_inc(w_in, 16)
                sp.dma_start(w2[:, :, :], W2.rearrange("(k p) f -> p k f", p=P)).then_inc(w_in, 16)
            for s in range(2):
                sp.dma_start(x[s][:, :, :], token_rows(x_d, s)).then_inc(x_in[s], 16)

            def store(g, s):
                sp.wait_ge(summed, GT * (g + 1))
                sp.dma_start(token_rows(sum_d, g), out[s][:, :, :]).then_inc(out_sem[s], 16)

            with sp.Fori(0, NGRP // 2 - 1) as i:
                for s in range(2):
                    store(2 * i + s, s)
                    sp.dma_start(x[s][:, :, :], token_rows(x_d, 2 * i + s + 2)).then_inc(x_in[s], 16)
            for s in range(2):
                store(NGRP - 2 + s, s)
            for s in range(2):
                sp.wait_ge(out_sem[s], 16 * NGRP // 2)

        @block.gpsimd
        def _(pool):
            def one(g, s):
                pool.wait_ge(y_in[s], 16 * 2 * GT * (g // 2))
                nc.gpsimd.tensor_copy(row_no[s][:, :, :], pos[:, :, bass.ds(g * GT, GT)]).then_inc(numbered, 1)
                pool.wait_ge(numbered, g + 1)
                if not isinstance(g, int) or g > 1:
                    pool.wait_ge(summed, GT * (g - 1))
                pool.sem_inc(passed, 1)
                for j in range(GT):
                    for a in range(2):
                        nc.gpsimd.indirect_dma_start(
                            out=y[s][:, j, a, :], out_offset=None, in_=y_d,
                            in_offset=bass.IndirectOffsetOnAxis(ap=row_no[s][:, a, j:j + 1], axis=0)).then_inc(y_in[s], 16)

            one(0, 0)
            one(1, 1)
            with pool.Fori(1, NGRP // 2) as i:
                one(2 * i, 0)
                one(2 * i + 1, 1)

        if shared:
            @block.tensor
            def _(pe):
                def up(g, s):
                    for f in range(KF):
                        if not isinstance(g, int) or KF * g + f > 1:
                            pe.wait_ge(h_ready, KF * g + f - 1)
                        for k in range(KD):
                            mm = nc.tensor.matmul(h_ps[f % 2][:, :], w1[:, k, f * P:(f + 1) * P],
                                                  xT[:, k, bass.ds(g * GRP, GRP)], start=(k == 0), stop=(k == KD - 1))
                        mm.then_inc(h_done, 1)

                def down(g, s):
                    pe.wait_ge(h_ready, KF * (g + 1))
                    for j in range(GT):
                        if not isinstance(g, int) or GT * g + j > 1:
                            pe.wait_ge(first, GT * g + j - 1)
                        for f in range(KF):
                            mm = nc.tensor.matmul(y_ps[j % 2][:, :], h[s][:, f, j * P:(j + 1) * P], w2[:, f, :],
                                                  start=(f == 0), stop=(f == KF - 1))
                        mm.then_inc(y_done, 1)

                pe.wait_ge(w_in, 32)
                up(0, 0)
                up(1, 1)
                down(0, 0)
                with pe.Fori(0, NGRP // 2 - 1) as i:
                    up(2 * i + 2, 0)
                    down(2 * i + 1, 1)
                    up(2 * i + 3, 1)
                    down(2 * i + 2, 0)
                down(NGRP - 1, 1)

            @block.scalar
            def _(act):
                def one(g, s):
                    if not isinstance(g, int) or g > 1:
                        act.wait_ge(y_done, GT * (g - 1))
                    for f in range(KF):
                        act.wait_ge(h_done, KF * g + f + 1)
                        nc.scalar.activation(h[s][:, f, :], h_ps[f % 2][:, :], ACT.Gelu).then_inc(h_ready, 1)

                one(0, 0)
                one(1, 1)
                with act.Fori(1, NGRP // 2) as i:
                    one(2 * i, 0)
                    one(2 * i + 1, 1)

        @block.vector
        def _(dve):
            with dve.Fori(0, NGRP // 2) as i:
                for s in range(2):
                    g = 2 * i + s
                    dve.wait_ge(x_in[s], 16 * (i + 1))
                    if shared:
                        for j in range(GT):
                            dve.wait_ge(y_done, GT * g + j + 1)
                            nc.vector.tensor_tensor(part[s][:, j, 0, :], y_ps[j % 2][:, :], x[s][:, j, :], ALU.add).then_inc(first, 1)
                        dve.wait_ge(first, GT * (g + 1))
                    dve.wait_ge(y_in[s], 16 * 2 * GT * (i + 1))
                    dve.wait_ge(out_sem[s], 16 * i)
                    for j in range(GT):
                        nc.vector.scalar_tensor_tensor(part[s][:, j, 1, :], y[s][:, j, 0, :], weight[:, 0, bass.ds(g * GT + j, 1)],
                                                       part[s][:, j, 0, :] if shared else x[s][:, j, :],
                                                       ALU.mult, ALU.add).then_inc(second, 1)
                    dve.wait_ge(second, GT * (g + 1))
                    for j in range(GT):
                        nc.vector.scalar_tensor_tensor(out[s][:, j, :], y[s][:, j, 1, :], weight[:, 1, bass.ds(g * GT + j, 1)],
                                                       part[s][:, j, 1, :], ALU.mult, ALU.add).then_inc(summed, 1)


def mix_tokens(nc, nT, x_d, WkT, WvT, WrT, WoT, decay, first_share, scale, x2_d):
    with ExitStack() as ctx:
        m = Mem(nc, ctx, "mix")
        w = m.sb("w", [P, 3, KD, D])
        wo_raw, wo = m.sb("wo_raw", [P, KD, D]), m.sb("wo", [P, KD, D])
        scale_row = m.sb("scale_row", [P, D])
        td, tf, e1, ew, eu = (m.sb(a, [P, KD]) for a in ("td", "tf", "e1", "ew", "eu"))
        x = [m.sb(f"x{i}", [P, GT, D]) for i in range(2)]
        out = [m.sb(f"out{i}", [P, GT, D]) for i in range(2)]
        k_sb, r_sb, kv, wkv = ([m.sb(f"{a}{c}", [P, GRP]) for c in range(KD)] for a in ("k_sb", "r_sb", "kv", "wkv"))
        state = [[m.sb(f"state{i}{c}", [P, GRP + 1]) for c in range(KD)] for i in range(2)]
        z = [m.sb(f"z{i}", [P, KD, GRP]) for i in range(2)]
        k_ps, v_ps, r_ps = ([m.ps(f"{a}_ps{c}", [P, GRP]) for c in range(KD)] for a in "kvr")
        o_ps = [m.ps(f"o_ps{i}", [P, D]) for i in range(2)]
        w_in, wo_ready, e1_done, shares_done, kvr_done, k_copied, r_ready = (m.sem(a) for a in (
            "w_in", "wo_ready", "e1_done", "shares_done", "kvr_done", "k_copied", "r_ready"))
        carried, kv_done, scanned, wkv_done, z_done, o_done, added = (m.sem(a) for a in (
            "carried", "kv_done", "scanned", "wkv_done", "z_done", "o_done", "added"))
        x_in, out_sem = ([m.sem(f"{a}{i}") for i in range(2)] for a in ("x_in", "out_sem"))
        NW = 16 * (5 + 2 * KD)
        block = ctx.enter_context(nc.Block())

        @block.sync
        def _(sp):
            for i, a in enumerate((WkT, WvT, WrT)):
                sp.dma_start(w[:, i], a.rearrange("(k p) n -> p k n", p=P)).then_inc(w_in, 16)
            sp.dma_start(wo_raw[:, :, :], WoT.rearrange("(k p) n -> p k n", p=P)).then_inc(w_in, 16)
            sp.dma_start(scale_row[:, :], row(scale).broadcast_to([P, D])).then_inc(w_in, 16)
            for k in range(KD):
                for a, b in ((td, decay), (tf, first_share)):
                    sp.dma_start(a[:, k:k + 1], b[k * P:(k + 1) * P].rearrange("(p a) -> p a", a=1)).then_inc(w_in, 16)
            for s in range(2):
                sp.dma_start(x[s][:, :, :], token_rows(x_d, s)).then_inc(x_in[s], 16)

            def store(g, s):
                sp.wait_ge(added, GT * (g + 1))
                sp.dma_start(token_rows(x2_d, g), out[s][:, :, :]).then_inc(out_sem[s], 16)

            with sp.Fori(0, NGRP // 2 - 1) as i:
                for s in range(2):
                    store(2 * i + s, s)
                    sp.dma_start(x[s][:, :, :], token_rows(x_d, 2 * i + s + 2)).then_inc(x_in[s], 16)
            for s in range(2):
                store(NGRP - 2 + s, s)
            for s in range(2):
                sp.wait_ge(out_sem[s], 16 * NGRP // 2)

        @block.tensor
        def _(pe):
            def project(g, s):
                for c in range(KD):
                    if not isinstance(g, int) or g > 0:
                        for used in (k_copied, kv_done, r_ready):
                            pe.wait_ge(used, KD * g + c - 1)
                    for i, bank in enumerate((k_ps, v_ps, r_ps)):
                        for k in range(KD):
                            mm = nc.tensor.matmul(bank[c][:, :], w[:, i, k, c * P:(c + 1) * P],
                                                  nT[:, k, bass.ds(g * GRP, GRP)], start=(k == 0), stop=(k == KD - 1))
                    mm.then_inc(kvr_done, 1)

            def mix(g, s):
                pe.wait_ge(z_done, KD * (g + 1))
                for j in range(GT):
                    if not isinstance(g, int) or GT * g + j > 1:
                        pe.wait_ge(added, GT * g + j - 1)
                    for k in range(KD):
                        mm = nc.tensor.matmul(o_ps[j % 2][:, :], z[s][:, k, j * P:(j + 1) * P], wo[:, k, :],
                                              start=(k == 0), stop=(k == KD - 1))
                    mm.then_inc(o_done, 1)

            pe.wait_ge(w_in, NW)
            project(0, 0)
            project(1, 1)
            pe.wait_ge(wo_ready, 1)
            mix(0, 0)
            with pe.Fori(0, NGRP // 2 - 1) as i:
                project(2 * i + 2, 0)
                mix(2 * i + 1, 1)
                project(2 * i + 3, 1)
                mix(2 * i + 2, 0)
            mix(NGRP - 1, 1)

        @block.scalar
        def _(act):
            act.wait_ge(w_in, NW)
            nc.scalar.activation(e1[:, :], td[:, :], ACT.Exp).then_inc(e1_done, 1)
            nc.scalar.activation(eu[:, :], tf[:, :], ACT.Exp)
            act.wait_ge(e1_done, 1)
            nc.scalar.activation(ew[:, :], e1[:, :], ACT.Exp, scale=-1.0).then_inc(shares_done, 1)
            with act.Fori(0, NGRP) as g:
                for c in range(KD):
                    act.wait_ge(kvr_done, KD * g + c + 1)
                    act.wait_ge(kv_done, KD * g)
                    nc.scalar.copy(k_sb[c][:, :], k_ps[c][:, :]).then_inc(k_copied, 1)
                    act.wait_ge(z_done, KD * g)
                    nc.scalar.activation(r_sb[c][:, :], r_ps[c][:, :], ACT.Sigmoid).then_inc(r_ready, 1)

        @block.vector
        def _(dve):
            for c in range(KD):
                nc.vector.memset(state[1][c][:, GRP:GRP + 1], 0.0).then_inc(carried, 1)
            dve.wait_ge(w_in, NW)
            nc.vector.tensor_tensor(wo[:, :, :], wo_raw[:, :, :],
                                    scale_row[:, :].rearrange("p (a d) -> p a d", a=1).broadcast_to([P, KD, D]),
                                    ALU.mult).then_inc(wo_ready, 1)
            dve.wait_ge(shares_done, 1)
            dve.wait_ge(carried, KD)

            def scan(g, s):
                if not isinstance(g, int) or g > 1:
                    dve.wait_ge(o_done, GT * (g - 1))
                for c in range(KD):
                    n = KD * g + c + 1
                    dve.wait_ge(k_copied, n)
                    nc.vector.tensor_tensor(kv[c][:, :], k_sb[c][:, :], v_ps[c][:, :], ALU.mult).then_inc(kv_done, 1)
                    nc.vector.tensor_copy(state[s][c][:, 0:1], state[1 - s][c][:, GRP:GRP + 1]).then_inc(carried, 1)
                for c in range(KD):
                    n = KD * g + c + 1
                    dve.wait_ge(kv_done, n)
                    dve.wait_ge(carried, KD + n)
                    nc.vector.tensor_tensor_scan(state[s][c][:, 1:GRP + 1], ew[:, c:c + 1].broadcast_to([P, GRP]), kv[c][:, :],
                                                 state[s][c][:, 0:1], ALU.mult, ALU.add).then_inc(scanned, 1)
                for c in range(KD):
                    n = KD * g + c + 1
                    dve.wait_ge(scanned, n)
                    nc.vector.scalar_tensor_tensor(wkv[c][:, :], kv[c][:, :], eu[:, c:c + 1], state[s][c][:, 0:GRP],
                                                   ALU.mult, ALU.add).then_inc(wkv_done, 1)
                for c in range(KD):
                    n = KD * g + c + 1
                    dve.wait_ge(r_ready, n)
                    dve.wait_ge(wkv_done, n)
                    nc.vector.tensor_tensor(z[s][:, c, :], wkv[c][:, :], r_sb[c][:, :], ALU.mult).then_inc(z_done, 1)

            def add(g, s):
                dve.wait_ge(x_in[s], 16 * (g // 2 + 1))
                dve.wait_ge(out_sem[s], 16 * (g // 2))
                for j in range(GT):
                    dve.wait_ge(o_done, GT * g + j + 1)
                    nc.vector.tensor_tensor(out[s][:, j, :], o_ps[j % 2][:, :], x[s][:, j, :], ALU.add).then_inc(added, 1)

            scan(0, 0)
            with dve.Fori(0, NGRP // 2 - 1) as i:
                scan(2 * i + 1, 1)
                add(2 * i, 0)
                scan(2 * i + 2, 0)
                add(2 * i + 1, 1)
            scan(NGRP - 1, 1)
            add(NGRP - 2, 0)
            add(NGRP - 1, 1)


def mix_channels(nc, nT, x_d, x2_d, WfcT, WmlpT, scale, sum_d):
    F = WfcT.shape[1]
    KF = F // P
    with ExitStack() as ctx:
        m = Mem(nc, ctx, "mlp")
        wf = m.sb("wf", [P, KD, F])
        wm_raw, wm = m.sb("wm_raw", [P, KF, D]), m.sb("wm", [P, KF, D])
        scale_row = m.sb("scale_row", [P, D])
        x = [m.sb(f"x{i}", [P, GT, D]) for i in range(2)]
        x2 = [m.sb(f"x2{i}", [P, GT, D]) for i in range(2)]
        both = [m.sb(f"both{i}", [P, GT, D]) for i in range(2)]
        out = [m.sb(f"out{i}", [P, GT, D]) for i in range(2)]
        half = [m.sb(f"half{i}", [P, GRP]) for i in range(2)]
        leaky = [m.sb(f"leaky{i}", [P, GRP]) for i in range(2)]
        h = [m.sb(f"h{i}", [P, KF, GRP]) for i in range(2)]
        h_ps = [m.ps(f"h_ps{i}", [P, GRP]) for i in range(4)]
        y_ps = [m.ps(f"y_ps{i}", [P, D]) for i in range(2)]
        w_in, wm_ready, h_done, leaked, h_ready, y_done, paired, summed, halved = (m.sem(a) for a in (
            "w_in", "wm_ready", "h_done", "leaked", "h_ready", "y_done", "paired", "summed", "halved"))
        x_in, out_sem = ([m.sem(f"{a}{i}") for i in range(2)] for a in ("x_in", "out_sem"))
        block = ctx.enter_context(nc.Block())

        @block.sync
        def _(sp):
            sp.dma_start(wf[:, :, :], WfcT.rearrange("(k p) n -> p k n", p=P)).then_inc(w_in, 16)
            sp.dma_start(wm_raw[:, :, :], WmlpT.rearrange("(k p) n -> p k n", p=P)).then_inc(w_in, 16)
            sp.dma_start(scale_row[:, :], row(scale).broadcast_to([P, D])).then_inc(w_in, 16)

            def load(g, s):
                sp.dma_start(x[s][:, :, :], token_rows(x_d, g)).then_inc(x_in[s], 16)
                sp.dma_start(x2[s][:, :, :], token_rows(x2_d, g)).then_inc(x_in[s], 16)

            def store(g, s):
                sp.wait_ge(summed, GT * (g + 1))
                sp.dma_start(token_rows(sum_d, g), out[s][:, :, :]).then_inc(out_sem[s], 16)

            load(0, 0)
            load(1, 1)
            with sp.Fori(0, NGRP // 2 - 1) as i:
                for s in range(2):
                    store(2 * i + s, s)
                    load(2 * i + s + 2, s)
            for s in range(2):
                store(NGRP - 2 + s, s)
            for s in range(2):
                sp.wait_ge(out_sem[s], 16 * NGRP // 2)

        @block.tensor
        def _(pe):
            def up(g, s):
                for f in range(KF):
                    if not isinstance(g, int) or KF * g + f > 3:
                        pe.wait_ge(leaked, KF * g + f - 3)
                    for k in range(KD):
                        mm = nc.tensor.matmul(h_ps[f % 4][:, :], wf[:, k, f * P:(f + 1) * P],
                                              nT[:, k, bass.ds(g * GRP, GRP)], start=(k == 0), stop=(k == KD - 1))
                    mm.then_inc(h_done, 1)

            def down(g, s):
                pe.wait_ge(h_ready, KF * (g + 1))
                for j in range(GT):
                    if not isinstance(g, int) or GT * g + j > 1:
                        pe.wait_ge(summed, GT * g + j - 1)
                    for f in range(KF):
                        mm = nc.tensor.matmul(y_ps[j % 2][:, :], h[s][:, f, j * P:(j + 1) * P], wm[:, f, :],
                                              start=(f == 0), stop=(f == KF - 1))
                    mm.then_inc(y_done, 1)

            pe.wait_ge(w_in, 48)
            up(0, 0)
            up(1, 1)
            pe.wait_ge(wm_ready, 1)
            down(0, 0)
            with pe.Fori(0, NGRP // 2 - 1) as i:
                up(2 * i + 2, 0)
                down(2 * i + 1, 1)
                up(2 * i + 3, 1)
                down(2 * i + 2, 0)
            down(NGRP - 1, 1)

        @block.scalar
        def _(act):
            def one(g, s):
                if not isinstance(g, int) or g > 1:
                    act.wait_ge(y_done, GT * (g - 1))
                for f in range(KF + 1):
                    if f < KF:
                        act.wait_ge(h_done, KF * g + f + 1)
                        if f > 1:
                            act.wait_ge(leaked, KF * g + f - 1)
                        nc.scalar.activation(half[f % 2][:, :], h_ps[f % 4][:, :], ACT.Copy, scale=0.5).then_inc(halved, 1)
                    if f > 0:
                        act.wait_ge(leaked, KF * g + f)
                        nc.scalar.activation(h[s][:, f - 1, :], leaky[(f - 1) % 2][:, :], ACT.Square).then_inc(h_ready, 1)

            one(0, 0)
            one(1, 1)
            with act.Fori(1, NGRP // 2) as i:
                one(2 * i, 0)
                one(2 * i + 1, 1)

        @block.gpsimd
        def _(pool):
            with pool.Fori(0, NGRP // 2) as i:
                for s in range(2):
                    g = 2 * i + s
                    pool.wait_ge(x_in[s], 32 * (i + 1))
                    pool.wait_ge(summed, GT * 2 * i)
                    for j in range(GT):
                        nc.gpsimd.tensor_tensor(both[s][:, j, :], x[s][:, j, :], x2[s][:, j, :], ALU.add).then_inc(paired, 1)

        @block.vector
        def _(dve):
            dve.wait_ge(w_in, 48)
            nc.vector.tensor_tensor(wm[:, :, :], wm_raw[:, :, :],
                                    scale_row[:, :].rearrange("p (a d) -> p a d", a=1).broadcast_to([P, KF, D]),
                                    ALU.mult).then_inc(wm_ready, 1)

            def leak(g, s):
                for f in range(KF):
                    dve.wait_ge(halved, KF * g + f + 1)
                    if not isinstance(g, int) or KF * g + f > 1:
                        dve.wait_ge(h_ready, KF * g + f - 1)
                    nc.vector.tensor_tensor(leaky[f % 2][:, :], h_ps[f % 4][:, :], half[f % 2][:, :], ALU.max).then_inc(leaked, 1)

            def add(g, s):
                dve.wait_ge(out_sem[s], 16 * (g // 2))
                for j in range(GT):
                    dve.wait_ge(y_done, GT * g + j + 1)
                    dve.wait_ge(paired, GT * g + j + 1)
                    nc.vector.tensor_tensor(out[s][:, j, :], y_ps[j % 2][:, :], both[s][:, j, :], ALU.add).then_inc(summed, 1)

            leak(0, 0)
            leak(1, 1)
            add(0, 0)
            with dve.Fori(0, NGRP // 2 - 1) as i:
                leak(2 * i + 2, 0)
                add(2 * i + 1, 1)
                leak(2 * i + 3, 1)
                add(2 * i + 2, 0)
            add(NGRP - 1, 1)




def network(nc, hidden, hidden_T, Wq, bq, Wk, bk, Wv, bv, gate0, up0, down0, shared1, shared2,
            mixk, mixv, mixr, mixo, decay, first_share, mix_scale, fc, mlp, mlp_scale,
            gate1, gate1_bias, w1, w2, w3, identity, upto_diagonal, out):
    TILES0 = (2 * T + E * (P - 1)) // P
    TILES0 += -TILES0 % 4
    CAPACITY = T * 5 // (4 * E)
    TILES1 = E * CAPACITY // P

    taken.clear()

    def scratch(name, *shape):
        return nc.dram_tensor(name, list(shape), F32).ap()

    rows = [scratch(f"rows{i}", T, D) for i in range(4)]
    sums = [scratch(f"sums{i}", T, D) for i in range(4)]
    expert_rows = [scratch("expert_rows0", TILES0 * P, D), scratch("expert_rows1", TILES1 * P + 1, D)]
    with ExitStack() as ctx:
        m = Mem(nc, ctx, "all")
        ident, upto = m.sb("ident", [P, P]), m.sb("upto", [P, P])
        loaded = m.sem("loaded")
        with nc.Block() as block:
            @block.sync
            def _(sp):
                sp.dma_start(ident[:, :], identity).then_inc(loaded, 16)
                sp.dma_start(upto[:, :], upto_diagonal).then_inc(loaded, 16)
                sp.wait_ge(loaded, 32)

        qk = scratch("qk", 2, 2, D, T)
        v = scratch("v", PAIRS, P, TT, 2 * VW)
        context, prob_sums = scratch("context", D, T), scratch("prob_sums", H, T)
        project_qkv(nc, hidden_T, Wq, bq, Wk, bk, Wv, bv, qk, v)
        attend(nc, qk, v, ident, context, prob_sums)
        merge_heads(nc, hidden, context, prob_sums, ident, sums[0])

        xT = m.sb("xT", [P, KD, T])
        weight, pos = m.sb("weight", [P, 2, TT]), m.sb("pos", [P, 2, TT], I32)
        table0, table1 = m.sb("table0", [P, TILES0], I32), m.sb("table1", [P, TILES1], I32)
        tile_expert = m.sb("tile_expert", [P, TILES0], I32)
        normalise(nc, "ln0", sums[0], rows[0], ident, xT, True, False)
        route(nc, "route0", xT, gate0, None, ident, upto, None, weight, pos, table0, tile_expert)
        experts_gelu(nc, rows[0], up0, down0, ident, table0, tile_expert, expert_rows[0])
        combine(nc, "combine0", rows[0], expert_rows[0], pos, weight, sums[1], xT, shared1, shared2)

        nc.clear_and_free_semaphores(taken)
        nc.all_engine_barrier()
        taken.clear()

        normalise(nc, "ln1", sums[1], rows[1], ident, xT, True, True)
        mix_tokens(nc, xT, rows[1], mixk, mixv, mixr, mixo, decay, first_share, mix_scale, rows[2])
        normalise(nc, "rms", rows[2], None, ident, xT, False, True)
        mix_channels(nc, xT, rows[1], rows[2], fc, mlp, mlp_scale, sums[2])

        normalise(nc, "ln2", sums[2], rows[3], ident, xT, True, False)
        route(nc, "route1", xT, gate1, gate1_bias, ident, upto, CAPACITY, weight, pos, table1, None)
        experts_silu(nc, rows[3], w1, w2, w3, ident, table1, CAPACITY, expert_rows[1])
        combine(nc, "combine1", rows[3], expert_rows[1], pos, weight, sums[3])
        normalise(nc, "ln3", sums[3], out, ident, None, True, False)


def kernel(**inputs):
    import numpy as np
    import concourse.bacc as bacc
    from concourse import mybir as _mybir
    from concourse.bass_utils import run_bass_kernel_spmd

    def plain(name):
        return np.ascontiguousarray(inputs[name])

    def turned(name):
        return np.ascontiguousarray(np.asarray(inputs[name]).T)

    hidden = np.ascontiguousarray(np.asarray(inputs["L0_attn_hidden_states"]).reshape(T, D))
    arrays = [hidden, np.ascontiguousarray(hidden.T),
              turned("L0_attn_Wq"), plain("L0_attn_bq"), turned("L0_attn_Wk"), plain("L0_attn_bk"),
              turned("L0_attn_Wv"), plain("L0_attn_bv"),
              plain("L0_ffn_Wg"), plain("L0_ffn_Wu"), plain("L0_ffn_Wd"), plain("L0_ffn_W1"), plain("L0_ffn_W2"),
              turned("L1_attn_Wk"), turned("L1_attn_Wv"), turned("L1_attn_Wr"), turned("L1_attn_Wo"),
              plain("L1_attn_time_decay"), plain("L1_attn_time_first"), plain("L1_attn_mixer_scale"),
              turned("L1_attn_Wfc"), turned("L1_attn_Wmlp"), plain("L1_attn_mlp_scale"),
              plain("L1_ffn_Wg"), plain("L1_ffn_bg"), plain("L1_ffn_W1"), plain("L1_ffn_W2"), plain("L1_ffn_W3"),
              np.eye(P, dtype=np.float32), np.triu(np.ones((P, P), np.float32))]
    nc = bacc.Bacc("TRN2", target_bir_lowering=False, num_devices=1)
    named = {f"in_{i}_dram": a for i, a in enumerate(arrays)}
    args = [nc.dram_tensor(name, a.shape, _mybir.dt.from_np(a.dtype), kind="ExternalInput").ap()
            for name, a in named.items()]
    out = nc.dram_tensor("out_0_dram", (T, D), _mybir.dt.float32, kind="ExternalOutput").ap()
    network(nc, *args, out)
    result = run_bass_kernel_spmd(nc, [named], core_ids=[0])
    return result.results[0]["out_0_dram"].reshape(1, T, D)
```

```python
from contextlib import ExitStack

import concourse.bass as bass
from concourse import mybir

F32 = mybir.dt.float32
F32R = mybir.dt.float32r
I32 = mybir.dt.int32
U32 = mybir.dt.uint32
ALU = mybir.AluOpType
ACT = mybir.ActivationFunctionType
AX = mybir.AxisListType

P = 128
T = 4096
D = 256
KD = D // P
TT = T // P
GRP = 512
NGRP = T // GRP
GT = GRP // P
H, HD = 16, 16
BLK = 64
NBLK = T // BLK
PAIRS = H // 2
VW = HD + 1
E = 8
LN_EPS = 1e-5
RMS_EPS = 1e-6



taken = []


class Mem:

    def __init__(self, nc, ctx, tag):
        self.nc, self.ctx, self.tag = nc, ctx, tag

    def sb(self, name, shape, dt=F32):
        return self.ctx.enter_context(self.nc.sbuf_tensor(f"{self.tag}_{name}", shape, dt))

    def ps(self, name, shape, dt=F32):
        return self.ctx.enter_context(self.nc.psum_tensor(f"{self.tag}_{name}", shape, dt))

    def sem(self, name):
        sem = self.nc.alloc_semaphore(f"{self.tag}_{name}")
        taken.append(sem)
        return sem


def row(ap):
    return ap.rearrange("(a d) -> a d", a=1)


def token_rows(a, g):
    return a[bass.ds(g * GRP, GRP), :].rearrange("(j p) d -> p j d", p=P)


def project_qkv(nc, hsT, WqT, bq, WkT, bk, WvT, bv, qk_d, v_d):
    with ExitStack() as ctx:
        m = Mem(nc, ctx, "qkv")
        w = m.sb("w", [P, 3, KD, D])
        b_col = m.sb("b_col", [P, 2, KD])
        b_colq = m.sb("b_colq", [P, 2, KD])
        bv_row = m.sb("bv_row", [P, D])
        x = [m.sb(f"x{i}", [P, KD, GRP]) for i in range(2)]
        whole = m.sb("whole", [P, 2, GRP])
        part = [m.sb(f"part{i}", [P, 2, GRP], F32R) for i in range(2)]
        v = m.sb("v", [P, PAIRS, TT, 2, VW])
        qk_ps = [m.ps(f"qk_ps{i}", [P, GRP]) for i in range(2)]
        v_ps = [m.ps(f"v_ps{i}", [P, D]) for i in range(2)]
        weights_in, ones_set, scaled = m.sem("weights_in"), m.sem("ones_set"), m.sem("scaled")
        x_in = [m.sem(f"x_in{i}") for i in range(2)]
        qk_done, whole_done, high_done = (m.sem("qk_done"),
                                                  m.sem("whole_done"), m.sem("high_done"))
        low_done, v_done, v_copied = m.sem("low_done"), m.sem("v_done"), m.sem("v_copied")
        part_out = [m.sem(f"part_out{i}") for i in range(2)]
        v_out = m.sem("v_out")
        NW = 8 * 16
        block = ctx.enter_context(nc.Block())

        @block.sync
        def _(sp):
            for i, a in enumerate((WqT, WkT, WvT)):
                sp.dma_start(w[:, i], a.rearrange("(k p) n -> p k n", p=P)).then_inc(weights_in, 16)
            for i, a in enumerate((bq, bk)):
                for k in range(KD):
                    sp.dma_start(b_col[:, i, k:k + 1],
                                 a[k * P:(k + 1) * P].rearrange("(p a) -> p a", a=1)).then_inc(weights_in, 16)
            sp.dma_start(bv_row[:, :], row(bv).broadcast_to([P, D])).then_inc(weights_in, 16)
            src = hsT.rearrange("(k p) t -> p k t", p=P)
            with sp.Fori(0, NGRP // 2) as i:
                for s in range(2):
                    sp.wait_ge(v_done, 8 * i)
                    sp.dma_start(x[s][:, :, :], src[:, :, bass.ds(i * 2 * GRP + s * GRP, GRP)]).then_inc(x_in[s], 16)

        @block.scalar
        def _(act):
            act.wait_ge(weights_in, NW)
            act.wait_ge(scaled, 1)
            with act.Fori(0, NGRP) as i:
                for j in range(4):
                    t, g = j // 2, j % 2
                    act.wait_ge(qk_done, 4 * i + j + 1)
                    act.wait_ge(low_done, 4 * i + max(j - 1, 0))
                    nc.scalar.activation(whole[:, j % 2, :], qk_ps[j % 2][:, :], ACT.Identity,
                                         bias=b_colq[:, t, g:g + 1],
                                         scale=0.25 if t == 0 else 1.0).then_inc(whole_done, 1)

        @block.vector
        def _(dve):
            nc.vector.memset(v[:, :, :, :, HD:VW], 1.0).then_inc(ones_set, 1)
            dve.wait_ge(weights_in, NW)
            nc.vector.tensor_scalar(b_colq[:, 0, :], b_col[:, 0, :], 0.25, None, ALU.mult)
            nc.vector.tensor_copy(b_colq[:, 1, :], b_col[:, 1, :]).then_inc(scaled, 1)
            with dve.Fori(0, NGRP) as i:
                for j in range(4):
                    s = j % 2
                    dve.wait_ge(whole_done, 4 * i + j + 1)
                    dve.wait_ge(part_out[s], 32 * 2 * i + 32 * (j // 2))
                    nc.vector.tensor_copy(part[s][:, 0, :], whole[:, s, :]).then_inc(high_done, 1)
                    dve.wait_ge(high_done, 4 * i + j + 1)
                    nc.vector.tensor_tensor(part[s][:, 1, :], whole[:, s, :], part[s][:, 0, :].bitcast(F32),
                                            ALU.subtract).then_inc(low_done, 1)
                    dve.wait_ge(v_done, 4 * i + j + 1)
                    nc.vector.tensor_tensor(
                        v[:, :, bass.ds(4 * i + j, 1), :, 0:HD].rearrange("p h t a d -> p (h t) a d"),
                        v_ps[s][:, :].rearrange("p (a h d) -> p h a d", a=2, d=HD),
                        bv_row[:, :].rearrange("p (a h d) -> p h a d", a=2, d=HD), ALU.add).then_inc(v_copied, 1)

        @block.tensor
        def _(pe):
            pe.wait_ge(weights_in, NW)
            with pe.Fori(0, NGRP // 2) as i2:
                for s in range(2):
                    i = 2 * i2 + s
                    pe.wait_ge(x_in[s], 16 * i2 + 16)
                    for j in range(4):
                        t, g = j // 2, j % 2
                        pe.wait_ge(whole_done, 4 * i + max(j - 1, 0))
                        for k in range(KD):
                            mm = nc.tensor.matmul(qk_ps[j % 2][:, :], w[:, t, k, g * P:(g + 1) * P], x[s][:, k, :],
                                                  start=(k == 0), stop=(k == KD - 1))
                        mm.then_inc(qk_done, 1)
                        pe.wait_ge(v_copied, 4 * i + max(j - 1, 0))
                        for k in range(KD):
                            mm = nc.tensor.matmul(v_ps[j % 2][:, :], x[s][:, k, j * P:(j + 1) * P], w[:, 2, k, :],
                                                  start=(k == 0), stop=(k == KD - 1))
                        mm.then_inc(v_done, 1)


        @block.gpsimd
        def _(pool):
            dst = qk_d.rearrange("t h (g p) n -> p t h g n", p=P)
            with pool.Fori(0, NGRP) as i:
                for j in range(4):
                    t, g = j // 2, j % 2
                    pool.wait_ge(low_done, 4 * i + j + 1)
                    for h in range(2):
                        pool.dma_start(dst[:, t, h, g, bass.ds(i * GRP, GRP)], part[j % 2][:, h, :].bitcast(F32)).then_inc(part_out[j % 2], 16)
            pool.wait_ge(v_copied, TT)
            pool.wait_ge(ones_set, 1)
            pool.dma_start(v_d.rearrange("h p t v -> p h t v"),
                           v[:, :, :, :, :].rearrange("p h t a v -> p h t (a v)")).then_inc(v_out, 16)
            pool.wait_ge(v_out, 16)
            for s in range(2):
                pool.wait_ge(part_out[s], 32 * 2 * NGRP)


def attend(nc, qk_d, v_d, ident, ctx_d, sums_d):
    FULL = 16
    BAND = (NBLK - 2) // 2
    STEPS = FULL + BAND
    UNITS = FULL + 2 * BAND
    LEAD = 3
    WARM = 12
    ROWS, MROW = 97, 96
    CHUNKS = 4
    CB = NBLK // CHUNKS
    CT = T // CHUNKS
    LOCAL = 3 * BLK
    with ExitStack() as ctx:
        m = Mem(nc, ctx, "att")
        q = [m.sb(f"q{i}", [P, NBLK, 2 * BLK], F32R) for i in range(2)]
        k = [m.sb(f"k{i}", [P, T + BLK], F32R) for i in range(2)]
        kgm = [m.sb(f"kgm{i}", [P, 2 * BLK], F32R) for i in range(2)]
        kg = [m.sb(f"kg{i}", [P, 2 * BLK], F32R) for i in range(2)]
        ve = [m.sb(f"ve{i}", [P, TT, 2 * VW]) for i in range(2)]
        vo = [m.sb(f"vo{i}", [P, TT, 2 * VW]) for i in range(2)]
        vg = [m.sb(f"vg{i}", [P, 3, 2 * VW]) for i in range(2)]
        neg_max = m.sb("neg_max", [P, NBLK])
        chunk_max = m.sb("chunk_max", [P, 2, FULL // 2])
        max_row = m.sb("max_row", [NBLK, P], F32R)
        prob = [m.sb(f"prob{i}", [P, 4 * P]) for i in range(2)]
        prob_c = [m.sb(f"prob_c{i}", [BLK, 2 * P]) for i in range(2)]
        raw = [m.sb(f"raw{i}", [2 * VW, NBLK, 2 * BLK]) for i in range(2)]
        m_ps = [m.ps(f"m_ps{i}", [P, 512]) for i in range(2)]
        s_ps = [m.ps(f"s_ps{i}", [P, 512]) for i in range(2)]
        c_ps = [m.ps(f"c_ps{i}", [P, 2 * P]) for i in range(2)]
        o_ps = [m.ps(f"o_ps{i}", [P, 512]) for i in range(2)]
        qk_in = [m.sem(f"qk_in{c}") for c in range(CHUNKS)]
        kg_in, v_in, cleared = m.sem("kg_in"), m.sem("v_in"), m.sem("cleared")
        globals_ready = m.sem("globals_ready")
        m_done, m_reduced, max_ready = m.sem("m_done"), m.sem("m_reduced"), m.sem("max_ready")
        row_turned, row_ready, row_in = m.sem("row_turned"), m.sem("row_ready"), m.sem("row_in")
        s_done, exp_done, pv_done, o_out = m.sem("s_done"), m.sem("exp_done"), m.sem("pv_done"), m.sem("o_out")
        raw_out = [m.sem(f"raw_out{i}") for i in range(2)]
        passed = m.sem("passed")
        block = ctx.enter_context(nc.Block())

        def rounds(eng, one):
            one(0, None, 0)
            with eng.Fori(0, PAIRS // 2 - 1) as j:
                one(2 * j + 1, 2 * j, 1)
                one(2 * j + 2, 2 * j + 1, 0)
            one(PAIRS - 1, PAIRS - 2, 1)
            one(None, PAIRS - 1, 0)

        def m_units(s):
            return [2 * s, 2 * s + 1] if s < BAND else [BAND + s]

        def m_stream(p, b):
            steps = [] if p is None else [(p, b, s) for s in range(LEAD, STEPS)]
            if p is not None and b_next(p):
                steps += [(p + 1, 1 - b, s) for s in range(LEAD)]
            return steps

        def b_next(p):
            return not (isinstance(p, int) and p == PAIRS - 1)

        @block.sync
        def _(sp):
            qk = qk_d.rearrange("t h (a f) n -> t h a f n", a=2)

            def head(p, t, h, a):
                return qk[t, h, a, bass.ds(p * HD, HD), :]

            def load_globals(p, b):
                for a in range(2):
                    for i, h in enumerate((0, 1, 0)):
                        r = 48 * a + 16 * i
                        sp.dma_start(kgm[b][r:r + HD, :].rearrange("f (g t) -> f g t", g=2).bitcast(F32),
                                     head(p, 1, h, a).rearrange("f (l t) -> f l t", t=BLK)[:, 0:NBLK:NBLK - 1, :]
                                     ).then_inc(kg_in, 16)

            def load_chunk(p, b, c):
                for a in range(2):
                    for i, (hq, hk) in enumerate(((0, 0), (0, 1), (1, 0))):
                        r = 48 * a + 16 * i
                        sp.dma_start(q[b][r:r + HD, c * CB:(c + 1) * CB, a * BLK:(a + 1) * BLK].bitcast(F32),
                                     head(p, 0, hq, a)[:, c * CT:(c + 1) * CT].rearrange("f (l t) -> f l t", t=BLK)
                                     ).then_inc(qk_in[c], 16)
                        sp.dma_start(k[b][r:r + HD, c * CT:(c + 1) * CT].bitcast(F32),
                                     head(p, 1, hk, a)[:, c * CT:(c + 1) * CT]).then_inc(qk_in[c], 16)

            def load_values(p, b):
                vp = v_d[bass.ds(p, 1)].rearrange("h p t v -> (h p) t v")
                sp.dma_start(ve[b][:, :, :], vp).then_inc(v_in, 16)
                sp.dma_start(vo[b][0:BLK, :, :], vp[BLK:P]).then_inc(v_in, 16)
                sp.dma_start(vo[b][BLK:P, 0:TT - 1, :], vp[0:BLK, 1:TT]).then_inc(v_in, 16)

            sp.wait_ge(cleared, 1)
            for p in range(2):
                load_globals(p, p)
                for c in range(CHUNKS):
                    load_chunk(p, p, c)
                    sp.wait_ge(qk_in[c], 192 * (p + 1))
                load_values(p, p)
                sp.wait_ge(kg_in, 96 * (p + 1))
                sp.wait_ge(v_in, 48 * (p + 1))

            def refill(p, b):
                load_globals(p + 1, 1 - b)
                for c in range(CHUNKS):
                    sp.wait_ge(s_done, (p - 1) * STEPS + FULL + min(CB // 2 * (c + 1), BAND))
                    sp.sem_inc(passed, 1)
                    load_chunk(p + 1, 1 - b, c)
                sp.wait_ge(pv_done, p * STEPS)
                load_values(p + 1, 1 - b)

            with sp.Fori(0, PAIRS // 2 - 1) as j:
                for r in range(2):
                    sp.wait_ge(globals_ready, 2 * j + 1 + r)
                    refill(2 * j + 1 + r, (1 + r) % 2)

        @block.tensor
        def _(pe):
            def maxima(p, b, s):
                if s == 0:
                    pe.wait_ge(kg_in, 96 * (p + 1))
                    pe.wait_ge(row_ready, p)
                for c in range(CHUNKS):
                    if s < BAND and (2 * s + 3) // CB == c and (s == 0 or (2 * s + 1) // CB < c):
                        pe.wait_ge(qk_in[c], 192 * (p + 1))
                for u in m_units(s):
                    pe.wait_ge(m_reduced, p * UNITS + max(u - 1, 0))
                    bank = m_ps[u % 2]
                    if u < 2 * BAND:
                        l = 1 + u
                        nc.tensor.matmul(bank[:, 0:LOCAL], q[b][0:MROW, l, :],
                                         k[b][0:MROW, (l - 1) * BLK:(l + 2) * BLK], start=True, stop=True)
                        nc.tensor.matmul(bank[:, LOCAL:LOCAL + 2 * BLK], q[b][0:MROW, l, :], kgm[b][0:MROW, :],
                                         start=True, stop=True).then_inc(m_done, 1)
                    else:
                        f = u - 2 * BAND
                        l, chunk = (0 if f < FULL // 2 else NBLK - 1), f % (FULL // 2)
                        nc.tensor.matmul(bank[:, :], q[b][0:MROW, l, :], k[b][0:MROW, chunk * 512:(chunk + 1) * 512],
                                         start=True, stop=True).then_inc(m_done, 1)

            def turn(p):
                pe.wait_ge(max_ready, p + 1)
                pe.sem_inc(passed, 1)
                nc.tensor.transpose(m_ps[0][0:NBLK, 0:P], neg_max[:, :], ident[:, :]).then_inc(row_turned, 1)

            def scores(e, c, s):
                if s == 0:
                    pe.wait_ge(row_in, 16 * (e + 1))
                if s == FULL:
                    pe.wait_ge(globals_ready, e + 1)
                pe.wait_ge(exp_done, e * STEPS + max(s - 1, 0))
                bank = s_ps[s % 2]
                if s < FULL:
                    for i in range(2):
                        t = 2 * s + i
                        for j, l in enumerate((0, NBLK - 1)):
                            o = (2 * i + j) * P
                            mm = nc.tensor.matmul(bank[:, o:o + P], k[c][0:ROWS, t * P:(t + 1) * P],
                                                  q[c][0:ROWS, l, :], start=True, stop=True)
                else:
                    l0 = 1 + 2 * (s - FULL)
                    nc.tensor.matmul(bank[:, 2 * P:4 * P], kg[c][0:ROWS, :],
                                     q[c][0:ROWS, l0:l0 + 2, :].rearrange("p l t -> p (l t)"), start=True, stop=True)
                    for j in range(2):
                        l = l0 + j
                        nc.tensor.matmul(bank[:, j * P:(j + 1) * P], k[c][0:ROWS, (l - 1) * BLK:(l + 1) * BLK],
                                         q[c][0:ROWS, l, :], start=True, stop=True)
                        mm = nc.tensor.matmul(c_ps[s % 2][:, j * P:(j + 1) * P],
                                              k[c][0:ROWS, (l + 1) * BLK:(l + 3) * BLK],
                                              q[c][0:ROWS, l, :], start=True, stop=True)
                mm.then_inc(s_done, 1)

            def values(e, c, s):
                pe.wait_ge(exp_done, e * STEPS + s + 1)
                pr, prc = prob[s % 2], prob_c[s % 2]
                if s < FULL:
                    if s == 0:
                        pe.wait_ge(v_in, 48 * (e + 1))
                        pe.wait_ge(o_out, e * (BAND + 1))
                        for _ in range(WARM):
                            nc.tensor.matmul(o_ps[0][:, :], k[c][0:MROW, 0:P], k[c][0:MROW, 0:512], start=True, stop=True)
                    for i in range(2):
                        t = 2 * s + i
                        mm = nc.tensor.matmul(o_ps[1][0:2 * VW, 0:2 * P], ve[c][:, t, :],
                                              pr[:, 2 * i * P:2 * (i + 1) * P], start=(t == 0), stop=(t == TT - 1))
                else:
                    n = s - FULL
                    pe.wait_ge(o_out, e * (BAND + 1) + max(n, 1))
                    out = o_ps[n % 2]
                    l0 = 1 + 2 * n
                    if l0 == 1:
                        parts = ((1, 0, P), (0, P, 2 * P))
                    elif l0 == NBLK - 3:
                        parts = ((0, 0, P), (2, P, 2 * P))
                    else:
                        parts = ((0, 0, 2 * P),)
                    for i, (g, x0, x1) in enumerate(parts):
                        nc.tensor.matmul(out[0:2 * VW, x0:x1], vg[c][:, g, :], pr[:, 2 * P + x0:2 * P + x1],
                                         start=(i == 0), stop=False, skip_group_check=True)
                    for j in range(2):
                        l = l0 + j
                        vl, t = (vo[c], l // 2 - 1) if l % 2 == 0 else (ve[c], (l - 1) // 2)
                        o = out[0:2 * VW, j * P:(j + 1) * P]
                        nc.tensor.matmul(o, vl[:, t, :], pr[:, j * P:(j + 1) * P], start=False, stop=False,
                                         skip_group_check=True)
                        mm = nc.tensor.matmul(o, vl[0:BLK, t + 1, :], prc[:, j * P:(j + 1) * P],
                                              start=False, stop=True, skip_group_check=True)
                mm.then_inc(pv_done, 1)

            def one(p, e, b):
                ms = m_stream(p, b)
                for s in range(STEPS):
                    if e is not None:
                        scores(e, 1 - b, s)
                    if p is not None and s == STEPS - LEAD:
                        if e is not None:
                            values(e, 1 - b, s - 1)
                        turn(p)
                    if s < len(ms):
                        maxima(*ms[s])
                    if e is not None and s > 0 and (p is None or s != STEPS - LEAD):
                        values(e, 1 - b, s - 1)
                if e is not None:
                    values(e, 1 - b, STEPS - 1)

            pe.wait_ge(cleared, 1)
            for s in range(LEAD):
                maxima(0, 0, s)
            rounds(pe, one)

        @block.scalar
        def _(act):
            def one(p, e, b):
                if e is None:
                    return
                for s in range(STEPS):
                    act.wait_ge(s_done, e * STEPS + s + 1)
                    act.wait_ge(pv_done, e * STEPS + max(s - 1, 0))
                    ins = nc.scalar.activation(prob[s % 2][:, :], s_ps[s % 2][:, :], ACT.Exp)
                    if s >= FULL:
                        ins = nc.scalar.activation(prob_c[s % 2][:, :], c_ps[s % 2][0:BLK, :], ACT.Exp)
                    ins.then_inc(exp_done, 1)
                    out(e, 1 - b, s - 2)
                out(e, 1 - b, STEPS - 2)
                out(e, 1 - b, STEPS - 1)

            def out(e, c, s):
                if s < FULL - 1:
                    return
                act.wait_ge(pv_done, e * STEPS + s + 1)
                if s == FULL - 1:
                    if not isinstance(e, int) or e > 0:
                        act.wait_ge(raw_out[c], 64 * (e // 2))
                    for j, l in enumerate((0, NBLK - 1)):
                        ins = nc.scalar.copy(raw[c][:, l, :], o_ps[1][0:2 * VW, j * P:(j + 1) * P])
                else:
                    n = s - FULL
                    ins = nc.scalar.copy(raw[c][:, 1 + 2 * n:3 + 2 * n, :].rearrange("p l t -> p (l t)"),
                                         o_ps[n % 2][0:2 * VW, 0:2 * P])
                ins.then_inc(o_out, 1)

            rounds(act, one)

        @block.vector
        def _(dve):
            for b in range(2):
                nc.vector.memset(vg[b][:, :, :].bitcast(U32), 0)
                nc.vector.memset(q[b][:, :, :].bitcast(U32), 0)
                nc.vector.memset(k[b][0:MROW, T:T + BLK].bitcast(U32), 0)
                nc.vector.memset(kgm[b][MROW:ROWS, :].bitcast(F32), 1.0)
                ins = nc.vector.memset(k[b][MROW:ROWS, :].bitcast(F32), 1.0)
            ins.then_inc(cleared, 1)

            def maximum(p, s):
                if s == 0:
                    dve.wait_ge(row_turned, p)
                for u in m_units(s):
                    dve.wait_ge(m_done, p * UNITS + u + 1)
                    if u < 2 * BAND:
                        l = 1 + u
                        ins = nc.vector.tensor_reduce(neg_max[:, l:l + 1], m_ps[u % 2][:, 0:LOCAL + 2 * BLK], AX.X,
                                                      ALU.max, negate=True)
                    else:
                        f = u - 2 * BAND
                        ins = nc.vector.tensor_reduce(chunk_max[:, f // 8, f % 8:f % 8 + 1], m_ps[u % 2][:, :],
                                                      AX.X, ALU.max)
                    ins.then_inc(m_reduced, 1)

            def close(p, b):
                dve.wait_ge(m_reduced, (p + 1) * UNITS)
                for i, l in enumerate((0, NBLK - 1)):
                    ins = nc.vector.tensor_reduce(neg_max[:, l:l + 1], chunk_max[:, i, :], AX.X, ALU.max, negate=True)
                ins.then_inc(max_ready, 1)
                dve.wait_ge(row_turned, p + 1)
                dve.wait_ge(row_in, 16 * p)
                nc.vector.tensor_copy(max_row[:, :], m_ps[0][0:NBLK, 0:P]).then_inc(row_ready, 1)
                if not isinstance(p, int) or p > 0:
                    dve.wait_ge(pv_done, (p - 1) * STEPS)
                nc.vector.tensor_copy(kg[b][0:ROWS, :], kgm[b][0:ROWS, :].bitcast(F32))
                dve.wait_ge(v_in, 48 * (p + 1))
                nc.vector.tensor_copy(vg[b][0:BLK, 0, :], ve[b][0:BLK, 0, :])
                nc.vector.tensor_copy(vg[b][0:BLK, 2, :], ve[b][0:BLK, 0, :])
                nc.vector.tensor_copy(vg[b][BLK:P, 0, :], ve[b][BLK:P, TT - 1, :])
                nc.vector.tensor_copy(vg[b][BLK:P, 1, :], ve[b][BLK:P, TT - 1, :]).then_inc(globals_ready, 1)

            def one(p, e, b):
                for pm, bm, s in m_stream(p, b):
                    maximum(pm, s)
                    if s == STEPS - 1:
                        close(pm, bm)

            for s in range(LEAD):
                maximum(0, s)
            rounds(dve, one)

        @block.gpsimd
        def _(pool):
            def one(p, e, b):
                if p is not None:
                    pool.wait_ge(row_ready, p + 1)
                    pool.sem_inc(passed, 1)
                    pool.dma_start(q[b][MROW:MROW + 1, :, :].rearrange("p l t -> p (l t)").bitcast(F32),
                                   max_row[:, :].bitcast(F32)).then_inc(row_in, 16)
                if e is not None:
                    pool.wait_ge(o_out, (e + 1) * (BAND + 1))
                    for a in range(2):
                        cols = raw[1 - b][a * VW:(a + 1) * VW, :, a * BLK:(a + 1) * BLK]
                        pool.dma_start(heads[a, bass.ds(e * HD, HD)].rearrange("f (l t) -> f l t", t=BLK),
                                       cols[0:HD]).then_inc(raw_out[1 - b], 16)
                        pool.dma_start(sums[a, bass.ds(e, 1)].rearrange("f (l t) -> f l t", t=BLK),
                                       cols[HD:VW]).then_inc(raw_out[1 - b], 16)

            heads = ctx_d.rearrange("(a f) n -> a f n", a=2)
            sums = sums_d.rearrange("(a f) n -> a f n", a=2)
            rounds(pool, one)
            for c in range(2):
                pool.wait_ge(raw_out[c], 64 * PAIRS // 2)


def beyond(g, n):
    return not isinstance(g, int) or g > n


def skewed(eng, first, last, step):
    for g in range(first, 2):
        step(g, g % 2)
    with eng.Fori(1, NGRP // 2 - 1) as i:
        step(2 * i, 0)
        step(2 * i + 1, 1)
    for g in range(NGRP - 2, NGRP + last):
        step(g, g % 2)


def exists(g):
    return not isinstance(g, int) or 0 <= g < NGRP


class Norm:

    def __init__(self, nc, m, x, ready, out_d, ident=None, xT=None):
        self.nc, self.x, self.ready, self.out_d, self.ident, self.xT = nc, x, ready, out_d, ident, xT
        self.y = [m.sb(f"y{i}", [P, GT, D]) for i in range(2)]
        self.part = [m.sb(f"part{i}", [P, GT, 6]) for i in range(2)]
        self.mean_var = [m.sb(f"mean_var{i}", [P, GT, 2]) for i in range(2)]
        self.std = [m.sb(f"std{i}", [P, GT]) for i in range(2)]
        self.inv = [m.sb(f"inv{i}", [P, GT]) for i in range(2)]
        self.eps = m.sb("eps", [P, 1])
        self.bank = [m.ps(f"turn{k}", [P, GRP]) for k in range(KD)] if xT is not None else None
        self.eps_set, self.parted, self.aggregated, self.std_done, self.inv_done, self.normed = (
            m.sem(a) for a in ("eps_set", "parted", "aggregated", "std_done", "inv_done", "normed"))
        self.turned, self.copied, self.passed = m.sem("turned"), m.sem("copied"), m.sem("ln_passed")
        self.stored = [m.sem(f"stored{i}") for i in range(2)]

    def begin(self):
        self.nc.vector.memset(self.eps[:, :], LN_EPS).then_inc(self.eps_set, 1)

    def stats(self, dve, g, s):
        dve.wait_ge(self.ready, GT * (g + 1))
        for j in range(GT):
            self.nc.vector.bn_stats(self.part[s][:, j, :], self.x[s][:, j, :]).then_inc(self.parted, 1)
        dve.wait_ge(self.parted, GT * (g + 1))
        dve.sem_inc(self.passed, 1)
        for j in range(GT):
            self.nc.vector.bn_aggr(self.mean_var[s][:, j, :], self.part[s][:, j, :]).then_inc(self.aggregated, 1)

    def root(self, act, g, s):
        act.wait_ge(self.eps_set, 1)
        act.wait_ge(self.aggregated, GT * (g + 1))
        if beyond(g, 1):
            act.wait_ge(self.inv_done, g - 1)
        var = self.mean_var[s][:, :, 1:2].rearrange("p g a -> p (g a)")
        self.nc.scalar.activation(self.std[s][:, :], var, ACT.Sqrt, bias=self.eps[:, 0:1]).then_inc(self.std_done, 1)

    def apply(self, dve, g, s):
        dve.wait_ge(self.std_done, g + 1)
        self.nc.vector.reciprocal(self.inv[s][:, :], self.std[s][:, :]).then_inc(self.inv_done, 1)
        if beyond(g, 1):
            dve.wait_ge(self.stored[s], 16 * (g // 2))
            if self.xT is not None:
                dve.wait_ge(self.turned, KD * (g - 1))
        dve.wait_ge(self.inv_done, g + 1)
        for j in range(GT):
            self.nc.vector.tensor_scalar(self.y[s][:, j, :], self.x[s][:, j, :], self.mean_var[s][:, j, 0:1],
                                         self.inv[s][:, j:j + 1], ALU.subtract, ALU.mult).then_inc(self.normed, 1)

    def turn(self, pe, g, s):
        pe.wait_ge(self.normed, GT * (g + 1))
        for k in range(KD):
            if beyond(g, 0):
                pe.wait_ge(self.copied, KD * (g - 1) + k + 1)
            for j in range(GT):
                mm = self.nc.tensor.transpose(self.bank[k][:, j * P:(j + 1) * P], self.y[s][:, j, k * P:(k + 1) * P],
                                              self.ident[:, :])
            mm.then_inc(self.turned, 1)

    def copy(self, act, g, s):
        for k in range(KD):
            act.wait_ge(self.turned, KD * g + k + 1)
            self.nc.scalar.copy(self.xT[:, k, bass.ds(g * GRP, GRP)], self.bank[k][:, :]).then_inc(self.copied, 1)

    def store(self, sp, g, s):
        sp.wait_ge(self.normed, GT * (g + 1))
        sp.dma_start(token_rows(self.out_d, g), self.y[s][:, :, :]).then_inc(self.stored[s], 16)

    def finish(self, sp):
        for s in range(2):
            sp.wait_ge(self.stored[s], 16 * NGRP // 2)


def merge_heads(nc, hs, ctx_d, sums_d, ident, out_d, xT):
    with ExitStack() as ctx:
        m = Mem(nc, ctx, "merge")
        c = [m.sb(f"c{i}", [P, KD, GRP]) for i in range(2)]
        z = [m.sb(f"z{i}", [H, GRP]) for i in range(2)]
        hidden = [m.sb(f"hidden{i}", [P, GT, D]) for i in range(2)]
        x = [m.sb(f"x{i}", [P, GT, D]) for i in range(2)]
        inv = [m.sb(f"inv_sum{i}", [P, H]) for i in range(2)]
        scaled = [m.sb(f"scaled{i}", [P, D]) for i in range(4)]
        ps = [m.ps(f"ps{i}", [P, 512]) for i in range(4)]
        in_ = [m.sem(f"in{i}") for i in range(2)]
        brought, inverted, multiplied, added = m.sem("brought"), m.sem("inverted"), m.sem("multiplied"), m.sem("added")
        norm = Norm(nc, m, x, added, out_d, ident, xT)
        block = ctx.enter_context(nc.Block())

        @block.sync
        def _(sp):
            def load(g, s):
                toks = bass.ds(g * GRP, GRP)
                sp.dma_start(c[s][:, :, :], ctx_d.rearrange("(k p) t -> p k t", p=P)[:, :, toks]).then_inc(in_[s], 16)
                sp.dma_start(z[s][:, :], sums_d[:, toks]).then_inc(in_[s], 16)
                sp.dma_start(hidden[s][:, :, :], token_rows(hs, g)).then_inc(in_[s], 16)

            def step(g, s):
                if exists(g + 2):
                    if beyond(g, -1):
                        sp.wait_ge(added, GT * (g + 1))
                    load(g + 2, s)
                if exists(g):
                    norm.store(sp, g, s)

            skewed(sp, -2, 0, step)
            norm.finish(sp)

        @block.tensor
        def _(pe):
            def bring(g, s):
                pe.wait_ge(in_[s], 48 * (g // 2 + 1))
                for j in range(GT):
                    if beyond(g, 0):
                        pe.wait_ge(multiplied, GT * (g - 1) + j + 1)
                    cols = slice(j * P, (j + 1) * P)
                    for k in range(KD):
                        nc.tensor.transpose(ps[j][:, k * P:(k + 1) * P], c[s][:, k, cols], ident[:, :])
                    nc.tensor.transpose(ps[j][:, D:D + H], z[s][:, cols], ident[0:H, 0:H]).then_inc(brought, 1)

            def step(g, s):
                if exists(g + 1):
                    bring(g + 1, 1 - s)
                if exists(g - 1):
                    norm.turn(pe, g - 1, 1 - s)

            skewed(pe, -1, 1, step)

        @block.vector
        def _(dve):
            norm.begin()

            def divide(g, s):
                for j in range(GT):
                    n = GT * g + j
                    dve.wait_ge(brought, n + 1)
                    nc.vector.reciprocal(inv[j % 2][:, :], ps[j][:, D:D + H]).then_inc(inverted, 1)
                    if beyond(g, 0):
                        dve.wait_ge(added, n - GT + 1)
                    dve.wait_ge(inverted, n + 1)
                    nc.vector.tensor_tensor(
                        scaled[j][:, :].rearrange("p (h d) -> p h d", h=H),
                        ps[j][:, 0:D].rearrange("p (h d) -> p h d", h=H),
                        inv[j % 2][:, :].rearrange("p (h a) -> p h a", a=1).broadcast_to([P, H, HD]),
                        ALU.mult).then_inc(multiplied, 1)

            def step(g, s):
                if exists(g + 1):
                    divide(g + 1, 1 - s)
                if exists(g):
                    norm.apply(dve, g, s)
                if exists(g + 1):
                    norm.stats(dve, g + 1, 1 - s)

            skewed(dve, -1, 0, step)

        @block.gpsimd
        def _(pool):
            def step(g, s):
                if beyond(g, 1):
                    pool.wait_ge(norm.normed, GT * (g - 1))
                for j in range(GT):
                    pool.wait_ge(multiplied, GT * g + j + 1)
                    nc.gpsimd.tensor_tensor(x[s][:, j, :], scaled[j][:, :], hidden[s][:, j, :], ALU.add).then_inc(added, 1)

            skewed(pool, 0, 0, step)

        @block.scalar
        def _(act):
            def step(g, s):
                if exists(g):
                    norm.root(act, g, s)
                if exists(g - 1):
                    norm.copy(act, g - 1, 1 - s)

            skewed(act, 0, 1, step)


def combine(nc, x_d, y_d, pos, weight, out_d):
    with ExitStack() as ctx:
        m = Mem(nc, ctx, "combine")
        x = [m.sb(f"x{i}", [P, GT, D]) for i in range(2)]
        y = [m.sb(f"y_rows{i}", [P, GT, 2, D]) for i in range(2)]
        row_no = [m.sb(f"row_no{i}", [P, 2, GT], I32) for i in range(2)]
        first, summed, numbered, passed = m.sem("first"), m.sem("summed"), m.sem("numbered"), m.sem("passed")
        x_in, y_in = ([m.sem(f"{a}{i}") for i in range(2)] for a in ("x_in", "y_in"))
        norm = Norm(nc, m, x, summed, out_d)
        block = ctx.enter_context(nc.Block())

        @block.sync
        def _(sp):
            def step(g, s):
                if exists(g):
                    norm.store(sp, g, s)
                if exists(g + 2):
                    sp.dma_start(x[s][:, :, :], token_rows(x_d, g + 2)).then_inc(x_in[s], 16)

            skewed(sp, -2, 0, step)
            norm.finish(sp)

        @block.gpsimd
        def _(pool):
            def step(g, s):
                gather_pairs(nc, pool, g, s, pos, y_d, y, row_no, y_in, numbered, summed, passed)

            skewed(pool, 0, 0, step)

        @block.vector
        def _(dve):
            norm.begin()

            def step(g, s):
                if exists(g + 1):
                    add_pairs(nc, dve, g + 1, 1 - s, weight, x, y, x_in, y_in, first, summed)
                if exists(g):
                    norm.apply(dve, g, s)
                if exists(g + 1):
                    norm.stats(dve, g + 1, 1 - s)

            skewed(dve, -1, 0, step)

        @block.scalar
        def _(act):
            skewed(act, 0, 0, lambda g, s: norm.root(act, g, s))


def gather_pairs(nc, pool, g, s, pos, y_d, y, row_no, y_in, numbered, summed, passed):
    pool.wait_ge(y_in[s], 16 * 2 * GT * (g // 2))
    nc.gpsimd.tensor_copy(row_no[s][:, :, :], pos[:, :, bass.ds(g * GT, GT)]).then_inc(numbered, 1)
    pool.wait_ge(numbered, g + 1)
    if beyond(g, 1):
        pool.wait_ge(summed, GT * (g - 1))
    pool.sem_inc(passed, 1)
    for j in range(GT):
        for a in range(2):
            nc.gpsimd.indirect_dma_start(
                out=y[s][:, j, a, :], out_offset=None, in_=y_d,
                in_offset=bass.IndirectOffsetOnAxis(ap=row_no[s][:, a, j:j + 1], axis=0)).then_inc(y_in[s], 16)


def add_pairs(nc, dve, g, s, weight, x, y, x_in, y_in, first, summed):
    dve.wait_ge(x_in[s], 16 * (g // 2 + 1))
    dve.wait_ge(y_in[s], 16 * 2 * GT * (g // 2 + 1))
    for j in range(GT):
        nc.vector.scalar_tensor_tensor(x[s][:, j, :], y[s][:, j, 0, :], weight[:, 0, bass.ds(g * GT + j, 1)],
                                       x[s][:, j, :], ALU.mult, ALU.add).then_inc(first, 1)
    for j in range(GT):
        dve.wait_ge(first, GT * g + j + 1)
        nc.vector.scalar_tensor_tensor(x[s][:, j, :], y[s][:, j, 1, :], weight[:, 1, bass.ds(g * GT + j, 1)],
                                       x[s][:, j, :], ALU.mult, ALU.add).then_inc(summed, 1)


def route(nc, tag, xT, Wg, bg, ident, upto, capacity, weight, pos, table, tile_expert, shared=None):
    NT = table.shape[1]
    BIG = 3.0e38
    BURSTS = 4
    RING = 2 * TT // BURSTS
    KF = shared[0].shape[1] // P if shared else 1
    with ExitStack() as ctx:
        m = Mem(nc, ctx, tag)
        wg = m.sb("wg", [P, KD, E])
        bias = m.sb("bias", [E, 1])
        logit_row = [m.sb(f"logit_row{i}", [E, GRP]) for i in range(2)]
        S = [P, E, TT]
        value, low, hit, cand, expo = (m.sb(a, S) for a in ("value", "low", "hit", "cand", "expo"))
        one = [m.sb(f"one{a}", S) for a in range(2)]
        labels, tile_sum, upto_tile, place, carry = (m.sb(a, S) for a in ("labels", "tile_sum", "upto_tile", "place", "carry"))
        number = m.sb("number", S)
        top = [m.sb(f"top{a}", [P, TT]) for a in range(2)]
        pick = m.sb("pick", [P, TT])
        total, inv = m.sb("total", [P, TT]), m.sb("inv", [P, TT])
        tiles, end, base = m.sb("tiles", [P, E]), m.sb("end", [P, E]), m.sb("base", [P, E])
        ones_e = m.sb("ones_e", [P, E])
        at_tile = m.sb("at_tile", [P, NT, E])
        tile_no = m.sb("tile_no", [P, NT])
        where = m.sb("where", [P, 2, TT])
        bits = m.sb("bits", [P, 2, TT], I32)
        slot, tile_of = m.sb("slot", [P, 2, TT]), m.sb("tile_of", [P, 2, TT])
        counts_i, tokens_i = m.sb("counts_i", [P, P], I32), m.sb("tokens_i", [P, TT], I32)
        counts, tokens = m.sb("counts", [P, P]), m.sb("tokens", [P, TT])
        ones = m.sb("ones", [P, P])
        in_slot = [m.sb(f"in_slot{i}", [P, P], F32R) for i in range(RING)]
        in_tile = [m.sb(f"in_tile{i}", [P, NT], F32R) for i in range(RING)]
        nothing = m.sb("nothing", [P, P], F32R)
        h_ps = [m.ps(f"h_ps{i}", [P, GRP]) for i in range(2)]
        y_ps = [m.ps(f"y_ps{i}", [P, D]) for i in range(2)]
        row_ps = [bank[0:E, :] for bank in h_ps]
        col_ps = [bank[:, 0:GT * E].rearrange("p (j e) -> p j e", j=GT) for bank in y_ps]
        count_ps, table_ps = m.ps("count_ps", [P, 2, E * TT]), m.ps("table_ps", [P, NT])
        cum_ps, sum_ps = (count_ps[:, i, :].rearrange("p (e t) -> p e t", e=E) for i in range(2))
        if shared:
            w1, w2 = m.sb("w1", [P, KD, KF * P]), m.sb("w2", [P, KF, D])
            x = [m.sb(f"x{i}", [P, GT, D]) for i in range(2)]
            y = [m.sb(f"y{i}", [P, GT, D]) for i in range(2)]
            h = [m.sb(f"h{i}", [P, KF, GRP]) for i in range(2)]
        w_in, h_done, h_ready, y_done, y_copied, summed = (m.sem(a) for a in (
            "w_in", "h_done", "h_ready", "y_done", "y_copied", "summed"))
        x_in, part_out = ([m.sem(f"{a}{i}") for i in range(2)] for a in ("x_in", "part_out"))
        wg_in, row_done, row_copied, turned, logits_in = (m.sem("wg_in"), m.sem("row_done"), m.sem("row_copied"),
                                                          m.sem("turned"), m.sem("logits_in"))
        step, exp_in, exp_done, labels_in, counted = m.sem("step"), m.sem("exp_in"), m.sem("exp_done"), m.sem("labels_in"), m.sem("counted")
        iotas, made, placed = m.sem("iotas"), m.sem("made"), m.sem("placed")
        NW = 16 * (1 + (bg is not None))
        passed = m.sem("passed")
        block = ctx.enter_context(nc.Block())

        @block.sync
        def _(sp):
            sp.dma_start(wg[:, :, :], Wg.rearrange("(k p) e -> p k e", p=P)).then_inc(wg_in, 16)
            if bg is not None:
                sp.dma_start(bias[:, :], bg.rearrange("(e a) -> e a", a=1)).then_inc(wg_in, 16)
            if shared:
                sp.dma_start(w1[:, :, :], shared[0].rearrange("(k p) f -> p k f", p=P)).then_inc(w_in, 16)
                sp.dma_start(w2[:, :, :], shared[1].rearrange("(k p) f -> p k f", p=P)).then_inc(w_in, 16)

                def step(g, s):
                    if exists(g):
                        sp.wait_ge(summed, GT * (g + 1))
                        sp.dma_start(token_rows(shared[3], g), y[s][:, :, :]).then_inc(part_out[s], 16)
                    if exists(g + 2):
                        sp.dma_start(x[s][:, :, :], token_rows(shared[2], g + 2)).then_inc(x_in[s], 16)

                skewed(sp, -2, 0, step)
                for s in range(2):
                    sp.wait_ge(part_out[s], 16 * NGRP // 2)

        @block.tensor
        def _(pe):
            pe.wait_ge(wg_in, NW)
            with pe.Fori(0, NGRP // 2) as i:
                for s in range(2):
                    g = 2 * i + s
                    pe.wait_ge(row_copied, 2 * i)
                    for k in range(KD):
                        mm = nc.tensor.matmul(row_ps[s], wg[:, k, :], xT[:, k, bass.ds(g * GRP, GRP)],
                                              start=(k == 0), stop=(k == KD - 1))
                    mm.then_inc(row_done, 1)
                for s in range(2):
                    g = 2 * i + s
                    pe.wait_ge(row_copied, g + 1)
                    pe.wait_ge(logits_in, 2 * i)
                    pe.sem_inc(passed, 1)
                    for j in range(GT):
                        mm = nc.tensor.transpose(col_ps[s][:, j, :], logit_row[s][:, j * P:(j + 1) * P], ident[0:E, 0:E])
                    mm.then_inc(turned, 1)

            def counts_of_labels():
                pe.wait_ge(labels_in, 1)
                flat = labels[:, :, :].rearrange("p e t -> p (e t)")
                nc.tensor.matmul(count_ps[:, 1, :], ones[:, :], flat, start=True, stop=True)
                nc.tensor.matmul(count_ps[:, 0, :], upto[:, :], flat, start=True, stop=True).then_inc(counted, 1)
                nc.tensor.matmul(table_ps[:, :], nothing[:, :], nothing[:, 0:NT], start=True, stop=False,
                                 skip_group_check=True)

            def burst(q):
                for r in range(RING):
                    pe.wait_ge(made, RING * q + r + 1)
                    nc.tensor.matmul(table_ps[:, :], in_slot[r][:, :], in_tile[r][:, :], start=False, stop=False,
                                     skip_group_check=True).then_inc(placed, 1)

            def up(g, s):
                for f in range(KF):
                    if beyond(g, 0) or f > 1:
                        pe.wait_ge(h_ready, KF * g + f - 1)
                    for k in range(KD):
                        mm = nc.tensor.matmul(h_ps[f % 2][:, :], w1[:, k, f * P:(f + 1) * P],
                                              xT[:, k, bass.ds(g * GRP, GRP)], start=(k == 0), stop=(k == KD - 1))
                    mm.then_inc(h_done, 1)

            def down(g, s):
                pe.wait_ge(h_ready, KF * (g + 1))
                for j in range(GT):
                    if beyond(g, 0) or j > 1:
                        pe.wait_ge(y_copied, GT * g + j - 1)
                    for f in range(KF):
                        mm = nc.tensor.matmul(y_ps[j % 2][:, :], h[s][:, f, j * P:(j + 1) * P], w2[:, f, :],
                                              start=(f == 0), stop=(f == KF - 1))
                    mm.then_inc(y_done, 1)

            def step(g, s):
                up(g, s)
                down(g - 1, 1 - s)

            pe.wait_ge(logits_in, NGRP)
            if shared:
                pe.wait_ge(w_in, 32)
                up(0, 0)
                step(1, 1)
                step(2, 0)
                counts_of_labels()
                step(3, 1)
                with pe.Fori(2, NGRP // 2) as i:
                    for s in range(2):
                        step(2 * i + s, s)
                        burst(2 * i + s - (NGRP - BURSTS))
                down(NGRP - 1, 1)
            else:
                counts_of_labels()
                with pe.Fori(0, BURSTS) as q:
                    burst(q)
            nc.tensor.matmul(table_ps[:, :], nothing[:, :], nothing[:, 0:NT], start=False, stop=True,
                             skip_group_check=True).then_inc(placed, 1)

        @block.scalar
        def _(act):
            act.wait_ge(wg_in, NW)
            with act.Fori(0, NGRP // 2) as i:
                for s in range(2):
                    act.wait_ge(row_done, 2 * i + s + 1)
                    act.wait_ge(turned, 2 * i)
                    if bg is None:
                        nc.scalar.copy(logit_row[s][:, :], row_ps[s]).then_inc(row_copied, 1)
                    else:
                        nc.scalar.activation(logit_row[s][:, :], row_ps[s], ACT.Identity,
                                             bias=bias[:, 0:1]).then_inc(row_copied, 1)

            def exponentials():
                act.wait_ge(exp_in, 1)
                if capacity is None:
                    nc.scalar.activation(expo[:, :, :], low[:, :, :], ACT.Exp).then_inc(exp_done, 1)
                else:
                    nc.scalar.activation(total[:, :], pick[:, :], ACT.Exp).then_inc(exp_done, 1)

            def hide(g, s):
                if beyond(g, 1):
                    act.wait_ge(y_done, GT * (g - 1))
                for f in range(KF):
                    act.wait_ge(h_done, KF * g + f + 1)
                    nc.scalar.activation(h[s][:, f, :], h_ps[f % 2][:, :], ACT.Gelu).then_inc(h_ready, 1)

            def take(g, s):
                if beyond(g, 1):
                    act.wait_ge(part_out[s], 16 * (g // 2))
                for j in range(GT):
                    act.wait_ge(y_done, GT * g + j + 1)
                    nc.scalar.copy(y[s][:, j, :], y_ps[j % 2][:, :]).then_inc(y_copied, 1)

            def step(g, s):
                hide(g, s)
                take(g - 1, 1 - s)

            exponentials()
            if shared:
                hide(0, 0)
                step(1, 1)
                with act.Fori(1, NGRP // 2) as i:
                    step(2 * i, 0)
                    step(2 * i + 1, 1)
                take(NGRP - 1, 1)

        @block.gpsimd
        def _(pool):
            nc.gpsimd.iota(counts_i[:, :], pattern=[[1, P]], base=0, channel_multiplier=0).then_inc(iotas, 1)
            nc.gpsimd.iota(tokens_i[:, :], pattern=[[P, TT]], base=0, channel_multiplier=1).then_inc(iotas, 1)

            def add(g, s):
                pool.wait_ge(x_in[s], 16 * (g // 2 + 1))
                for j in range(GT):
                    pool.wait_ge(y_copied, GT * g + j + 1)
                    nc.gpsimd.tensor_tensor(y[s][:, j, :], y[s][:, j, :], x[s][:, j, :], ALU.add).then_inc(summed, 1)

            if shared:
                skewed(pool, 0, 0, add)

        @block.vector
        def _(dve):
            count = [0]

            def settle(ins):
                ins.then_inc(step, 1)
                count[0] += 1
                dve.wait_ge(step, count[0])

            def over_experts(a):
                return a[:, :, :].rearrange("p e t -> p t e")

            def to_experts(a):
                return a.rearrange("p (a t) -> p a t", a=1).broadcast_to(S)

            def to_tiles(a):
                return a.rearrange("p (e a) -> p e a", a=1).broadcast_to(S)

            dve.wait_ge(iotas, 2)
            nc.vector.memset(nothing[:, :].bitcast(U32), 0)
            for e in range(E):
                nc.vector.memset(number[:, e, :], float(e - E))
            nc.vector.memset(ones_e[:, :], 1.0)
            nc.vector.memset(ones[:, :], 1.0)
            nc.vector.memset(carry[:, :, 1:TT], 1.0)
            nc.vector.memset(carry[:, :, 0:1], 0.0)
            nc.vector.tensor_copy(tokens[:, :], tokens_i[:, :])
            settle(nc.vector.tensor_copy(counts[:, :], counts_i[:, :]))
            with dve.Fori(0, NGRP // 2) as i:
                for s in range(2):
                    g = 2 * i + s
                    dve.wait_ge(turned, g + 1)
                    nc.vector.tensor_copy(value[:, :, bass.ds(g * GT, GT)].rearrange("p e j -> p j e"),
                                          col_ps[s][:, :, :]).then_inc(logits_in, 1)
            dve.wait_ge(logits_in, NGRP)
            if capacity is None:
                settle(nc.vector.tensor_reduce(top[0][:, :], over_experts(value), AX.X, ALU.max))
                nc.vector.tensor_tensor(low[:, :, :], value[:, :, :], to_experts(top[0][:, :]), ALU.subtract).then_inc(exp_in, 1)
                dve.wait_ge(exp_done, 1)
                settle(nc.vector.tensor_reduce(total[:, :], over_experts(expo), AX.X, ALU.add))
                settle(nc.vector.reciprocal(inv[:, :], total[:, :]))
                settle(nc.vector.tensor_tensor(value[:, :, :], expo[:, :, :], to_experts(inv[:, :]), ALU.mult))
            for a in range(2):
                src = value if a == 0 else low
                settle(nc.vector.tensor_reduce(top[a][:, :], over_experts(src), AX.X, ALU.max))
                settle(nc.vector.tensor_tensor(hit[:, :, :], src[:, :, :], to_experts(top[a][:, :]), ALU.is_equal))
                settle(nc.vector.scalar_tensor_tensor(cand[:, :, :], hit[:, :, :], float(-E), number[:, :, :], ALU.mult, ALU.add))
                settle(nc.vector.tensor_reduce(pick[:, :], over_experts(cand), AX.X, ALU.min))
                settle(nc.vector.tensor_scalar(pick[:, :], pick[:, :], float(E), None, ALU.add))
                settle(nc.vector.tensor_tensor(one[a][:, :, :], number[:, :, :], to_experts(pick[:, :]), ALU.is_equal))
                if a == 0:
                    settle(nc.vector.scalar_tensor_tensor(low[:, :, :], one[0][:, :, :], -BIG, value[:, :, :], ALU.mult, ALU.add))
            if capacity is None:
                settle(nc.vector.tensor_tensor(total[:, :], top[0][:, :], top[1][:, :], ALU.add))
                settle(nc.vector.reciprocal(inv[:, :], total[:, :]))
                for a in range(2):
                    nc.vector.tensor_tensor(weight[:, a, :], top[a][:, :], inv[:, :], ALU.mult)
            else:
                nc.vector.tensor_tensor(pick[:, :], top[1][:, :], top[0][:, :], ALU.subtract).then_inc(exp_in, 1)
                dve.wait_ge(exp_done, 1)
                settle(nc.vector.tensor_scalar(inv[:, :], total[:, :], 1.0, None, ALU.add))
                settle(nc.vector.reciprocal(weight[:, 0, :], inv[:, :]))
                settle(nc.vector.tensor_tensor(weight[:, 1, :], total[:, :], weight[:, 0, :], ALU.mult))
            nc.vector.tensor_tensor(labels[:, :, :], one[0][:, :, :], one[1][:, :, :], ALU.add).then_inc(labels_in, 1)
            dve.wait_ge(counted, 1)
            settle(nc.vector.tensor_copy(tile_sum[:, :, :], sum_ps))
            settle(nc.vector.tensor_tensor_scan(upto_tile[:, :, :].rearrange("p e t -> p (e t)"),
                                                carry[:, :, :].rearrange("p e t -> p (e t)"),
                                                tile_sum[:, :, :].rearrange("p e t -> p (e t)"), 0.0, ALU.mult, ALU.add))
            settle(nc.vector.tensor_tensor(place[:, :, :], upto_tile[:, :, :], tile_sum[:, :, :], ALU.subtract))
            settle(nc.vector.tensor_tensor(place[:, :, :], cum_ps, place[:, :, :], ALU.add))
            if capacity is None:
                settle(nc.vector.tensor_scalar(hit[:, 0, :], counts[:, 0:TT], float(P), None, ALU.mult))
                settle(nc.vector.tensor_tensor(cand[:, :, :], upto_tile[:, :, TT - 1:TT].broadcast_to(S),
                                               hit[:, 0:1, :].broadcast_to(S), ALU.is_gt))
                settle(nc.vector.tensor_reduce(tiles[:, :], cand[:, :, :], AX.X, ALU.add))
                settle(nc.vector.tensor_tensor_scan(end[:, :], ones_e[:, :], tiles[:, :], 0.0, ALU.mult, ALU.add))
                settle(nc.vector.tensor_tensor(base[:, :], end[:, :], tiles[:, :], ALU.subtract))
                settle(nc.vector.tensor_scalar(base[:, :], base[:, :], float(P), -1.0, ALU.mult, ALU.add))
                settle(nc.vector.tensor_tensor(place[:, :, :], place[:, :, :], to_tiles(base[:, :]), ALU.add))
                settle(nc.vector.tensor_tensor(at_tile[:, :, :],
                                               end[:, :].rearrange("p (a e) -> p a e", a=1).broadcast_to([P, NT, E]),
                                               counts[:, 0:NT].rearrange("p (t a) -> p t a", a=1).broadcast_to([P, NT, E]),
                                               ALU.is_le))
                settle(nc.vector.tensor_reduce(tile_no[:, :], at_tile[:, :, :], AX.X, ALU.add))
                settle(nc.vector.tensor_scalar(tile_expert[:, :], tile_no[:, :], float(E - 1), None, ALU.min))
            else:
                settle(nc.vector.tensor_scalar(hit[:, :, :], place[:, :, :], float(capacity), None, ALU.is_le))
                settle(nc.vector.tensor_scalar(cand[:, :, :], number[:, :, :], float(capacity), -1.0, ALU.mult, ALU.add))
                settle(nc.vector.tensor_tensor(place[:, :, :], place[:, :, :], cand[:, :, :], ALU.add))
                settle(nc.vector.tensor_tensor(place[:, :, :], place[:, :, :], hit[:, :, :], ALU.mult))
                settle(nc.vector.tensor_scalar(place[:, :, :], place[:, :, :], float(E * capacity), None, ALU.add))
            for a in range(2):
                settle(nc.vector.tensor_tensor(hit[:, :, :], one[a][:, :, :], place[:, :, :], ALU.mult))
                settle(nc.vector.tensor_reduce(where[:, a, :], over_experts(hit), AX.X, ALU.add))
            settle(nc.vector.tensor_copy(pos[:, :, :], where[:, :, :]))
            settle(nc.vector.tensor_scalar(bits[:, :, :], pos[:, :, :], P - 1, None, ALU.bitwise_and))
            settle(nc.vector.tensor_copy(slot[:, :, :], bits[:, :, :]))
            settle(nc.vector.tensor_scalar(bits[:, :, :], pos[:, :, :], 7, None, ALU.arith_shift_right))
            settle(nc.vector.tensor_copy(tile_of[:, :, :], bits[:, :, :]))
            with dve.Fori(0, BURSTS) as q:
                for r in range(RING):
                    t = (RING // 2) * q + r // 2
                    if r == 0:
                        dve.wait_ge(placed, RING * q)
                    nc.vector.tensor_scalar(in_slot[r][:, :], counts[:, :], slot[:, r % 2, bass.ds(t, 1)], None, ALU.is_equal)
                    nc.vector.tensor_scalar(in_tile[r][:, :], counts[:, 0:NT], tile_of[:, r % 2, bass.ds(t, 1)],
                                            tokens[:, bass.ds(t, 1)], ALU.is_equal, ALU.mult).then_inc(made, 1)
            dve.wait_ge(placed, 2 * TT + 1)
            settle(nc.vector.tensor_copy(table[:, :], table_ps[:, :]))


def experts_gelu(nc, x_d, Wu, Wd, ident, table, tile_expert, y_d):
    NT = table.shape[1]
    F = Wu.shape[2]
    KF = F // P
    XS = 4
    with ExitStack() as ctx:
        m = Mem(nc, ctx, "gelu")
        wu, wd = m.sb("wu", [P, KD, E, F]), m.sb("wd", [P, KF, E, D])
        row_no = [m.sb(f"row_no{i}", [P, 1], I32) for i in range(XS)]
        x = [m.sb(f"x{i}", [P, D]) for i in range(XS)]
        xT = [m.sb(f"xT{i}", [P, D]) for i in range(2)]
        h = [m.sb(f"h{i}", [P, F]) for i in range(2)]
        hT = [m.sb(f"hT{i}", [P, F]) for i in range(2)]
        y = [m.sb(f"y{i}", [P, D]) for i in range(2)]
        x_ps = m.ps("x_ps", [P, D])
        h_ps, t_ps, y_ps = ([m.ps(f"{a}_ps{i}", [P, n]) for i in range(2)] for a, n in (("h", F), ("t", F), ("y", D)))
        w_in, x_turned, xT_ready, h_done, h_ready, h_turned, hT_ready, y_done, y_ready, numbered = (m.sem(a) for a in (
            "w_in", "x_turned", "xT_ready", "h_done", "h_ready", "h_turned", "hT_ready", "y_done", "y_ready", "numbered"))
        x_in = [m.sem(f"x_in{i}") for i in range(XS)]
        y_out = [m.sem(f"y_out{i}") for i in range(2)]
        passed = m.sem("passed")
        block = ctx.enter_context(nc.Block())

        @block.sync
        def _(sp):
            for k in range(KD):
                sp.dma_start(wu[:, k, :, :], Wu[:, k * P:(k + 1) * P, :].rearrange("e p f -> p e f")).then_inc(w_in, 16)
            for k in range(KF):
                sp.dma_start(wd[:, k, :, :], Wd[:, k * P:(k + 1) * P, :].rearrange("e p f -> p e f")).then_inc(w_in, 16)
            with sp.Fori(0, NT // 2) as i:
                for s in range(2):
                    n = 2 * i + s
                    sp.wait_ge(y_ready, n + 1)
                    sp.dma_start(y_d[bass.ds(n * P, P), :], y[s][:, :]).then_inc(y_out[s], 16)
            for s in range(2):
                sp.wait_ge(y_out[s], 16 * NT // 2)

        @block.gpsimd
        def _(pool):
            with pool.Fori(0, NT // XS) as i:
                for s in range(XS):
                    n = XS * i + s
                    pool.wait_ge(x_in[s], 16 * i)
                    nc.gpsimd.tensor_copy(row_no[s][:, :], table[:, bass.ds(n, 1)]).then_inc(numbered, 1)
                for s in range(XS):
                    n = XS * i + s
                    pool.wait_ge(numbered, n + 1)
                    pool.wait_ge(x_turned, XS * i)
                    pool.sem_inc(passed, 1)
                    nc.gpsimd.indirect_dma_start(out=x[s][:, :], out_offset=None, in_=x_d,
                                                 in_offset=bass.IndirectOffsetOnAxis(ap=row_no[s][:, 0:1], axis=0)
                                                 ).then_inc(x_in[s], 16)

        @block.tensor
        def _(pe):
            def turn_x(n, s):
                pe.wait_ge(x_in[s], 16 * (n // XS + 1))
                pe.wait_ge(xT_ready, n)
                for k in range(KD):
                    mm = nc.tensor.transpose(x_ps[:, k * P:(k + 1) * P], x[s][:, k * P:(k + 1) * P], ident[:, :])
                mm.then_inc(x_turned, 1)

            def up(n, s):
                e = pe.value_load(tile_expert[0:1, bass.ds(n, 1)], min_val=0, max_val=E - 1)
                pe.wait_ge(xT_ready, n + 1)
                if not isinstance(n, int) or n > 1:
                    pe.wait_ge(h_ready, n - 1)
                for k in range(KD):
                    mm = nc.tensor.matmul(h_ps[s][:, :], xT[s][:, k * P:(k + 1) * P],
                                          wu[:, k, bass.ds(e, 1), :].rearrange("p e f -> p (e f)"),
                                          start=(k == 0), stop=(k == KD - 1))
                mm.then_inc(h_done, 1)

            def turn_h(n, s):
                pe.wait_ge(h_ready, n + 1)
                for k in range(KF):
                    mm = nc.tensor.transpose(t_ps[s][:, k * P:(k + 1) * P], h[s][:, k * P:(k + 1) * P], ident[:, :])
                mm.then_inc(h_turned, 1)

            def down(n, s):
                e = pe.value_load(tile_expert[0:1, bass.ds(n, 1)], min_val=0, max_val=E - 1)
                pe.wait_ge(hT_ready, n + 1)
                if not isinstance(n, int) or n > 1:
                    pe.wait_ge(y_ready, n - 1)
                for k in range(KF):
                    mm = nc.tensor.matmul(y_ps[s][:, :], hT[s][:, k * P:(k + 1) * P],
                                          wd[:, k, bass.ds(e, 1), :].rearrange("p e f -> p (e f)"),
                                          start=(k == 0), stop=(k == KF - 1))
                mm.then_inc(y_done, 1)

            def one(n, s):
                turn_h(n, s % 2)
                if not (isinstance(n, int) and n + 1 >= NT):
                    up(n + 1, (s + 1) % 2)
                down(n, s % 2)
                if not (isinstance(n, int) and n + 2 >= NT):
                    turn_x(n + 2, (s + 2) % XS)

            pe.wait_ge(w_in, 16 * (KD + KF))
            turn_x(0, 0)
            turn_x(1, 1)
            up(0, 0)
            one(0, 0)
            one(1, 1)
            one(2, 2)
            one(3, 3)
            with pe.Fori(1, NT // XS - 1) as i:
                for s in range(XS):
                    one(XS * i + s, s)
            for s in range(XS):
                one(NT - XS + s, s)

        @block.scalar
        def _(act):
            with act.Fori(0, NT // 2) as i:
                for s in range(2):
                    n = 2 * i + s
                    act.wait_ge(h_done, n + 1)
                    act.wait_ge(h_turned, 2 * i)
                    nc.scalar.activation(h[s][:, :], h_ps[s][:, :], ACT.Gelu).then_inc(h_ready, 1)
                    act.wait_ge(h_turned, n + 1)
                    act.wait_ge(y_done, 2 * i)
                    nc.scalar.copy(hT[s][:, :], t_ps[s][:, :]).then_inc(hT_ready, 1)

        @block.vector
        def _(dve):
            def take_x(n, s):
                dve.wait_ge(x_turned, n + 1)
                if not isinstance(n, int) or n > 1:
                    dve.wait_ge(h_done, n - 1)
                nc.vector.tensor_copy(xT[s][:, :], x_ps[:, :]).then_inc(xT_ready, 1)

            def take_y(n, s):
                dve.wait_ge(y_done, n + 1)
                dve.wait_ge(y_out[s], 16 * (n // 2))
                nc.vector.tensor_copy(y[s][:, :], y_ps[s][:, :]).then_inc(y_ready, 1)

            take_x(0, 0)
            take_x(1, 1)
            with dve.Fori(0, NT // 2 - 1) as i:
                for s in range(2):
                    take_y(2 * i + s, s)
                    take_x(2 * i + s + 2, s)
            for s in range(2):
                take_y(NT - 2 + s, s)


def experts_silu(nc, x_d, W1, W2, W3, ident, table, capacity, y_d):
    NT = table.shape[1]
    F = W1.shape[2]
    KF = F // P
    CT = capacity // P
    HALF = capacity // 2
    with ExitStack() as ctx:
        m = Mem(nc, ctx, "silu")
        w12 = [m.sb(f"w12{i}", [P, 2, KD, F]) for i in range(2)]
        w3 = [m.sb(f"w3{i}", [P, KF, D]) for i in range(2)]
        row_no = m.sb("row_no", [P, CT], I32)
        x = [m.sb(f"x{i}", [P, CT, D]) for i in range(2)]
        xT = [m.sb(f"xT{i}", [P, KD, capacity]) for i in range(2)]
        gate = [m.sb(f"gate{i}", [P, HALF]) for i in range(2)]
        h = m.sb("h", [P, KF, capacity])
        y = [m.sb(f"y{i}", [P, D]) for i in range(2)]
        zero = m.sb("zero", [1, D])
        x_ps = [m.ps(f"x_ps{i}", [P, KD, P]) for i in range(2)]
        h_ps = [[m.ps(f"h_ps{i}{a}", [P, HALF]) for a in range(2)] for i in range(2)]
        y_ps = [m.ps(f"y_ps{i}", [P, D]) for i in range(2)]
        x_turned, xT_ready, h_done, gated, h_ready, y_done, y_ready, numbered, zeroed = (m.sem(a) for a in (
            "x_turned", "xT_ready", "h_done", "gated", "h_ready", "y_done", "y_ready", "numbered", "zeroed"))
        w_in = [m.sem(f"w_in{i}") for i in range(2)]
        x_in = [m.sem(f"x_in{i}") for i in range(2)]
        y_out, zero_out = [m.sem(f"y_out{i}") for i in range(2)], m.sem("zero_out")
        UNITS = 2 * KF
        passed = m.sem("passed")
        block = ctx.enter_context(nc.Block())

        @block.sync
        def _(sp):
            def load(e, s):
                ex = bass.ds(e, 1)
                for a, W in enumerate((W1, W2)):
                    sp.dma_start(w12[s][:, a, :, :], W[ex].rearrange("e (k p) f -> p (e k) f", p=P)).then_inc(w_in[s], 16)
                sp.dma_start(w3[s][:, :, :], W3[ex].rearrange("e (k p) f -> p (e k) f", p=P)).then_inc(w_in[s], 16)

            def store(e, s):
                for j in range(CT):
                    sp.wait_ge(y_ready, CT * e + j + 1)
                    b = (s + j) % 2
                    sp.dma_start(y_d[bass.ds((CT * e + j) * P, P), :], y[b][:, :]).then_inc(y_out[b], 16)

            load(0, 0)
            load(1, 1)
            with sp.Fori(0, E // 2 - 1) as i:
                for s in range(2):
                    store(2 * i + s, s)
                    load(2 * i + s + 2, s)
            for s in range(2):
                store(E - 2 + s, s)
            for b in range(2):
                sp.wait_ge(y_out[b], 16 * NT // 2)

        @block.gpsimd
        def _(pool):
            nc.gpsimd.memset(zero[:, :], 0.0).then_inc(zeroed, 1)
            pool.wait_ge(zeroed, 1)
            pool.dma_start(y_d[NT * P:NT * P + 1, :], zero[:, :]).then_inc(zero_out, 16)
            with pool.Fori(0, E // 2) as i:
                for s in range(2):
                    e = 2 * i + s
                    pool.wait_ge(x_in[1 - s], 16 * CT * (i + s))
                    nc.gpsimd.tensor_copy(row_no[:, :], table[:, bass.ds(e * CT, CT)]).then_inc(numbered, 1)
                    pool.wait_ge(numbered, e + 1)
                    pool.wait_ge(x_turned, CT * 2 * i)
                    pool.sem_inc(passed, 1)
                    for j in range(CT):
                        nc.gpsimd.indirect_dma_start(out=x[s][:, j, :], out_offset=None, in_=x_d,
                                                     in_offset=bass.IndirectOffsetOnAxis(ap=row_no[:, j:j + 1], axis=0)
                                                     ).then_inc(x_in[s], 16)
            pool.wait_ge(zero_out, 16)

        @block.tensor
        def _(pe):
            def turn(e, s):
                pe.wait_ge(x_in[s], 16 * CT * (e // 2 + 1))
                for j in range(CT):
                    if not isinstance(e, int) or CT * e + j > 1:
                        pe.wait_ge(xT_ready, CT * e + j - 1)
                    for k in range(KD):
                        mm = nc.tensor.transpose(x_ps[(s + j) % 2][:, k, :], x[s][:, j, k * P:(k + 1) * P], ident[:, :])
                    mm.then_inc(x_turned, 1)

            def work(e, s, more):
                pe.wait_ge(w_in[s], 48 * (e // 2 + 1))
                pe.wait_ge(xT_ready, CT * (e + 1))
                for u in range(UNITS):
                    f, half = u // 2, u % 2
                    if not isinstance(e, int) or UNITS * e + u > 1:
                        pe.wait_ge(h_ready, UNITS * e + u - 1)
                    for a in range(2):
                        for k in range(KD):
                            mm = nc.tensor.matmul(h_ps[u % 2][a][:, :], w12[s][:, a, k, f * P:(f + 1) * P],
                                                  xT[s][:, k, half * HALF:(half + 1) * HALF],
                                                  start=(k == 0), stop=(k == KD - 1))
                    mm.then_inc(h_done, 1)
                if more:
                    turn(e + 1, 1 - s)
                pe.wait_ge(h_ready, UNITS * (e + 1))
                for j in range(CT):
                    if not isinstance(e, int) or CT * e + j > 1:
                        pe.wait_ge(y_ready, CT * e + j - 1)
                    for f in range(KF):
                        mm = nc.tensor.matmul(y_ps[(s + j) % 2][:, :], h[:, f, j * P:(j + 1) * P], w3[s][:, f, :],
                                              start=(f == 0), stop=(f == KF - 1))
                    mm.then_inc(y_done, 1)

            turn(0, 0)
            work(0, 0, True)
            with pe.Fori(0, E // 2 - 1) as i:
                work(2 * i + 1, 1, True)
                work(2 * i + 2, 0, True)
            work(E - 1, 1, False)

        @block.scalar
        def _(act):
            def one(e):
                for u in range(UNITS):
                    act.wait_ge(h_done, UNITS * e + u + 1)
                    if not isinstance(e, int) or UNITS * e + u > 1:
                        act.wait_ge(h_ready, UNITS * e + u - 1)
                    nc.scalar.activation(gate[u % 2][:, :], h_ps[u % 2][0][:, :], ACT.Silu).then_inc(gated, 1)

            one(0)
            with act.Fori(1, E) as e:
                one(e)

        @block.vector
        def _(dve):
            def take_x(e, s):
                if not isinstance(e, int) or e > 1:
                    dve.wait_ge(h_done, UNITS * (e - 1))
                for j in range(CT):
                    dve.wait_ge(x_turned, CT * e + j + 1)
                    nc.vector.tensor_copy(xT[s][:, :, j * P:(j + 1) * P], x_ps[(s + j) % 2][:, :, :]).then_inc(xT_ready, 1)

            def work(e, s, more):
                dve.wait_ge(y_done, CT * e)
                for u in range(UNITS):
                    dve.wait_ge(gated, UNITS * e + u + 1)
                    nc.vector.tensor_tensor(h[:, u // 2, (u % 2) * HALF:(u % 2 + 1) * HALF], gate[u % 2][:, :],
                                            h_ps[u % 2][1][:, :], ALU.mult).then_inc(h_ready, 1)
                if more:
                    take_x(e + 1, 1 - s)
                for j in range(CT):
                    b = (s + j) % 2
                    dve.wait_ge(y_done, CT * e + j + 1)
                    if not isinstance(e, int) or CT * e + j > 1:
                        dve.wait_ge(y_out[b], 16 * ((CT * e + j) // 2))
                    nc.vector.tensor_copy(y[b][:, :], y_ps[b][:, :]).then_inc(y_ready, 1)

            take_x(0, 0)
            work(0, 0, True)
            with dve.Fori(0, E // 2 - 1) as i:
                work(2 * i + 1, 1, True)
                work(2 * i + 2, 0, True)
            work(E - 1, 1, False)


def mix_tokens(nc, part_d, y_d, pos, weight, ident, WkT, WvT, WrT, WoT, decay, first_share, scale, x, x2, nT2):
    with ExitStack() as ctx:
        m = Mem(nc, ctx, "mix")
        w = m.sb("w", [P, 3, KD, D])
        wo = m.sb("wo", [P, KD, D])
        scale_row = m.sb("scale_row", [P, D])
        td, tf, e1, ew, eu = (m.sb(a, [P, KD]) for a in ("td", "tf", "e1", "ew", "eu"))
        base = [m.sb(f"base{i}", [P, GT, D]) for i in range(2)]
        y = [m.sb(f"y{i}", [P, GT, 2, D]) for i in range(2)]
        row_no = [m.sb(f"row_no{i}", [P, 2, GT], I32) for i in range(2)]
        part = [m.sb(f"part{i}", [P, GT, 6]) for i in range(2)]
        mean_var = [m.sb(f"mean_var{i}", [P, GT, 2]) for i in range(2)]
        std, inv, q1, q, root1, inv1, both_inv, total, root2, inv2 = (
            [m.sb(f"{a}{i}", [P, GT]) for i in range(2)]
            for a in ("std", "inv", "q1", "q", "root1", "inv1", "both_inv", "total", "root2", "inv2"))
        square = [m.sb(f"square{i}", [P, D]) for i in range(2)]
        n1 = [m.sb(f"n1{i}", [P, GT, D]) for i in range(2)]
        n2 = [m.sb(f"n2{i}", [P, GT, D]) for i in range(2)]
        nT = [m.sb(f"nT{i}", [P, KD, GRP]) for i in range(2)]
        eps = m.sb("eps", [P, 2])
        k_sb, r_sb, kv, wkv = ([m.sb(f"{a}{c}", [P, GRP]) for c in range(KD)] for a in ("k_sb", "r_sb", "kv", "wkv"))
        state = [m.sb(f"state{c}", [P, GRP + 1]) for c in range(KD)]
        last = [m.sb(f"last{c}", [P, 1]) for c in range(KD)]
        z = [m.sb(f"z{i}", [P, KD, GRP]) for i in range(2)]
        k_ps, r_ps = m.ps("k_ps", [P, GRP]), m.ps("r_ps", [P, GRP])
        v_ps = [m.ps(f"v_ps{c}", [P, GRP]) for c in range(KD)]
        o_ps = [m.ps(f"o_ps{i}", [P, D]) for i in range(2)]
        turn1_ps, turn2_ps = m.ps("turn1_ps", [P, GRP]), m.ps("turn2_ps", [P, GRP])
        w_in, wo_ready, e1_done, shares_done, k_done, v_done, r_done, k_copied, r_ready = (m.sem(a) for a in (
            "w_in", "wo_ready", "e1_done", "shares_done", "k_done", "v_done", "r_done", "k_copied", "r_ready"))
        carried, kept, kv_done, scanned, wkv_done, z_done, o_done, added = (m.sem(a) for a in (
            "carried", "kept", "kv_done", "scanned", "wkv_done", "z_done", "o_done", "added"))
        first, summed, numbered, passed, eps_set, parted, aggregated, std_done, inv_done, q1_done, q_done = (m.sem(a) for a in (
            "first", "summed", "numbered", "passed", "eps_set", "parted", "aggregated", "std_done", "inv_done", "q1_done", "q_done"))
        normed, root1_done, inv1_done, both_done, n1_done, turned1, copied1 = (m.sem(a) for a in (
            "normed", "root1_done", "inv1_done", "both_done", "n1_done", "turned1", "copied1"))
        squared, root2_done, inv2_done, n2_done, turned2, copied2 = (m.sem(a) for a in (
            "squared", "root2_done", "inv2_done", "n2_done", "turned2", "copied2"))
        base_in, y_in = ([m.sem(f"{a}{i}") for i in range(2)] for a in ("base_in", "y_in"))
        NW = 16 * (5 + 2 * KD)
        block = ctx.enter_context(nc.Block())

        def tile(a, g, j):
            return a[:, bass.ds(g * GT + j, 1), :].rearrange("p a d -> p (a d)")

        @block.sync
        def _(sp):
            for i, a in enumerate((WkT, WvT, WrT)):
                sp.dma_start(w[:, i], a.rearrange("(k p) n -> p k n", p=P)).then_inc(w_in, 16)
            sp.dma_start(wo[:, :, :], WoT.rearrange("(k p) n -> p k n", p=P)).then_inc(w_in, 16)
            sp.dma_start(scale_row[:, :], row(scale).broadcast_to([P, D])).then_inc(w_in, 16)
            for k in range(KD):
                for a, b in ((td, decay), (tf, first_share)):
                    sp.dma_start(a[:, k:k + 1], b[k * P:(k + 1) * P].rearrange("(p a) -> p a", a=1)).then_inc(w_in, 16)

            def step(g, s):
                if beyond(g, 1):
                    sp.wait_ge(n1_done, GT * (g - 1))
                sp.dma_start(base[s][:, :, :], token_rows(part_d, g)).then_inc(base_in[s], 16)

            skewed(sp, 0, 0, step)

        @block.gpsimd
        def _(pool):
            def step(g, s):
                gather_pairs(nc, pool, g, s, pos, y_d, y, row_no, y_in, numbered, summed, passed)

            skewed(pool, 0, 0, step)

        @block.tensor
        def _(pe):
            def turn1(g, s):
                pe.wait_ge(n1_done, GT * (g + 1))
                for k in range(KD):
                    pe.wait_ge(copied1, KD * g + k)
                    for j in range(GT):
                        mm = nc.tensor.transpose(turn1_ps[:, j * P:(j + 1) * P], n1[s][:, j, k * P:(k + 1) * P], ident[:, :])
                    mm.then_inc(turned1, 1)

            def turn2(g, s):
                pe.wait_ge(n2_done, GT * (g + 1))
                for k in range(KD):
                    pe.wait_ge(copied2, KD * g + k)
                    for j in range(GT):
                        mm = nc.tensor.transpose(turn2_ps[:, j * P:(j + 1) * P], n2[s][:, j, k * P:(k + 1) * P], ident[:, :])
                    mm.then_inc(turned2, 1)

            def project(g, s):
                pe.wait_ge(copied1, KD * (g + 1))
                for c in range(KD):
                    for i, (bank, done, used) in enumerate(((k_ps, k_done, k_copied), (v_ps[c], v_done, kv_done), (r_ps, r_done, r_ready))):
                        if i != 1:
                            pe.wait_ge(used, KD * g + c)
                        elif beyond(g, 0):
                            pe.wait_ge(used, KD * (g - 1) + c + 1)
                        for k in range(KD):
                            mm = nc.tensor.matmul(bank[:, :], w[:, i, k, c * P:(c + 1) * P], nT[s][:, k, :],
                                                  start=(k == 0), stop=(k == KD - 1))
                        mm.then_inc(done, 1)

            def mix(g, s):
                pe.wait_ge(z_done, KD * (g + 1))
                for j in range(GT):
                    if beyond(g, 0) or j > 1:
                        pe.wait_ge(added, GT * g + j - 1)
                    for k in range(KD):
                        mm = nc.tensor.matmul(o_ps[j % 2][:, :], z[s][:, k, j * P:(j + 1) * P], wo[:, k, :],
                                              start=(k == 0), stop=(k == KD - 1))
                    mm.then_inc(o_done, 1)

            def step(g, s):
                if exists(g + 1):
                    project(g + 1, 1 - s)
                if exists(g - 1):
                    turn2(g - 1, 1 - s)
                if exists(g + 2):
                    turn1(g + 2, s)
                if exists(g):
                    mix(g, s)

            pe.wait_ge(w_in, NW)
            pe.wait_ge(wo_ready, 1)
            skewed(pe, -2, 1, step)

        @block.scalar
        def _(act):
            act.wait_ge(w_in, NW)
            nc.scalar.activation(e1[:, :], td[:, :], ACT.Exp).then_inc(e1_done, 1)
            nc.scalar.activation(eu[:, :], tf[:, :], ACT.Exp)
            act.wait_ge(e1_done, 1)
            nc.scalar.activation(ew[:, :], e1[:, :], ACT.Exp, scale=-1.0).then_inc(shares_done, 1)
            act.wait_ge(eps_set, 1)

            def deviation(g, s):
                act.wait_ge(aggregated, GT * (g + 1))
                nc.scalar.activation(std[s][:, :], mean_var[s][:, :, 1:2].rearrange("p g a -> p (g a)"), ACT.Sqrt,
                                     bias=eps[:, 0:1]).then_inc(std_done, 1)

            def size1(g, s):
                act.wait_ge(q_done, g + 1)
                nc.scalar.activation(root1[s][:, :], q[s][:, :], ACT.Sqrt, bias=eps[:, 1:2]).then_inc(root1_done, 1)

            def size2(g, s):
                for j in range(GT):
                    act.wait_ge(added, GT * g + j + 1)
                    if beyond(g, 0) or j > 1:
                        act.wait_ge(squared, GT * g + j - 1)
                    nc.scalar.activation(square[j % 2][:, :], tile(x2, g, j), ACT.Square,
                                         accum_out=total[s][:, j:j + 1]).then_inc(squared, 1)
                act.wait_ge(squared, GT * (g + 1))
                nc.scalar.activation(root2[s][:, :], total[s][:, :], ACT.Sqrt, bias=eps[:, 1:2],
                                     scale=1.0 / D).then_inc(root2_done, 1)

            def copy1(g, s):
                if beyond(g, 1):
                    act.wait_ge(r_done, KD * (g - 1))
                for k in range(KD):
                    act.wait_ge(turned1, KD * g + k + 1)
                    nc.scalar.copy(nT[s][:, k, :], turn1_ps[:, :]).then_inc(copied1, 1)

            def copy2(g, s):
                for k in range(KD):
                    act.wait_ge(turned2, KD * g + k + 1)
                    nc.scalar.copy(nT2[:, k, bass.ds(g * GRP, GRP)], turn2_ps[:, :]).then_inc(copied2, 1)

            def key_and_gate(g, s):
                for c in range(KD):
                    act.wait_ge(k_done, KD * g + c + 1)
                    if beyond(g, 0):
                        act.wait_ge(kv_done, KD * (g - 1) + c + 1)
                    nc.scalar.copy(k_sb[c][:, :], k_ps[:, :]).then_inc(k_copied, 1)
                    act.wait_ge(r_done, KD * g + c + 1)
                    if beyond(g, 0):
                        act.wait_ge(z_done, KD * (g - 1) + c + 1)
                    nc.scalar.activation(r_sb[c][:, :], r_ps[:, :], ACT.Sigmoid).then_inc(r_ready, 1)

            def step(g, s):
                if exists(g + 1):
                    key_and_gate(g + 1, 1 - s)
                if exists(g + 2):
                    deviation(g + 2, s)
                    size1(g + 2, s)
                if exists(g - 1):
                    copy2(g - 1, 1 - s)
                if exists(g + 2):
                    copy1(g + 2, s)
                if exists(g):
                    size2(g, s)

            skewed(act, -2, 1, step)

        @block.vector
        def _(dve):
            nc.vector.memset(eps[:, 0:1], LN_EPS)
            nc.vector.memset(eps[:, 1:2], RMS_EPS).then_inc(eps_set, 1)
            for c in range(KD):
                nc.vector.memset(last[c][:, :], 0.0).then_inc(kept, 1)
            dve.wait_ge(w_in, NW)
            nc.vector.tensor_tensor(wo[:, :, :], wo[:, :, :],
                                    scale_row[:, :].rearrange("p (a d) -> p a d", a=1).broadcast_to([P, KD, D]),
                                    ALU.mult).then_inc(wo_ready, 1)
            dve.wait_ge(shares_done, 1)

            def stats(g, s):
                dve.wait_ge(summed, GT * (g + 1))
                for j in range(GT):
                    nc.vector.bn_stats(part[s][:, j, :], base[s][:, j, :]).then_inc(parted, 1)
                dve.wait_ge(parted, GT * (g + 1))
                dve.sem_inc(passed, 1)
                for j in range(GT):
                    nc.vector.bn_aggr(mean_var[s][:, j, :], part[s][:, j, :]).then_inc(aggregated, 1)

            def norms(g, s):
                dve.wait_ge(std_done, g + 1)
                nc.vector.reciprocal(inv[s][:, :], std[s][:, :]).then_inc(inv_done, 1)
                dve.wait_ge(inv_done, g + 1)
                var = mean_var[s][:, :, 1:2].rearrange("p g a -> p (g a)")
                nc.vector.tensor_tensor(q1[s][:, :], var, inv[s][:, :], ALU.mult).then_inc(q1_done, 1)
                dve.wait_ge(q1_done, g + 1)
                nc.vector.tensor_tensor(q[s][:, :], q1[s][:, :], inv[s][:, :], ALU.mult).then_inc(q_done, 1)
                for j in range(GT):
                    nc.vector.tensor_scalar(tile(x, g, j), base[s][:, j, :], mean_var[s][:, j, 0:1],
                                            inv[s][:, j:j + 1], ALU.subtract, ALU.mult).then_inc(normed, 1)
                dve.wait_ge(root1_done, g + 1)
                nc.vector.reciprocal(inv1[s][:, :], root1[s][:, :]).then_inc(inv1_done, 1)
                dve.wait_ge(inv1_done, g + 1)
                nc.vector.tensor_tensor(both_inv[s][:, :], inv1[s][:, :], inv[s][:, :], ALU.mult).then_inc(both_done, 1)
                dve.wait_ge(both_done, g + 1)
                if beyond(g, 1):
                    dve.wait_ge(turned1, KD * (g - 1))
                for j in range(GT):
                    nc.vector.tensor_scalar(n1[s][:, j, :], base[s][:, j, :], mean_var[s][:, j, 0:1],
                                            both_inv[s][:, j:j + 1], ALU.subtract, ALU.mult).then_inc(n1_done, 1)

            def scan(g, s):
                for c in range(KD):
                    n = KD * g + c + 1
                    dve.wait_ge(k_copied, n)
                    dve.wait_ge(v_done, n)
                    nc.vector.tensor_tensor(kv[c][:, :], k_sb[c][:, :], v_ps[c][:, :], ALU.mult).then_inc(kv_done, 1)
                    dve.wait_ge(kept, n)
                    nc.vector.tensor_copy(state[c][:, 0:1], last[c][:, :]).then_inc(carried, 1)
                    dve.wait_ge(kv_done, n)
                    dve.wait_ge(carried, n)
                    nc.vector.tensor_tensor_scan(state[c][:, 1:GRP + 1], ew[:, c:c + 1].broadcast_to([P, GRP]), kv[c][:, :],
                                                 state[c][:, 0:1], ALU.mult, ALU.add).then_inc(scanned, 1)
                for c in range(KD):
                    n = KD * g + c + 1
                    dve.wait_ge(scanned, n)
                    nc.vector.scalar_tensor_tensor(wkv[c][:, :], kv[c][:, :], eu[:, c:c + 1], state[c][:, 0:GRP],
                                                   ALU.mult, ALU.add).then_inc(wkv_done, 1)
                    nc.vector.tensor_copy(last[c][:, :], state[c][:, GRP:GRP + 1]).then_inc(kept, 1)
                if beyond(g, 1):
                    dve.wait_ge(o_done, GT * (g - 1))
                for c in range(KD):
                    n = KD * g + c + 1
                    dve.wait_ge(r_ready, n)
                    dve.wait_ge(wkv_done, n)
                    nc.vector.tensor_tensor(z[s][:, c, :], wkv[c][:, :], r_sb[c][:, :], ALU.mult).then_inc(z_done, 1)

            def add(g, s):
                dve.wait_ge(normed, GT * (g + 1))
                for j in range(GT):
                    dve.wait_ge(o_done, GT * g + j + 1)
                    nc.vector.tensor_tensor(tile(x2, g, j), o_ps[j % 2][:, :], tile(x, g, j), ALU.add).then_inc(added, 1)

            def scale2(g, s):
                dve.wait_ge(root2_done, g + 1)
                nc.vector.reciprocal(inv2[s][:, :], root2[s][:, :]).then_inc(inv2_done, 1)
                dve.wait_ge(inv2_done, g + 1)
                if beyond(g, 1):
                    dve.wait_ge(turned2, KD * (g - 1))
                for j in range(GT):
                    nc.vector.tensor_scalar(n2[s][:, j, :], tile(x2, g, j), inv2[s][:, j:j + 1], None, ALU.mult).then_inc(n2_done, 1)

            def step(g, s):
                if exists(g + 2):
                    add_pairs(nc, dve, g + 2, s, weight, base, y, base_in, y_in, first, summed)
                    stats(g + 2, s)
                    norms(g + 2, s)
                if exists(g + 1):
                    scan(g + 1, 1 - s)
                if exists(g):
                    add(g, s)
                    scale2(g, s)

            skewed(dve, -2, 0, step)


def mix_channels(nc, nT, x, x2, WfcT, WmlpT, scale, ident, out_d):
    F = WfcT.shape[1]
    KF = F // P
    with ExitStack() as ctx:
        m = Mem(nc, ctx, "mlp")
        wf = m.sb("wf", [P, KD, F])
        wm = m.sb("wm", [P, KF, D])
        scale_row = m.sb("scale_row", [P, D])
        both = [m.sb(f"both{i}", [P, GT, D]) for i in range(2)]
        out = [m.sb(f"out{i}", [P, GT, D]) for i in range(2)]
        half = [m.sb(f"half{i}", [P, GRP]) for i in range(2)]
        leaky = [m.sb(f"leaky{i}", [P, GRP]) for i in range(2)]
        h = [m.sb(f"h{i}", [P, KF, GRP]) for i in range(2)]
        h_ps = [m.ps(f"h_ps{i}", [P, GRP]) for i in range(4)]
        y_ps = [m.ps(f"y_ps{i}", [P, D]) for i in range(2)]
        w_in, wm_ready, h_done, leaked, h_ready, y_done, paired, summed, halved = (m.sem(a) for a in (
            "w_in", "wm_ready", "h_done", "leaked", "h_ready", "y_done", "paired", "summed", "halved"))
        norm = Norm(nc, m, out, summed, out_d, ident, nT)
        block = ctx.enter_context(nc.Block())

        @block.sync
        def _(sp):
            sp.dma_start(wf[:, :, :], WfcT.rearrange("(k p) n -> p k n", p=P)).then_inc(w_in, 16)
            sp.dma_start(wm[:, :, :], WmlpT.rearrange("(k p) n -> p k n", p=P)).then_inc(w_in, 16)
            sp.dma_start(scale_row[:, :], row(scale).broadcast_to([P, D])).then_inc(w_in, 16)

            skewed(sp, 0, 0, lambda g, s: norm.store(sp, g, s))
            norm.finish(sp)

        @block.tensor
        def _(pe):
            def up(g, s):
                for f in range(KF):
                    if not isinstance(g, int) or KF * g + f > 3:
                        pe.wait_ge(leaked, KF * g + f - 3)
                    for k in range(KD):
                        mm = nc.tensor.matmul(h_ps[f % 4][:, :], wf[:, k, f * P:(f + 1) * P],
                                              nT[:, k, bass.ds(g * GRP, GRP)], start=(k == 0), stop=(k == KD - 1))
                    mm.then_inc(h_done, 1)

            def down(g, s):
                pe.wait_ge(h_ready, KF * (g + 1))
                for j in range(GT):
                    if not isinstance(g, int) or GT * g + j > 1:
                        pe.wait_ge(summed, GT * g + j - 1)
                    for f in range(KF):
                        mm = nc.tensor.matmul(y_ps[j % 2][:, :], h[s][:, f, j * P:(j + 1) * P], wm[:, f, :],
                                              start=(f == 0), stop=(f == KF - 1))
                    mm.then_inc(y_done, 1)

            pe.wait_ge(w_in, 48)
            pe.wait_ge(wm_ready, 1)

            def step(g, s):
                if exists(g + 1):
                    up(g + 1, 1 - s)
                if exists(g - 1):
                    norm.turn(pe, g - 1, 1 - s)
                if exists(g):
                    down(g, s)

            skewed(pe, -1, 1, step)

        @block.scalar
        def _(act):
            def one(g, s):
                if not isinstance(g, int) or g > 1:
                    act.wait_ge(y_done, GT * (g - 1))
                for f in range(KF + 1):
                    if f < KF:
                        act.wait_ge(h_done, KF * g + f + 1)
                        if f > 1:
                            act.wait_ge(leaked, KF * g + f - 1)
                        nc.scalar.activation(half[f % 2][:, :], h_ps[f % 4][:, :], ACT.Copy, scale=0.5).then_inc(halved, 1)
                    if f > 0:
                        act.wait_ge(leaked, KF * g + f)
                        nc.scalar.activation(h[s][:, f - 1, :], leaky[(f - 1) % 2][:, :], ACT.Square).then_inc(h_ready, 1)

            def step(g, s):
                if exists(g + 1):
                    one(g + 1, 1 - s)
                if exists(g - 1):
                    norm.copy(act, g - 1, 1 - s)
                if exists(g):
                    norm.root(act, g, s)

            skewed(act, -1, 1, step)

        @block.gpsimd
        def _(pool):
            def step(g, s):
                if beyond(g, 1):
                    pool.wait_ge(summed, GT * (g - 1))
                for j in range(GT):
                    a, b = (v[:, bass.ds(g * GT + j, 1), :].rearrange("p a d -> p (a d)") for v in (x, x2))
                    nc.gpsimd.tensor_tensor(both[s][:, j, :], a, b, ALU.add).then_inc(paired, 1)

            skewed(pool, 0, 0, step)

        @block.vector
        def _(dve):
            norm.begin()
            dve.wait_ge(w_in, 48)
            nc.vector.tensor_tensor(wm[:, :, :], wm[:, :, :],
                                    scale_row[:, :].rearrange("p (a d) -> p a d", a=1).broadcast_to([P, KF, D]),
                                    ALU.mult).then_inc(wm_ready, 1)

            def leak(g, s):
                for f in range(KF):
                    dve.wait_ge(halved, KF * g + f + 1)
                    if not isinstance(g, int) or KF * g + f > 1:
                        dve.wait_ge(h_ready, KF * g + f - 1)
                    nc.vector.tensor_tensor(leaky[f % 2][:, :], h_ps[f % 4][:, :], half[f % 2][:, :], ALU.max).then_inc(leaked, 1)

            def add(g, s):
                if beyond(g, 1):
                    dve.wait_ge(norm.normed, GT * (g - 1))
                for j in range(GT):
                    dve.wait_ge(y_done, GT * g + j + 1)
                    dve.wait_ge(paired, GT * g + j + 1)
                    nc.vector.tensor_tensor(out[s][:, j, :], y_ps[j % 2][:, :], both[s][:, j, :], ALU.add).then_inc(summed, 1)

            def step(g, s):
                if exists(g + 1):
                    leak(g + 1, 1 - s)
                if exists(g):
                    add(g, s)
                    norm.stats(dve, g, s)
                    norm.apply(dve, g, s)

            skewed(dve, -1, 0, step)




def network(nc, hidden, hidden_T, Wq, bq, Wk, bk, Wv, bv, gate0, up0, down0, shared1, shared2,
            mixk, mixv, mixr, mixo, decay, first_share, mix_scale, fc, mlp, mlp_scale,
            gate1, gate1_bias, w1, w2, w3, identity, upto_diagonal, out):
    TILES0 = (2 * T + E * (P - 1)) // P
    TILES0 += -TILES0 % 4
    CAPACITY = T * 5 // (4 * E)
    TILES1 = E * CAPACITY // P

    taken.clear()

    def scratch(name, *shape):
        return nc.dram_tensor(name, list(shape), F32).ap()

    rows = [scratch(f"rows{i}", T, D) for i in range(2)]
    part = scratch("part", T, D)
    expert_rows = [scratch("expert_rows0", TILES0 * P, D), scratch("expert_rows1", TILES1 * P + 1, D)]
    with ExitStack() as ctx:
        m = Mem(nc, ctx, "all")
        ident, upto = m.sb("ident", [P, P]), m.sb("upto", [P, P])
        loaded = m.sem("loaded")
        with nc.Block() as block:
            @block.sync
            def _(sp):
                sp.dma_start(ident[:, :], identity).then_inc(loaded, 16)
                sp.dma_start(upto[:, :], upto_diagonal).then_inc(loaded, 16)
                sp.wait_ge(loaded, 32)

        qk = scratch("qk", 2, 2, D, T)
        v = scratch("v", PAIRS, P, TT, 2 * VW)
        context, prob_sums = scratch("context", D, T), scratch("prob_sums", H, T)
        project_qkv(nc, hidden_T, Wq, bq, Wk, bk, Wv, bv, qk, v)
        attend(nc, qk, v, ident, context, prob_sums)

        xT = m.sb("xT", [P, KD, T])
        weight, pos = m.sb("weight", [P, 2, TT]), m.sb("pos", [P, 2, TT], I32)
        table0, table1 = m.sb("table0", [P, TILES0], I32), m.sb("table1", [P, TILES1], I32)
        tile_expert = m.sb("tile_expert", [P, TILES0], I32)
        merge_heads(nc, hidden, context, prob_sums, ident, rows[0], xT)
        route(nc, "route0", xT, gate0, None, ident, upto, None, weight, pos, table0, tile_expert,
              (shared1, shared2, rows[0], part))
        experts_gelu(nc, rows[0], up0, down0, ident, table0, tile_expert, expert_rows[0])
        nc.clear_and_free_semaphores(taken)
        nc.all_engine_barrier()
        taken.clear()

        with ExitStack() as layer:
            m1 = Mem(nc, layer, "layer1")
            x, x2 = m1.sb("x", [P, TT, D]), m1.sb("x2", [P, TT, D])
            mix_tokens(nc, part, expert_rows[0], pos, weight, ident, mixk, mixv, mixr, mixo, decay, first_share,
                       mix_scale, x, x2, xT)
            mix_channels(nc, xT, x, x2, fc, mlp, mlp_scale, ident, rows[1])
        route(nc, "route1", xT, gate1, gate1_bias, ident, upto, CAPACITY, weight, pos, table1, None)
        experts_silu(nc, rows[1], w1, w2, w3, ident, table1, CAPACITY, expert_rows[1])
        combine(nc, rows[1], expert_rows[1], pos, weight, out)


def kernel(**inputs):
    import numpy as np
    import concourse.bacc as bacc
    from concourse import mybir as _mybir
    from concourse.bass_utils import run_bass_kernel_spmd

    def plain(name):
        return np.ascontiguousarray(inputs[name])

    def turned(name):
        return np.ascontiguousarray(np.asarray(inputs[name]).T)

    hidden = np.ascontiguousarray(np.asarray(inputs["L0_attn_hidden_states"]).reshape(T, D))
    arrays = [hidden, np.ascontiguousarray(hidden.T),
              turned("L0_attn_Wq"), plain("L0_attn_bq"), turned("L0_attn_Wk"), plain("L0_attn_bk"),
              turned("L0_attn_Wv"), plain("L0_attn_bv"),
              plain("L0_ffn_Wg"), plain("L0_ffn_Wu"), plain("L0_ffn_Wd"), plain("L0_ffn_W1"), plain("L0_ffn_W2"),
              turned("L1_attn_Wk"), turned("L1_attn_Wv"), turned("L1_attn_Wr"), turned("L1_attn_Wo"),
              plain("L1_attn_time_decay"), plain("L1_attn_time_first"), plain("L1_attn_mixer_scale"),
              turned("L1_attn_Wfc"), turned("L1_attn_Wmlp"), plain("L1_attn_mlp_scale"),
              plain("L1_ffn_Wg"), plain("L1_ffn_bg"), plain("L1_ffn_W1"), plain("L1_ffn_W2"), plain("L1_ffn_W3"),
              np.eye(P, dtype=np.float32), np.triu(np.ones((P, P), np.float32))]
    nc = bacc.Bacc("TRN2", target_bir_lowering=False, num_devices=1)
    named = {f"in_{i}_dram": a for i, a in enumerate(arrays)}
    args = [nc.dram_tensor(name, a.shape, _mybir.dt.from_np(a.dtype), kind="ExternalInput").ap()
            for name, a in named.items()]
    out = nc.dram_tensor("out_0_dram", (T, D), _mybir.dt.float32, kind="ExternalOutput").ap()
    network(nc, *args, out)
    result = run_bass_kernel_spmd(nc, [named], core_ids=[0])
    return result.results[0]["out_0_dram"].reshape(1, T, D)
```

```python
from contextlib import ExitStack

import concourse.bass as bass
from concourse import mybir

F32 = mybir.dt.float32
F32R = mybir.dt.float32r
I32 = mybir.dt.int32
U32 = mybir.dt.uint32
ALU = mybir.AluOpType
ACT = mybir.ActivationFunctionType
AX = mybir.AxisListType

P = 128
T = 4096
D = 256
KD = D // P
TT = T // P
GRP = 512
NGRP = T // GRP
GT = GRP // P
H, HD = 16, 16
BLK = 64
NBLK = T // BLK
PAIRS = H // 2
VW = HD + 1
E = 8
TERMS = ((0, 0), (0, 1), (1, 0))
LN_EPS = 1e-5
RMS_EPS = 1e-6



taken = []


class Mem:

    def __init__(self, nc, ctx, tag):
        self.nc, self.ctx, self.tag = nc, ctx, tag

    def sb(self, name, shape, dt=F32):
        return self.ctx.enter_context(self.nc.sbuf_tensor(f"{self.tag}_{name}", shape, dt))

    def ps(self, name, shape, dt=F32):
        return self.ctx.enter_context(self.nc.psum_tensor(f"{self.tag}_{name}", shape, dt))

    def sem(self, name):
        sem = self.nc.alloc_semaphore(f"{self.tag}_{name}")
        taken.append(sem)
        return sem


def row(ap):
    return ap.rearrange("(a d) -> a d", a=1)


def token_rows(a, g):
    return a[bass.ds(g * GRP, GRP), :].rearrange("(j p) d -> p j d", p=P)


def project_qkv(nc, hsT, WqT, bq, WkT, bk, WvT, bv, qk_d, v_d):
    with ExitStack() as ctx:
        m = Mem(nc, ctx, "qkv")
        w = m.sb("w", [P, 3, KD, D])
        w_part = [m.sb(f"w_part{u}", [P, 3, KD, D], F32R) for u in range(2)]
        b_col = m.sb("b_col", [P, 2, KD])
        b_colq = m.sb("b_colq", [P, 2, KD])
        bv_row = m.sb("bv_row", [P, D])
        x = [m.sb(f"x{i}", [P, KD, GRP]) for i in range(2)]
        x_part = [[m.sb(f"x_part{i}{u}", [P, KD, GRP], F32R) for u in range(2)] for i in range(2)]
        whole = m.sb("whole", [P, 2, GRP])
        part = [m.sb(f"part{i}", [P, 2, GRP], F32R) for i in range(2)]
        v = m.sb("v", [P, PAIRS, TT, 2, VW])
        qk_ps = [m.ps(f"qk_ps{i}", [P, GRP]) for i in range(2)]
        v_ps = [m.ps(f"v_ps{i}", [P, D]) for i in range(2)]
        weights_in, ones_set, scaled = m.sem("weights_in"), m.sem("ones_set"), m.sem("scaled")
        x_in = [m.sem(f"x_in{i}") for i in range(2)]
        qk_done, whole_done, high_done = (m.sem("qk_done"),
                                                  m.sem("whole_done"), m.sem("high_done"))
        low_done, v_done, v_copied = m.sem("low_done"), m.sem("v_done"), m.sem("v_copied")
        part_out = [m.sem(f"part_out{i}") for i in range(2)]
        v_out = m.sem("v_out")
        w_high, w_low, x_high, x_low = (m.sem(a) for a in ("w_high", "w_low", "x_high", "x_low"))
        NW = 8 * 16
        block = ctx.enter_context(nc.Block())

        @block.sync
        def _(sp):
            for i, a in enumerate((WqT, WkT, WvT)):
                sp.dma_start(w[:, i], a.rearrange("(k p) n -> p k n", p=P)).then_inc(weights_in, 16)
            for i, a in enumerate((bq, bk)):
                for k in range(KD):
                    sp.dma_start(b_col[:, i, k:k + 1],
                                 a[k * P:(k + 1) * P].rearrange("(p a) -> p a", a=1)).then_inc(weights_in, 16)
            sp.dma_start(bv_row[:, :], row(bv).broadcast_to([P, D])).then_inc(weights_in, 16)
            src = hsT.rearrange("(k p) t -> p k t", p=P)
            with sp.Fori(0, NGRP // 2) as i:
                for s in range(2):
                    sp.wait_ge(x_low, 2 * i)
                    sp.dma_start(x[s][:, :, :], src[:, :, bass.ds(i * 2 * GRP + s * GRP, GRP)]).then_inc(x_in[s], 16)

        @block.scalar
        def _(act):
            act.wait_ge(weights_in, NW)
            act.wait_ge(scaled, 1)
            nc.scalar.copy(w_part[0][:, :, :, :], w[:, :, :, :]).then_inc(w_high, 1)

            def high_x(g, s):
                act.wait_ge(x_in[s], 16 * (g // 2 + 1))
                if beyond(g, 1):
                    act.wait_ge(v_done, 4 * (g - 1))
                nc.scalar.copy(x_part[s][0][:, :, :], x[s][:, :, :]).then_inc(x_high, 1)

            def finish(i):
                for j in range(4):
                    t, g = j // 2, j % 2
                    act.wait_ge(qk_done, 4 * i + j + 1)
                    act.wait_ge(low_done, 4 * i + max(j - 1, 0))
                    nc.scalar.activation(whole[:, j % 2, :], qk_ps[j % 2][:, :], ACT.Identity,
                                         bias=b_colq[:, t, g:g + 1],
                                         scale=0.25 if t == 0 else 1.0).then_inc(whole_done, 1)

            def step(g, s):
                if exists(g + 1):
                    high_x(g + 1, 1 - s)
                if exists(g):
                    finish(g)

            skewed(act, -1, 0, step)

        @block.vector
        def _(dve):
            nc.vector.memset(v[:, :, :, :, HD:VW], 1.0).then_inc(ones_set, 1)
            dve.wait_ge(weights_in, NW)
            nc.vector.tensor_scalar(b_colq[:, 0, :], b_col[:, 0, :], 0.25, None, ALU.mult)
            nc.vector.tensor_copy(b_colq[:, 1, :], b_col[:, 1, :]).then_inc(scaled, 1)
            dve.wait_ge(w_high, 1)
            nc.vector.tensor_tensor(w_part[1][:, :, :, :], w[:, :, :, :], w_part[0][:, :, :, :].bitcast(F32),
                                    ALU.subtract).then_inc(w_low, 1)

            def low_x(g, s):
                dve.wait_ge(x_high, g + 1)
                nc.vector.tensor_tensor(x_part[s][1][:, :, :], x[s][:, :, :], x_part[s][0][:, :, :].bitcast(F32),
                                        ALU.subtract).then_inc(x_low, 1)

            def finish(i):
                for j in range(4):
                    s = j % 2
                    dve.wait_ge(whole_done, 4 * i + j + 1)
                    dve.wait_ge(part_out[s], 16 * 2 * i + 16 * (j // 2))
                    nc.vector.tensor_copy(part[s][:, 0, :], whole[:, s, :]).then_inc(high_done, 1)
                    dve.wait_ge(high_done, 4 * i + j + 1)
                    nc.vector.tensor_tensor(part[s][:, 1, :], whole[:, s, :], part[s][:, 0, :].bitcast(F32),
                                            ALU.subtract).then_inc(low_done, 1)
                    dve.wait_ge(v_done, 4 * i + j + 1)
                    nc.vector.tensor_tensor(
                        v[:, :, bass.ds(4 * i + j, 1), :, 0:HD].rearrange("p h t a d -> p (h t) a d"),
                        v_ps[s][:, :].rearrange("p (a h d) -> p h a d", a=2, d=HD),
                        bv_row[:, :].rearrange("p (a h d) -> p h a d", a=2, d=HD), ALU.add).then_inc(v_copied, 1)

            def step(g, s):
                if exists(g + 1):
                    low_x(g + 1, 1 - s)
                if exists(g):
                    finish(g)

            skewed(dve, -1, 0, step)

        @block.tensor
        def _(pe):
            pe.wait_ge(w_low, 1)

            def project(i, s):
                pe.wait_ge(x_low, i + 1)
                products = [(k, *term) for k in range(KD) for term in TERMS]
                for j in range(4):
                    t, g = j // 2, j % 2
                    pe.wait_ge(whole_done, 4 * i + max(j - 1, 0))
                    for n, (k, wp, xp) in enumerate(products):
                        mm = nc.tensor.matmul(qk_ps[j % 2][:, :], w_part[wp][:, t, k, g * P:(g + 1) * P], x_part[s][xp][:, k, :],
                                              start=(n == 0), stop=(n == len(products) - 1))
                    mm.then_inc(qk_done, 1)
                    pe.wait_ge(v_copied, 4 * i + max(j - 1, 0))
                    for n, (k, xp, wp) in enumerate(products):
                        mm = nc.tensor.matmul(v_ps[j % 2][:, :], x_part[s][xp][:, k, j * P:(j + 1) * P], w_part[wp][:, 2, k, :],
                                              start=(n == 0), stop=(n == len(products) - 1))
                    mm.then_inc(v_done, 1)

            skewed(pe, 0, 0, project)

        @block.gpsimd
        def _(pool):
            dst = qk_d.rearrange("t h (g p) n -> p t h g n", p=P)
            pool.wait_ge(ones_set, 1)
            with pool.Fori(0, NGRP) as i:
                for j in range(4):
                    t, g = j // 2, j % 2
                    pool.wait_ge(low_done, 4 * i + j + 1)
                    pool.dma_start(dst[:, t, :, g, bass.ds(i * GRP, GRP)], part[j % 2][:, :, :].bitcast(F32)
                                   ).then_inc(part_out[j % 2], 16)
                pool.wait_ge(v_copied, GT * (i + 1))
                pool.dma_start(v_d.rearrange("h p t v -> p h t v")[:, :, bass.ds(i * GT, GT), :],
                               v[:, :, bass.ds(i * GT, GT), :, :].rearrange("p h t a v -> p h t (a v)")
                               ).then_inc(v_out, 16)
            pool.wait_ge(v_out, 16 * NGRP)
            for s in range(2):
                pool.wait_ge(part_out[s], 16 * 2 * NGRP)


def attend(nc, qk_d, v_d, ident, ctx_d, sums_d):
    FULL = 16
    BAND = (NBLK - 2) // 2
    STEPS = FULL + BAND
    UNITS = FULL + 2 * BAND
    LEAD = 3
    WARM = 12
    ROWS, MROW = 97, 96
    CHUNKS = 4
    CB = NBLK // CHUNKS
    CT = T // CHUNKS
    LOCAL = 3 * BLK
    with ExitStack() as ctx:
        m = Mem(nc, ctx, "att")
        q = [m.sb(f"q{i}", [P, NBLK, 2 * BLK], F32R) for i in range(2)]
        k = [m.sb(f"k{i}", [P, T], F32R) for i in range(2)]
        kgm = [m.sb(f"kgm{i}", [P, 2 * BLK], F32R) for i in range(2)]
        kg = [m.sb(f"kg{i}", [P, 2 * BLK], F32R) for i in range(2)]
        v = [m.sb(f"v{i}", [P, TT, 2 * VW]) for i in range(2)]
        vg = [m.sb(f"vg{i}", [P, 3, 2 * VW]) for i in range(2)]
        neg_max = m.sb("neg_max", [P, NBLK])
        chunk_max = m.sb("chunk_max", [P, 2, FULL // 2])
        max_row = m.sb("max_row", [NBLK, P], F32R)
        prob = [m.sb(f"prob{i}", [P, 4 * P]) for i in range(2)]
        prob_b = [m.sb(f"prob_b{i}", [P, 3 * P]) for i in range(2)]
        raw = [m.sb(f"raw{i}", [2 * VW, NBLK, 2 * BLK]) for i in range(2)]
        m_ps = [m.ps(f"m_ps{i}", [P, 512]) for i in range(2)]
        s_ps = [m.ps(f"s_ps{i}", [P, 512]) for i in range(2)]
        b_ps = [m.ps(f"b_ps{i}", [P, 2 * P]) for i in range(2)]
        o_ps = [m.ps(f"o_ps{i}", [P, 512]) for i in range(2)]
        qk_in = [m.sem(f"qk_in{c}") for c in range(CHUNKS)]
        probs_cleared = m.sem("probs_cleared")
        kg_in, v_in, cleared, ones_set = m.sem("kg_in"), m.sem("v_in"), m.sem("cleared"), m.sem("ones_set")
        globals_ready = m.sem("globals_ready")
        m_done, m_reduced, max_ready = m.sem("m_done"), m.sem("m_reduced"), m.sem("max_ready")
        row_turned, row_ready, row_in = m.sem("row_turned"), m.sem("row_ready"), m.sem("row_in")
        s_done, exp_done, pv_done, o_out = m.sem("s_done"), m.sem("exp_done"), m.sem("pv_done"), m.sem("o_out")
        raw_out = [m.sem(f"raw_out{i}") for i in range(2)]
        passed = m.sem("passed")
        block = ctx.enter_context(nc.Block())

        def rounds(eng, one):
            one(0, None, 0)
            with eng.Fori(0, PAIRS // 2 - 1) as j:
                one(2 * j + 1, 2 * j, 1)
                one(2 * j + 2, 2 * j + 1, 0)
            one(PAIRS - 1, PAIRS - 2, 1)
            one(None, PAIRS - 1, 0)

        def m_units(s):
            return [2 * s, 2 * s + 1] if s < BAND else [BAND + s]

        def m_stream(p, b):
            steps = [] if p is None else [(p, b, s) for s in range(LEAD, STEPS)]
            if p is not None and b_next(p):
                steps += [(p + 1, 1 - b, s) for s in range(LEAD)]
            return steps

        def b_next(p):
            return not (isinstance(p, int) and p == PAIRS - 1)

        qk = qk_d.rearrange("t h (a f) n -> t h a f n", a=2)

        def head(p, t, h, a):
            return qk[t, h, a, bass.ds(p * HD, HD), :]

        def load_queries(eng, p, b, c):
            for a in range(2):
                for i, h in enumerate((0, 0, 1)):
                    r = 48 * a + 16 * i
                    eng.dma_start(q[b][r:r + HD, c * CB:(c + 1) * CB, a * BLK:(a + 1) * BLK].bitcast(F32),
                                  head(p, 0, h, a)[:, c * CT:(c + 1) * CT].rearrange("f (l t) -> f l t", t=BLK)
                                  ).then_inc(qk_in[c], 16)

        @block.sync
        def _(sp):
            def load_globals(p, b):
                for a in range(2):
                    for i, h in enumerate((0, 1, 0)):
                        r = 48 * a + 16 * i
                        sp.dma_start(kgm[b][r:r + HD, :].rearrange("f (g t) -> f g t", g=2).bitcast(F32),
                                     head(p, 1, h, a).rearrange("f (l t) -> f l t", t=BLK)[:, 0:NBLK:NBLK - 1, :]
                                     ).then_inc(kg_in, 16)

            def load_keys(p, b, c):
                for a in range(2):
                    for i, h in enumerate((0, 1, 0)):
                        r = 48 * a + 16 * i
                        sp.dma_start(k[b][r:r + HD, c * CT:(c + 1) * CT].bitcast(F32),
                                     head(p, 1, h, a)[:, c * CT:(c + 1) * CT]).then_inc(qk_in[c], 16)

            def load_values(p, b):
                vp = v_d[bass.ds(p, 1)].rearrange("h p t v -> (h p) t v")
                sp.dma_start(v[b][:, :, :], vp).then_inc(v_in, 16)

            for p in range(2):
                sp.wait_ge(ones_set, p + 1)
                if p > 0:
                    sp.wait_ge(kg_in, 96 * p)
                load_globals(p, p)
                for c in range(CHUNKS):
                    if p > 0:
                        sp.wait_ge(qk_in[c], 192 * p)
                    load_keys(p, p, c)
                    if p > 0:
                        sp.wait_ge(cleared, CHUNKS * p + c + 1)
                        load_queries(sp, p, p, c)
                if p > 0:
                    sp.wait_ge(v_in, 16 * p)
                load_values(p, p)

            def refill(p, b):
                sp.wait_ge(kg_in, 96 * (p + 1))
                sp.sem_inc(passed, 1)
                load_globals(p + 1, 1 - b)
                for c in range(CHUNKS):
                    sp.wait_ge(s_done, (p - 1) * STEPS + FULL + min(CB // 2 * (c + 1), BAND))
                    sp.sem_inc(passed, 1)
                    sp.wait_ge(qk_in[c], 192 * (p + 1))
                    sp.sem_inc(passed, 1)
                    load_keys(p + 1, 1 - b, c)
                    load_queries(sp, p + 1, 1 - b, c)
                sp.wait_ge(pv_done, p * STEPS)
                sp.sem_inc(passed, 1)
                sp.wait_ge(v_in, 16 * (p + 1))
                sp.sem_inc(passed, 1)
                load_values(p + 1, 1 - b)

            with sp.Fori(0, PAIRS // 2 - 1) as j:
                for r in range(2):
                    sp.wait_ge(globals_ready, 2 * j + 1 + r)
                    sp.sem_inc(passed, 1)
                    refill(2 * j + 1 + r, (1 + r) % 2)

        @block.tensor
        def _(pe):
            def maxima(p, b, s):
                if s == 0:
                    pe.wait_ge(kg_in, 96 * (p + 1))
                    pe.wait_ge(row_ready, p)
                for c in range(CHUNKS):
                    if s < BAND and (2 * s + 3) // CB == c and (s == 0 or (2 * s + 1) // CB < c):
                        pe.wait_ge(qk_in[c], 192 * (p + 1))
                for u in m_units(s):
                    pe.wait_ge(m_reduced, p * UNITS + max(u - 1, 0))
                    bank = m_ps[u % 2]
                    if u < 2 * BAND:
                        l = 1 + u
                        nc.tensor.matmul(bank[:, 0:LOCAL], q[b][0:MROW, l, :],
                                         k[b][0:MROW, (l - 1) * BLK:(l + 2) * BLK], start=True, stop=True)
                        nc.tensor.matmul(bank[:, LOCAL:LOCAL + 2 * BLK], q[b][0:MROW, l, :], kgm[b][0:MROW, :],
                                         start=True, stop=True).then_inc(m_done, 1)
                    else:
                        f = u - 2 * BAND
                        l, chunk = (0 if f < FULL // 2 else NBLK - 1), f % (FULL // 2)
                        nc.tensor.matmul(bank[:, :], q[b][0:MROW, l, :], k[b][0:MROW, chunk * 512:(chunk + 1) * 512],
                                         start=True, stop=True).then_inc(m_done, 1)

            def turn(p):
                pe.wait_ge(max_ready, p + 1)
                pe.sem_inc(passed, 1)
                nc.tensor.transpose(m_ps[0][0:NBLK, 0:P], neg_max[:, :], ident[:, :]).then_inc(row_turned, 1)

            def scores(e, c, s):
                if s == 0:
                    pe.wait_ge(row_in, 16 * (e + 1))
                if s == FULL:
                    pe.wait_ge(globals_ready, e + 1)
                pe.wait_ge(exp_done, e * STEPS + max(s - 1, 0))
                bank = s_ps[s % 2]
                if s < FULL:
                    for i in range(2):
                        t = 2 * s + i
                        mm = nc.tensor.matmul(bank[:, 2 * i * P:2 * (i + 1) * P], k[c][0:ROWS, t * P:(t + 1) * P],
                                              q[c][0:ROWS, 0:NBLK:NBLK - 1, :], start=True, stop=True)
                else:
                    l0 = 1 + 2 * (s - FULL)
                    both = q[c][0:ROWS, l0:l0 + 2, :].rearrange("p l t -> p (l t)")
                    nc.tensor.matmul(bank[:, 0:2 * P], kg[c][0:ROWS, :], both, start=True, stop=True)
                    nc.tensor.matmul(bank[:, 2 * P:4 * P], k[c][0:ROWS, (l0 - 1) * BLK:(l0 + 1) * BLK], both,
                                     start=True, stop=True)
                    mm = nc.tensor.matmul(b_ps[s % 2][:, :], k[c][0:ROWS, (l0 + 1) * BLK:(l0 + 3) * BLK], both,
                                          start=True, stop=True)
                mm.then_inc(s_done, 1)

            def values(e, c, s):
                pe.wait_ge(exp_done, e * STEPS + s + 1)
                pr, prb = prob[s % 2], prob_b[s % 2]
                if s < FULL:
                    if s == 0:
                        pe.wait_ge(v_in, 16 * (e + 1))
                        pe.wait_ge(o_out, e * (BAND + 1))
                        for _ in range(WARM):
                            nc.tensor.matmul(o_ps[0][:, :], k[c][0:MROW, 0:P], k[c][0:MROW, 0:512], start=True, stop=True)
                    for i in range(2):
                        t = 2 * s + i
                        mm = nc.tensor.matmul(o_ps[1][0:2 * VW, 0:2 * P], v[c][:, t, :],
                                              pr[:, 2 * i * P:2 * (i + 1) * P], start=(t == 0), stop=(t == TT - 1))
                else:
                    n = s - FULL
                    pe.wait_ge(o_out, e * (BAND + 1) + max(n, 1))
                    out = o_ps[n % 2]
                    l0 = 1 + 2 * n
                    if l0 == 1:
                        parts = ((1, 0, P), (0, P, 2 * P))
                    elif l0 == NBLK - 3:
                        parts = ((0, 0, P), (2, P, 2 * P))
                    else:
                        parts = ((0, 0, 2 * P),)
                    for i, (g, x0, x1) in enumerate(parts):
                        nc.tensor.matmul(out[0:2 * VW, x0:x1], vg[c][:, g, :], pr[:, x0:x1],
                                         start=(i == 0), stop=False, skip_group_check=True)
                    for j, source, t in ((0, pr[:, 2 * P:3 * P], n), (1, prb[:, 0:P], n),
                                         (0, prb[:, P:2 * P], n + 1), (1, prb[:, 2 * P:3 * P], n + 1)):
                        mm = nc.tensor.matmul(out[0:2 * VW, j * P:(j + 1) * P], v[c][:, t, :], source,
                                              start=False, stop=(t > n), skip_group_check=True)
                mm.then_inc(pv_done, 1)

            def one(p, e, b):
                ms = m_stream(p, b)
                for s in range(STEPS):
                    if e is not None:
                        scores(e, 1 - b, s)
                    if p is not None and s == STEPS - LEAD:
                        if e is not None:
                            values(e, 1 - b, s - 1)
                        turn(p)
                    if s < len(ms):
                        maxima(*ms[s])
                    if e is not None and s > 0 and (p is None or s != STEPS - LEAD):
                        values(e, 1 - b, s - 1)
                if e is not None:
                    values(e, 1 - b, STEPS - 1)

            for s in range(LEAD):
                maxima(0, 0, s)
            rounds(pe, one)

        @block.scalar
        def _(act):
            def one(p, e, b):
                if e is None:
                    return
                for s in range(STEPS):
                    act.wait_ge(s_done, e * STEPS + s + 1)
                    act.wait_ge(pv_done, e * STEPS + max(s - 1, 0))
                    x, lower, upper = s % 2, slice(0, BLK), slice(BLK, P)
                    if s < FULL:
                        ins = nc.scalar.activation(prob[x][:, :], s_ps[x][:, :], ACT.Exp)
                    else:
                        nc.scalar.activation(prob[x][:, 0:3 * P], s_ps[x][:, 0:3 * P], ACT.Exp)
                        nc.scalar.activation(prob_b[x][upper, 0:P], s_ps[x][upper, 3 * P:4 * P], ACT.Exp)
                        nc.scalar.activation(prob_b[x][lower, P:2 * P], b_ps[x][lower, 0:P], ACT.Exp)
                        ins = nc.scalar.activation(prob_b[x][:, 2 * P:3 * P], b_ps[x][:, P:2 * P], ACT.Exp)
                    ins.then_inc(exp_done, 1)
                    out(e, 1 - b, s - 2)
                out(e, 1 - b, STEPS - 2)
                out(e, 1 - b, STEPS - 1)

            def out(e, c, s):
                if s < FULL - 1:
                    return
                act.wait_ge(pv_done, e * STEPS + s + 1)
                if s == FULL - 1:
                    if not isinstance(e, int) or e > 0:
                        act.wait_ge(raw_out[c], 64 * (e // 2))
                    for j, l in enumerate((0, NBLK - 1)):
                        ins = nc.scalar.copy(raw[c][:, l, :], o_ps[1][0:2 * VW, j * P:(j + 1) * P])
                else:
                    n = s - FULL
                    ins = nc.scalar.copy(raw[c][:, 1 + 2 * n:3 + 2 * n, :].rearrange("p l t -> p (l t)"),
                                         o_ps[n % 2][0:2 * VW, 0:2 * P])
                ins.then_inc(o_out, 1)

            for c in range(CHUNKS):
                act.wait_ge(cleared, c + 1)
                load_queries(act, 0, 0, c)
            act.wait_ge(probs_cleared, 1)
            rounds(act, one)

        @block.vector
        def _(dve):
            for b in range(2):
                for c in range(CHUNKS):
                    nc.vector.memset(q[b][:, c * CB:(c + 1) * CB, :].bitcast(U32), 0).then_inc(cleared, 1)
            for b in range(2):
                nc.vector.memset(vg[b][:, :, :].bitcast(U32), 0)

            def maximum(p, s):
                if s == 0:
                    dve.wait_ge(row_turned, p)
                for u in m_units(s):
                    dve.wait_ge(m_done, p * UNITS + u + 1)
                    if u < 2 * BAND:
                        l = 1 + u
                        ins = nc.vector.tensor_reduce(neg_max[:, l:l + 1], m_ps[u % 2][:, 0:LOCAL + 2 * BLK], AX.X,
                                                      ALU.max, negate=True)
                    else:
                        f = u - 2 * BAND
                        ins = nc.vector.tensor_reduce(chunk_max[:, f // 8, f % 8:f % 8 + 1], m_ps[u % 2][:, :],
                                                      AX.X, ALU.max)
                    ins.then_inc(m_reduced, 1)

            def close(p, b):
                dve.wait_ge(m_reduced, (p + 1) * UNITS)
                for i, l in enumerate((0, NBLK - 1)):
                    ins = nc.vector.tensor_reduce(neg_max[:, l:l + 1], chunk_max[:, i, :], AX.X, ALU.max, negate=True)
                ins.then_inc(max_ready, 1)
                dve.wait_ge(row_turned, p + 1)
                dve.wait_ge(row_in, 16 * p)
                nc.vector.tensor_copy(max_row[:, :], m_ps[0][0:NBLK, 0:P]).then_inc(row_ready, 1)
                if not isinstance(p, int) or p > 0:
                    dve.wait_ge(pv_done, (p - 1) * STEPS)
                nc.vector.tensor_copy(kg[b][0:ROWS, :], kgm[b][0:ROWS, :].bitcast(F32))
                dve.wait_ge(v_in, 16 * (p + 1))
                nc.vector.tensor_copy(vg[b][0:BLK, 0, :], v[b][0:BLK, 0, :])
                nc.vector.tensor_copy(vg[b][0:BLK, 2, :], v[b][0:BLK, 0, :])
                nc.vector.tensor_copy(vg[b][BLK:P, 0, :], v[b][BLK:P, TT - 1, :])
                nc.vector.tensor_copy(vg[b][BLK:P, 1, :], v[b][BLK:P, TT - 1, :]).then_inc(globals_ready, 1)

            def one(p, e, b):
                for pm, bm, s in m_stream(p, b):
                    maximum(pm, s)
                    if s == STEPS - 1:
                        close(pm, bm)

            for s in range(LEAD):
                maximum(0, s)
            rounds(dve, one)

        @block.gpsimd
        def _(pool):
            def one(p, e, b):
                if p is not None:
                    pool.wait_ge(row_ready, p + 1)
                    pool.sem_inc(passed, 1)
                    pool.dma_start(q[b][MROW:MROW + 1, :, :].rearrange("p l t -> p (l t)").bitcast(F32),
                                   max_row[:, :].bitcast(F32)).then_inc(row_in, 16)
                if e is not None:
                    pool.wait_ge(o_out, (e + 1) * (BAND + 1))
                    for a in range(2):
                        cols = raw[1 - b][a * VW:(a + 1) * VW, :, a * BLK:(a + 1) * BLK]
                        pool.dma_start(heads[a, bass.ds(e * HD, HD)].rearrange("f (l t) -> f l t", t=BLK),
                                       cols[0:HD]).then_inc(raw_out[1 - b], 16)
                        pool.dma_start(sums[a, bass.ds(e, 1)].rearrange("f (l t) -> f l t", t=BLK),
                                       cols[HD:VW]).then_inc(raw_out[1 - b], 16)

            for b in range(2):
                nc.gpsimd.memset(kgm[b][MROW:ROWS, :].bitcast(F32), 1.0)
                nc.gpsimd.memset(k[b][MROW:ROWS, :].bitcast(F32), 1.0).then_inc(ones_set, 1)

            pool.wait_ge(ones_set, 2)
            nc.gpsimd.memset(prob_b[0][:, :], 0.0)
            nc.gpsimd.memset(prob_b[1][:, :], 0.0).then_inc(probs_cleared, 1)

            heads = ctx_d.rearrange("(a f) n -> a f n", a=2)
            sums = sums_d.rearrange("(a f) n -> a f n", a=2)
            rounds(pool, one)
            for c in range(2):
                pool.wait_ge(raw_out[c], 64 * PAIRS // 2)


def beyond(g, n):
    return not isinstance(g, int) or g > n


def skewed(eng, first, last, step, start=2):
    for g in range(first, start):
        step(g, g % 2)
    with eng.Fori(start // 2, NGRP // 2 - 1) as i:
        step(2 * i, 0)
        step(2 * i + 1, 1)
    for g in range(NGRP - 2, NGRP + last):
        step(g, g % 2)


def exists(g):
    return not isinstance(g, int) or 0 <= g < NGRP


class Norm:

    def __init__(self, nc, m, x, ready, out_d, ident=None, xT=None):
        self.nc, self.x, self.ready, self.out_d, self.ident, self.xT = nc, x, ready, out_d, ident, xT
        self.y = [m.sb(f"y{i}", [P, GT, D]) for i in range(2)]
        self.part = [m.sb(f"part{i}", [P, GT, 6]) for i in range(2)]
        self.mean_var = [m.sb(f"mean_var{i}", [P, GT, 2]) for i in range(2)]
        self.std = [m.sb(f"std{i}", [P, GT]) for i in range(2)]
        self.inv = [m.sb(f"inv{i}", [P, GT]) for i in range(2)]
        self.eps = m.sb("eps", [P, 1])
        self.bank = [m.ps(f"turn{k}", [P, GRP]) for k in range(KD)] if xT is not None else None
        self.eps_set, self.parted, self.aggregated, self.std_done, self.inv_done, self.normed = (
            m.sem(a) for a in ("eps_set", "parted", "aggregated", "std_done", "inv_done", "normed"))
        self.turned, self.copied, self.passed = m.sem("turned"), m.sem("copied"), m.sem("ln_passed")
        self.stored = [m.sem(f"stored{i}") for i in range(2)]

    def begin(self):
        self.nc.vector.memset(self.eps[:, :], LN_EPS).then_inc(self.eps_set, 1)

    def stats(self, dve, g, s):
        dve.wait_ge(self.ready, GT * (g + 1))
        for j in range(GT):
            self.nc.vector.bn_stats(self.part[s][:, j, :], self.x[s][:, j, :]).then_inc(self.parted, 1)
        dve.wait_ge(self.parted, GT * (g + 1))
        dve.sem_inc(self.passed, 1)
        for j in range(GT):
            self.nc.vector.bn_aggr(self.mean_var[s][:, j, :], self.part[s][:, j, :]).then_inc(self.aggregated, 1)

    def root(self, act, g, s):
        act.wait_ge(self.eps_set, 1)
        act.wait_ge(self.aggregated, GT * (g + 1))
        if beyond(g, 1):
            act.wait_ge(self.inv_done, g - 1)
        var = self.mean_var[s][:, :, 1:2].rearrange("p g a -> p (g a)")
        self.nc.scalar.activation(self.std[s][:, :], var, ACT.Sqrt, bias=self.eps[:, 0:1]).then_inc(self.std_done, 1)

    def apply(self, dve, g, s):
        dve.wait_ge(self.std_done, g + 1)
        self.nc.vector.reciprocal(self.inv[s][:, :], self.std[s][:, :]).then_inc(self.inv_done, 1)
        if beyond(g, 1):
            dve.wait_ge(self.stored[s], 16 * (g // 2))
            if self.xT is not None:
                dve.wait_ge(self.turned, KD * (g - 1))
        dve.wait_ge(self.inv_done, g + 1)
        for j in range(GT):
            self.nc.vector.tensor_scalar(self.y[s][:, j, :], self.x[s][:, j, :], self.mean_var[s][:, j, 0:1],
                                         self.inv[s][:, j:j + 1], ALU.subtract, ALU.mult).then_inc(self.normed, 1)

    def turn(self, pe, g, s):
        pe.wait_ge(self.normed, GT * (g + 1))
        for k in range(KD):
            if beyond(g, 0):
                pe.wait_ge(self.copied, KD * (g - 1) + k + 1)
            for j in range(GT):
                mm = self.nc.tensor.transpose(self.bank[k][:, j * P:(j + 1) * P], self.y[s][:, j, k * P:(k + 1) * P],
                                              self.ident[:, :])
            mm.then_inc(self.turned, 1)

    def copy(self, act, g, s):
        for k in range(KD):
            act.wait_ge(self.turned, KD * g + k + 1)
            self.nc.scalar.copy(self.xT[:, k, bass.ds(g * GRP, GRP)], self.bank[k][:, :]).then_inc(self.copied, 1)

    def store(self, sp, g, s):
        sp.wait_ge(self.normed, GT * (g + 1))
        sp.dma_start(token_rows(self.out_d, g), self.y[s][:, :, :]).then_inc(self.stored[s], 16)

    def finish(self, sp):
        for s in range(2):
            sp.wait_ge(self.stored[s], 16 * NGRP // 2)


def merge_heads(nc, hs, ctx_d, sums_d, ident, out_d, xT):
    with ExitStack() as ctx:
        m = Mem(nc, ctx, "merge")
        c = [m.sb(f"c{i}", [P, KD, GRP]) for i in range(2)]
        z = [m.sb(f"z{i}", [H, GRP]) for i in range(2)]
        hidden = [m.sb(f"hidden{i}", [P, GT, D]) for i in range(2)]
        x = [m.sb(f"x{i}", [P, GT, D]) for i in range(2)]
        inv = [m.sb(f"inv_sum{i}", [P, H]) for i in range(2)]
        scaled = [m.sb(f"scaled{i}", [P, D]) for i in range(4)]
        ps = [m.ps(f"ps{i}", [P, 512]) for i in range(4)]
        in_ = [m.sem(f"in{i}") for i in range(2)]
        brought, inverted, multiplied, added = m.sem("brought"), m.sem("inverted"), m.sem("multiplied"), m.sem("added")
        norm = Norm(nc, m, x, added, out_d, ident, xT)
        block = ctx.enter_context(nc.Block())

        @block.sync
        def _(sp):
            def load(g, s):
                toks = bass.ds(g * GRP, GRP)
                sp.dma_start(c[s][:, :, :], ctx_d.rearrange("(k p) t -> p k t", p=P)[:, :, toks]).then_inc(in_[s], 16)
                sp.dma_start(z[s][:, :], sums_d[:, toks]).then_inc(in_[s], 16)
                sp.dma_start(hidden[s][:, :, :], token_rows(hs, g)).then_inc(in_[s], 16)

            def step(g, s):
                if exists(g + 2):
                    if beyond(g, -1):
                        sp.wait_ge(added, GT * (g + 1))
                    load(g + 2, s)
                if exists(g):
                    norm.store(sp, g, s)

            skewed(sp, -2, 0, step)
            norm.finish(sp)

        @block.tensor
        def _(pe):
            def bring(g, s):
                pe.wait_ge(in_[s], 48 * (g // 2 + 1))
                for j in range(GT):
                    if beyond(g, 0):
                        pe.wait_ge(multiplied, GT * (g - 1) + j + 1)
                    cols = slice(j * P, (j + 1) * P)
                    for k in range(KD):
                        nc.tensor.transpose(ps[j][:, k * P:(k + 1) * P], c[s][:, k, cols], ident[:, :])
                    nc.tensor.transpose(ps[j][:, D:D + H], z[s][:, cols], ident[0:H, 0:H]).then_inc(brought, 1)

            def step(g, s):
                if exists(g + 1):
                    bring(g + 1, 1 - s)
                if exists(g - 1):
                    norm.turn(pe, g - 1, 1 - s)

            skewed(pe, -1, 1, step)

        @block.vector
        def _(dve):
            norm.begin()

            def divide(g, s):
                for j in range(GT):
                    n = GT * g + j
                    dve.wait_ge(brought, n + 1)
                    nc.vector.reciprocal(inv[j % 2][:, :], ps[j][:, D:D + H]).then_inc(inverted, 1)
                    if beyond(g, 0):
                        dve.wait_ge(added, n - GT + 1)
                    dve.wait_ge(inverted, n + 1)
                    nc.vector.tensor_tensor(
                        scaled[j][:, :].rearrange("p (h d) -> p h d", h=H),
                        ps[j][:, 0:D].rearrange("p (h d) -> p h d", h=H),
                        inv[j % 2][:, :].rearrange("p (h a) -> p h a", a=1).broadcast_to([P, H, HD]),
                        ALU.mult).then_inc(multiplied, 1)

            def step(g, s):
                if exists(g + 1):
                    divide(g + 1, 1 - s)
                if exists(g):
                    norm.apply(dve, g, s)
                if exists(g + 1):
                    norm.stats(dve, g + 1, 1 - s)

            skewed(dve, -1, 0, step)

        @block.gpsimd
        def _(pool):
            def step(g, s):
                if beyond(g, 1):
                    pool.wait_ge(norm.normed, GT * (g - 1))
                for j in range(GT):
                    pool.wait_ge(multiplied, GT * g + j + 1)
                    nc.gpsimd.tensor_tensor(x[s][:, j, :], scaled[j][:, :], hidden[s][:, j, :], ALU.add).then_inc(added, 1)

            skewed(pool, 0, 0, step)

        @block.scalar
        def _(act):
            def step(g, s):
                if exists(g):
                    norm.root(act, g, s)
                if exists(g - 1):
                    norm.copy(act, g - 1, 1 - s)

            skewed(act, 0, 1, step)


def combine(nc, x_d, y_d, pos, weight, out_d):
    with ExitStack() as ctx:
        m = Mem(nc, ctx, "combine")
        x = [m.sb(f"x{i}", [P, GT, D]) for i in range(2)]
        y = [m.sb(f"y_rows{i}", [P, GT, 2, D]) for i in range(2)]
        row_no = [m.sb(f"row_no{i}", [P, 2, GT], I32) for i in range(2)]
        first, summed, numbered, passed = m.sem("first"), m.sem("summed"), m.sem("numbered"), m.sem("passed")
        x_in, y_in = ([m.sem(f"{a}{i}") for i in range(2)] for a in ("x_in", "y_in"))
        norm = Norm(nc, m, x, summed, out_d)
        block = ctx.enter_context(nc.Block())

        @block.sync
        def _(sp):
            def step(g, s):
                if exists(g):
                    norm.store(sp, g, s)
                if exists(g + 2):
                    sp.dma_start(x[s][:, :, :], token_rows(x_d, g + 2)).then_inc(x_in[s], 16)

            skewed(sp, -2, 0, step)
            norm.finish(sp)

        @block.gpsimd
        def _(pool):
            def step(g, s):
                gather_pairs(nc, pool, g, s, pos, y_d, y, row_no, y_in, numbered, summed, passed)

            skewed(pool, 0, 0, step)

        @block.vector
        def _(dve):
            norm.begin()

            def step(g, s):
                if exists(g + 1):
                    add_pairs(nc, dve, g + 1, 1 - s, weight, x, y, x_in, y_in, first, summed)
                if exists(g):
                    norm.apply(dve, g, s)
                if exists(g + 1):
                    norm.stats(dve, g + 1, 1 - s)

            skewed(dve, -1, 0, step)

        @block.scalar
        def _(act):
            skewed(act, 0, 0, lambda g, s: norm.root(act, g, s))


def gather_pairs(nc, pool, g, s, pos, y_d, y, row_no, y_in, numbered, summed, passed):
    pool.wait_ge(y_in[s], 16 * 2 * GT * (g // 2))
    nc.gpsimd.tensor_copy(row_no[s][:, :, :], pos[:, :, bass.ds(g * GT, GT)]).then_inc(numbered, 1)
    pool.wait_ge(numbered, g + 1)
    if beyond(g, 1):
        pool.wait_ge(summed, GT * (g - 1))
    pool.sem_inc(passed, 1)
    for j in range(GT):
        for a in range(2):
            nc.gpsimd.indirect_dma_start(
                out=y[s][:, j, a, :], out_offset=None, in_=y_d,
                in_offset=bass.IndirectOffsetOnAxis(ap=row_no[s][:, a, j:j + 1], axis=0)).then_inc(y_in[s], 16)


def add_pairs(nc, dve, g, s, weight, x, y, x_in, y_in, first, summed):
    dve.wait_ge(x_in[s], 16 * (g // 2 + 1))
    dve.wait_ge(y_in[s], 16 * 2 * GT * (g // 2 + 1))
    for j in range(GT):
        nc.vector.scalar_tensor_tensor(x[s][:, j, :], y[s][:, j, 0, :], weight[:, 0, bass.ds(g * GT + j, 1)],
                                       x[s][:, j, :], ALU.mult, ALU.add).then_inc(first, 1)
    for j in range(GT):
        dve.wait_ge(first, GT * g + j + 1)
        nc.vector.scalar_tensor_tensor(x[s][:, j, :], y[s][:, j, 1, :], weight[:, 1, bass.ds(g * GT + j, 1)],
                                       x[s][:, j, :], ALU.mult, ALU.add).then_inc(summed, 1)


def route(nc, tag, xT, Wg, bg, ident, upto, capacity, weight, pos, table, tile_expert, prefetch, shared=None):
    NT = table.shape[1]
    BIG = 3.0e38
    BURSTS = 8 if shared else 4
    RING = 2 * TT // BURSTS
    KF = shared[0].shape[1] // P if shared else 1
    with ExitStack() as ctx:
        m = Mem(nc, ctx, tag)
        wg = m.sb("wg", [P, KD, E])
        bias = m.sb("bias", [E, 1])
        logit_row = [m.sb(f"logit_row{i}", [E, GRP]) for i in range(2)]
        S = [P, E, TT]
        value, low, hit, cand = (m.sb(a, S) for a in ("value", "low", "hit", "cand"))
        expo = cand
        one = [m.sb(f"one{a}", S) for a in range(2)]
        labels, tile_sum, upto_tile, place, carry = (m.sb(a, S) for a in ("labels", "tile_sum", "upto_tile", "place", "carry"))
        number = m.sb("number", S)
        top = [m.sb(f"top{a}", [P, TT]) for a in range(2)]
        pick = m.sb("pick", [P, TT])
        total, inv = m.sb("total", [P, TT]), m.sb("inv", [P, TT])
        tiles, end, base = m.sb("tiles", [P, E]), m.sb("end", [P, E]), m.sb("base", [P, E])
        ones_e = m.sb("ones_e", [P, E])
        at_tile = m.sb("at_tile", [P, NT, E])
        tile_no = m.sb("tile_no", [P, NT])
        where = m.sb("where", [P, 2, TT])
        bits = m.sb("bits", [P, 2, TT], I32)
        slot, tile_of = m.sb("slot", [P, 2, TT]), m.sb("tile_of", [P, 2, TT])
        counts_i, tokens_i = m.sb("counts_i", [P, P], I32), m.sb("tokens_i", [P, TT], I32)
        counts, tokens = m.sb("counts", [P, P]), m.sb("tokens", [P, TT])
        ones = m.sb("ones", [P, P])
        in_slot = [m.sb(f"in_slot{i}", [P, P], F32R) for i in range(RING)]
        in_tile = [m.sb(f"in_tile{i}", [P, NT], F32R) for i in range(RING)]
        nothing = m.sb("nothing", [P, P], F32R)
        h_ps = [m.ps(f"h_ps{i}", [P, GRP]) for i in range(2)]
        y_ps = [m.ps(f"y_ps{i}", [P, D]) for i in range(2)]
        row_ps = [bank[0:E, :] for bank in h_ps]
        col_ps = [bank[:, 0:GT * E].rearrange("p (j e) -> p j e", j=GT) for bank in y_ps]
        count_ps, table_ps = m.ps("count_ps", [P, 2, E * TT]), m.ps("table_ps", [P, NT])
        cum_ps, sum_ps = (count_ps[:, i, :].rearrange("p (e t) -> p e t", e=E) for i in range(2))
        if shared:
            y = [m.sb(f"y{i}", [P, GT, D]) for i in range(2)]
            product = m.sb("product", [P, GT, D])
            w1_part = [m.sb(f"w1_part{u}", [P, KD, KF * P], F32R) for u in range(2)]
            w2_part = [m.sb(f"w2_part{u}", [P, KF, D], F32R) for u in range(2)]
            x_part = [[m.sb(f"x_part{i}{u}", [P, KD, GRP], F32R) for u in range(2)] for i in range(2)]
            whole = m.sb("whole", [P, 2, GRP])
            h_part = [[m.sb(f"h_part{i}{u}", [P, KF, GRP], F32R) for u in range(2)] for i in range(2)]
            w1 = y[0][:, :, :].rearrange("p j d -> p (j d)").rearrange("p (k f) -> p k f", k=KD)
            w2 = y[1][:, :, :].rearrange("p j d -> p (j d)").rearrange("p (k d) -> p k d", k=KF)
        w_in, h_done, h_ready, y_done, y_copied, summed = (m.sem(a) for a in (
            "w_in", "h_done", "h_ready", "y_done", "y_copied", "summed"))
        w_high, w_low, x_high, x_low, h_whole, h_high = (m.sem(a) for a in (
            "w_high", "w_low", "x_high", "x_low", "h_whole", "h_high"))
        x_in, part_out = ([m.sem(f"{a}{i}") for i in range(2)] for a in ("x_in", "part_out"))
        wg_in, row_done, row_copied, turned, logits_in = (m.sem("wg_in"), m.sem("row_done"), m.sem("row_copied"),
                                                          m.sem("turned"), m.sem("logits_in"))
        step, exp_in, exp_done, labels_in, counted = m.sem("step"), m.sem("exp_in"), m.sem("exp_done"), m.sem("labels_in"), m.sem("counted")
        iotas, made, placed = m.sem("iotas"), m.sem("made"), m.sem("placed")
        NW = 16 * (1 + (bg is not None))
        passed = m.sem("passed")
        block = ctx.enter_context(nc.Block())

        @block.sync
        def _(sp):
            sp.dma_start(wg[:, :, :], Wg.rearrange("(k p) e -> p k e", p=P)).then_inc(wg_in, 16)
            if bg is not None:
                sp.dma_start(bias[:, :], bg.rearrange("(e a) -> e a", a=1)).then_inc(wg_in, 16)
            if not shared:
                prefetch(sp)
            if shared:
                sp.dma_start(w1, shared[0].rearrange("(k p) f -> p k f", p=P)).then_inc(w_in, 16)
                sp.dma_start(w2, shared[1].rearrange("(k p) f -> p k f", p=P)).then_inc(w_in, 16)
                for s in range(2):
                    sp.wait_ge(w_low, s + 1)
                    sp.dma_start(y[s][:, :, :], token_rows(shared[2], s)).then_inc(x_in[s], 16)
                prefetch(sp)

                def step(g, s):
                    if exists(g):
                        sp.wait_ge(summed, GT * (g + 1))
                        sp.dma_start(token_rows(shared[3], g), y[s][:, :, :]).then_inc(part_out[s], 16)
                    if exists(g + 2):
                        sp.wait_ge(part_out[s], 16 * (g // 2 + 1))
                        sp.sem_inc(passed, 1)
                        sp.dma_start(y[s][:, :, :], token_rows(shared[2], g + 2)).then_inc(x_in[s], 16)

                skewed(sp, 0, 0, step)
                for s in range(2):
                    sp.wait_ge(part_out[s], 16 * NGRP // 2)

        @block.tensor
        def _(pe):
            pe.wait_ge(wg_in, NW)
            with pe.Fori(0, NGRP // 2) as i:
                for s in range(2):
                    g = 2 * i + s
                    pe.wait_ge(row_copied, 2 * i)
                    for k in range(KD):
                        mm = nc.tensor.matmul(row_ps[s], wg[:, k, :], xT[:, k, bass.ds(g * GRP, GRP)],
                                              start=(k == 0), stop=(k == KD - 1))
                    mm.then_inc(row_done, 1)
                for s in range(2):
                    g = 2 * i + s
                    pe.wait_ge(row_copied, g + 1)
                    pe.wait_ge(logits_in, 2 * i)
                    pe.sem_inc(passed, 1)
                    for j in range(GT):
                        mm = nc.tensor.transpose(col_ps[s][:, j, :], logit_row[s][:, j * P:(j + 1) * P], ident[0:E, 0:E])
                    mm.then_inc(turned, 1)

            def counts_of_labels():
                pe.wait_ge(labels_in, 1)
                flat = labels[:, :, :].rearrange("p e t -> p (e t)")
                nc.tensor.matmul(count_ps[:, 1, :], ones[:, :], flat, start=True, stop=True)
                nc.tensor.matmul(count_ps[:, 0, :], upto[:, :], flat, start=True, stop=True).then_inc(counted, 1)
                nc.tensor.matmul(table_ps[:, :], nothing[:, :], nothing[:, 0:NT], start=True, stop=False,
                                 skip_group_check=True)

            def burst(q):
                for r in range(RING):
                    pe.wait_ge(made, RING * q + r + 1)
                    nc.tensor.matmul(table_ps[:, :], in_slot[r][:, :], in_tile[r][:, :], start=False, stop=False,
                                     skip_group_check=True).then_inc(placed, 1)

            def up(g, s):
                products = [(k, *term) for k in range(KD) for term in TERMS]
                pe.wait_ge(x_low, g + 1)
                for f in range(KF):
                    if beyond(g, 0) or f > 1:
                        pe.wait_ge(h_whole, KF * g + f - 1)
                    for n, (k, wp, xp) in enumerate(products):
                        mm = nc.tensor.matmul(h_ps[f % 2][:, :], w1_part[wp][:, k, f * P:(f + 1) * P],
                                              x_part[s][xp][:, k, :], start=(n == 0), stop=(n == len(products) - 1))
                    mm.then_inc(h_done, 1)

            def down(g, s):
                products = [(f, *term) for f in range(KF) for term in TERMS]
                pe.wait_ge(h_ready, KF * (g + 1))
                for j in range(GT):
                    if beyond(g, 0) or j > 1:
                        pe.wait_ge(y_copied, GT * g + j - 1)
                    for n, (f, hp, wp) in enumerate(products):
                        mm = nc.tensor.matmul(y_ps[j % 2][:, :], h_part[s][hp][:, f, j * P:(j + 1) * P],
                                              w2_part[wp][:, f, :], start=(n == 0), stop=(n == len(products) - 1))
                    mm.then_inc(y_done, 1)

            def step(g, s, bursts=False):
                up(g, s)
                if bursts:
                    burst(2 * g - BURSTS)
                down(g - 1, 1 - s)
                if bursts:
                    burst(2 * g - BURSTS + 1)

            pe.wait_ge(logits_in, NGRP)
            if shared:
                pe.wait_ge(w_low, 2)
                up(0, 0)
                step(1, 1)
                step(2, 0)
                counts_of_labels()
                step(3, 1)
                with pe.Fori(2, NGRP // 2) as i:
                    for s in range(2):
                        step(2 * i + s, s, bursts=True)
                down(NGRP - 1, 1)
            else:
                counts_of_labels()
                with pe.Fori(0, BURSTS) as q:
                    burst(q)
            nc.tensor.matmul(table_ps[:, :], nothing[:, :], nothing[:, 0:NT], start=False, stop=True,
                             skip_group_check=True).then_inc(placed, 1)

        @block.scalar
        def _(act):
            act.wait_ge(wg_in, NW)
            with act.Fori(0, NGRP // 2) as i:
                for s in range(2):
                    act.wait_ge(row_done, 2 * i + s + 1)
                    act.wait_ge(turned, 2 * i)
                    if bg is None:
                        nc.scalar.copy(logit_row[s][:, :], row_ps[s]).then_inc(row_copied, 1)
                    else:
                        nc.scalar.activation(logit_row[s][:, :], row_ps[s], ACT.Identity,
                                             bias=bias[:, 0:1]).then_inc(row_copied, 1)

            def exponentials():
                act.wait_ge(exp_in, 1)
                if capacity is None:
                    nc.scalar.activation(expo[:, :, :], low[:, :, :], ACT.Exp).then_inc(exp_done, 1)
                else:
                    nc.scalar.activation(total[:, :], pick[:, :], ACT.Exp).then_inc(exp_done, 1)

            def high_x(g, s):
                if beyond(g, 1):
                    act.wait_ge(h_done, KF * (g - 1))
                nc.scalar.copy(x_part[s][0][:, :, :], xT[:, :, bass.ds(g * GRP, GRP)]).then_inc(x_high, 1)

            def hide(g, s):
                if beyond(g, 1):
                    act.wait_ge(y_done, GT * (g - 1))
                for f in range(KF):
                    act.wait_ge(h_done, KF * g + f + 1)
                    if beyond(g, 0) or f > 1:
                        act.wait_ge(h_ready, KF * g + f - 1)
                    nc.scalar.activation(whole[:, f % 2, :], h_ps[f % 2][:, :], ACT.Gelu).then_inc(h_whole, 1)
                    act.wait_ge(h_whole, KF * g + f + 1)
                    nc.scalar.copy(h_part[s][0][:, f, :], whole[:, f % 2, :]).then_inc(h_high, 1)

            def take(g, s):
                for j in range(GT):
                    act.wait_ge(y_done, GT * g + j + 1)
                    if beyond(g, 0):
                        act.wait_ge(summed, GT * (g - 1) + j + 1)
                    nc.scalar.copy(product[:, j, :], y_ps[j % 2][:, :]).then_inc(y_copied, 1)

            def step(g, s):
                if exists(g + 1):
                    high_x(g + 1, 1 - s)
                if exists(g):
                    hide(g, s)
                if exists(g - 1):
                    take(g - 1, 1 - s)

            if shared:
                act.wait_ge(w_in, 32)
                nc.scalar.copy(w1_part[0][:, :, :], w1).then_inc(w_high, 1)
                nc.scalar.copy(w2_part[0][:, :, :], w2).then_inc(w_high, 1)
                high_x(0, 0)
            exponentials()
            if shared:
                skewed(act, 0, 1, step)

        @block.gpsimd
        def _(pool):
            nc.gpsimd.iota(counts_i[:, :], pattern=[[1, P]], base=0, channel_multiplier=0).then_inc(iotas, 1)
            nc.gpsimd.iota(tokens_i[:, :], pattern=[[P, TT]], base=0, channel_multiplier=1).then_inc(iotas, 1)

            def add(g, s):
                pool.wait_ge(x_in[s], 16 * (g // 2 + 1))
                for j in range(GT):
                    pool.wait_ge(y_copied, GT * g + j + 1)
                    nc.gpsimd.tensor_tensor(y[s][:, j, :], product[:, j, :], y[s][:, j, :], ALU.add).then_inc(summed, 1)

            def low_x(g, s):
                pool.wait_ge(x_high, g + 1)
                nc.gpsimd.tensor_tensor(x_part[s][1][:, :, :], xT[:, :, bass.ds(g * GRP, GRP)],
                                        x_part[s][0][:, :, :].bitcast(F32), ALU.subtract).then_inc(x_low, 1)

            def low_h(g, s):
                for f in range(KF):
                    pool.wait_ge(h_high, KF * g + f + 1)
                    nc.gpsimd.tensor_tensor(h_part[s][1][:, f, :], whole[:, f % 2, :],
                                            h_part[s][0][:, f, :].bitcast(F32), ALU.subtract).then_inc(h_ready, 1)

            def step(g, s):
                if exists(g + 1):
                    low_x(g + 1, 1 - s)
                if exists(g):
                    low_h(g, s)
                if exists(g - 1):
                    add(g - 1, 1 - s)

            if shared:
                for i, (a, of) in enumerate(((w1_part, w1), (w2_part, w2))):
                    pool.wait_ge(w_high, i + 1)
                    nc.gpsimd.tensor_tensor(a[1][:, :, :], of, a[0][:, :, :].bitcast(F32),
                                            ALU.subtract).then_inc(w_low, 1)
                skewed(pool, -1, 1, step)

        @block.vector
        def _(dve):
            count = [0]

            def settle(ins):
                ins.then_inc(step, 1)
                count[0] += 1
                dve.wait_ge(step, count[0])

            def over_experts(a):
                return a[:, :, :].rearrange("p e t -> p t e")

            def to_experts(a):
                return a.rearrange("p (a t) -> p a t", a=1).broadcast_to(S)

            def to_tiles(a):
                return a.rearrange("p (e a) -> p e a", a=1).broadcast_to(S)

            dve.wait_ge(iotas, 2)
            nc.vector.memset(nothing[:, :].bitcast(U32), 0)
            for e in range(E):
                nc.vector.memset(number[:, e, :], float(e - E))
            nc.vector.memset(ones_e[:, :], 1.0)
            nc.vector.memset(ones[:, :], 1.0)
            nc.vector.memset(carry[:, :, 1:TT], 1.0)
            nc.vector.memset(carry[:, :, 0:1], 0.0)
            nc.vector.tensor_copy(tokens[:, :], tokens_i[:, :])
            settle(nc.vector.tensor_copy(counts[:, :], counts_i[:, :]))
            with dve.Fori(0, NGRP // 2) as i:
                for s in range(2):
                    g = 2 * i + s
                    dve.wait_ge(turned, g + 1)
                    nc.vector.tensor_copy(value[:, :, bass.ds(g * GT, GT)].rearrange("p e j -> p j e"),
                                          col_ps[s][:, :, :]).then_inc(logits_in, 1)
            dve.wait_ge(logits_in, NGRP)
            if capacity is None:
                settle(nc.vector.tensor_reduce(top[0][:, :], over_experts(value), AX.X, ALU.max))
                nc.vector.tensor_tensor(low[:, :, :], value[:, :, :], to_experts(top[0][:, :]), ALU.subtract).then_inc(exp_in, 1)
                dve.wait_ge(exp_done, 1)
                settle(nc.vector.tensor_reduce(total[:, :], over_experts(expo), AX.X, ALU.add))
                settle(nc.vector.reciprocal(inv[:, :], total[:, :]))
                settle(nc.vector.tensor_tensor(value[:, :, :], expo[:, :, :], to_experts(inv[:, :]), ALU.mult))
            for a in range(2):
                src = value if a == 0 else low
                settle(nc.vector.tensor_reduce(top[a][:, :], over_experts(src), AX.X, ALU.max))
                settle(nc.vector.tensor_tensor(hit[:, :, :], src[:, :, :], to_experts(top[a][:, :]), ALU.is_equal))
                settle(nc.vector.scalar_tensor_tensor(cand[:, :, :], hit[:, :, :], float(-E), number[:, :, :], ALU.mult, ALU.add))
                settle(nc.vector.tensor_reduce(pick[:, :], over_experts(cand), AX.X, ALU.min))
                settle(nc.vector.tensor_scalar(pick[:, :], pick[:, :], float(E), None, ALU.add))
                settle(nc.vector.tensor_tensor(one[a][:, :, :], number[:, :, :], to_experts(pick[:, :]), ALU.is_equal))
                if a == 0:
                    settle(nc.vector.scalar_tensor_tensor(low[:, :, :], one[0][:, :, :], -BIG, value[:, :, :], ALU.mult, ALU.add))
            if capacity is None:
                settle(nc.vector.tensor_tensor(total[:, :], top[0][:, :], top[1][:, :], ALU.add))
                settle(nc.vector.reciprocal(inv[:, :], total[:, :]))
                for a in range(2):
                    nc.vector.tensor_tensor(weight[:, a, :], top[a][:, :], inv[:, :], ALU.mult)
            else:
                nc.vector.tensor_tensor(pick[:, :], top[1][:, :], top[0][:, :], ALU.subtract).then_inc(exp_in, 1)
                dve.wait_ge(exp_done, 1)
                settle(nc.vector.tensor_scalar(inv[:, :], total[:, :], 1.0, None, ALU.add))
                settle(nc.vector.reciprocal(weight[:, 0, :], inv[:, :]))
                settle(nc.vector.tensor_tensor(weight[:, 1, :], total[:, :], weight[:, 0, :], ALU.mult))
            nc.vector.tensor_tensor(labels[:, :, :], one[0][:, :, :], one[1][:, :, :], ALU.add).then_inc(labels_in, 1)
            dve.wait_ge(counted, 1)
            settle(nc.vector.tensor_copy(tile_sum[:, :, :], sum_ps))
            settle(nc.vector.tensor_tensor_scan(upto_tile[:, :, :].rearrange("p e t -> p (e t)"),
                                                carry[:, :, :].rearrange("p e t -> p (e t)"),
                                                tile_sum[:, :, :].rearrange("p e t -> p (e t)"), 0.0, ALU.mult, ALU.add))
            settle(nc.vector.tensor_tensor(place[:, :, :], upto_tile[:, :, :], tile_sum[:, :, :], ALU.subtract))
            settle(nc.vector.tensor_tensor(place[:, :, :], cum_ps, place[:, :, :], ALU.add))
            if capacity is None:
                settle(nc.vector.tensor_scalar(hit[:, 0, :], counts[:, 0:TT], float(P), None, ALU.mult))
                settle(nc.vector.tensor_tensor(cand[:, :, :], upto_tile[:, :, TT - 1:TT].broadcast_to(S),
                                               hit[:, 0:1, :].broadcast_to(S), ALU.is_gt))
                settle(nc.vector.tensor_reduce(tiles[:, :], cand[:, :, :], AX.X, ALU.add))
                settle(nc.vector.tensor_tensor_scan(end[:, :], ones_e[:, :], tiles[:, :], 0.0, ALU.mult, ALU.add))
                settle(nc.vector.tensor_tensor(base[:, :], end[:, :], tiles[:, :], ALU.subtract))
                settle(nc.vector.tensor_scalar(base[:, :], base[:, :], float(P), -1.0, ALU.mult, ALU.add))
                settle(nc.vector.tensor_tensor(place[:, :, :], place[:, :, :], to_tiles(base[:, :]), ALU.add))
                settle(nc.vector.tensor_tensor(at_tile[:, :, :],
                                               end[:, :].rearrange("p (a e) -> p a e", a=1).broadcast_to([P, NT, E]),
                                               counts[:, 0:NT].rearrange("p (t a) -> p t a", a=1).broadcast_to([P, NT, E]),
                                               ALU.is_le))
                settle(nc.vector.tensor_reduce(tile_no[:, :], at_tile[:, :, :], AX.X, ALU.add))
                settle(nc.vector.tensor_scalar(tile_expert[:, :], tile_no[:, :], float(E - 1), None, ALU.min))
            else:
                settle(nc.vector.tensor_scalar(hit[:, :, :], place[:, :, :], float(capacity), None, ALU.is_le))
                settle(nc.vector.tensor_scalar(cand[:, :, :], number[:, :, :], float(capacity), -1.0, ALU.mult, ALU.add))
                settle(nc.vector.tensor_tensor(place[:, :, :], place[:, :, :], cand[:, :, :], ALU.add))
                settle(nc.vector.tensor_tensor(place[:, :, :], place[:, :, :], hit[:, :, :], ALU.mult))
                settle(nc.vector.tensor_scalar(place[:, :, :], place[:, :, :], float(E * capacity), None, ALU.add))
            for a in range(2):
                settle(nc.vector.tensor_tensor(hit[:, :, :], one[a][:, :, :], place[:, :, :], ALU.mult))
                settle(nc.vector.tensor_reduce(where[:, a, :], over_experts(hit), AX.X, ALU.add))
            settle(nc.vector.tensor_copy(pos[:, :, :], where[:, :, :]))
            settle(nc.vector.tensor_scalar(bits[:, :, :], pos[:, :, :], P - 1, None, ALU.bitwise_and))
            settle(nc.vector.tensor_copy(slot[:, :, :], bits[:, :, :]))
            settle(nc.vector.tensor_scalar(bits[:, :, :], pos[:, :, :], 7, None, ALU.arith_shift_right))
            settle(nc.vector.tensor_copy(tile_of[:, :, :], bits[:, :, :]))
            with dve.Fori(0, BURSTS) as q:
                for r in range(RING):
                    t = (RING // 2) * q + r // 2
                    if r == 0:
                        dve.wait_ge(placed, RING * q)
                    nc.vector.tensor_scalar(in_slot[r][:, :], counts[:, :], slot[:, r % 2, bass.ds(t, 1)], None, ALU.is_equal)
                    nc.vector.tensor_scalar(in_tile[r][:, :], counts[:, 0:NT], tile_of[:, r % 2, bass.ds(t, 1)],
                                            tokens[:, bass.ds(t, 1)], ALU.is_equal, ALU.mult).then_inc(made, 1)
            dve.wait_ge(placed, 2 * TT + 1)
            settle(nc.vector.tensor_copy(table[:, :], table_ps[:, :]))


def experts_gelu(nc, x_d, wu, wd, w_in, ident, table, tile_expert, y_d):
    NT = table.shape[1]
    F = wu.shape[3]
    KF = F // P
    XS = 4
    with ExitStack() as ctx:
        m = Mem(nc, ctx, "gelu")
        row_no = [m.sb(f"row_no{i}", [P, 1], I32) for i in range(XS)]
        x = [m.sb(f"x{i}", [P, D]) for i in range(XS)]
        wu_part = [m.sb(f"wu_part{u}", [P, KD, E, F], F32R) for u in range(2)]
        xT = [[m.sb(f"xT{i}{u}", [P, D], F32R) for u in range(2)] for i in range(2)]
        h = [m.sb(f"h{i}", [P, F]) for i in range(2)]
        hT = [m.sb(f"hT{i}", [P, F]) for i in range(2)]
        y = [m.sb(f"y{i}", [P, D]) for i in range(2)]
        x_ps = m.ps("x_ps", [P, D])
        h_ps, t_ps, y_ps = ([m.ps(f"{a}_ps{i}", [P, n]) for i in range(2)] for a, n in (("h", F), ("t", F), ("y", D)))
        x_turned, xT_ready, h_done, h_ready, h_turned, hT_ready, y_done, y_ready, numbered = (m.sem(a) for a in (
            "x_turned", "xT_ready", "h_done", "h_ready", "h_turned", "hT_ready", "y_done", "y_ready", "numbered"))
        xT_high, wu_high, wu_low = m.sem("xT_high"), m.sem("wu_high"), m.sem("wu_low")
        wu_pieces = [(k, slice(e, e + E // 2)) for k in range(KD) for e in (0, E // 2)]
        x_in = [m.sem(f"x_in{i}") for i in range(XS)]
        y_out = [m.sem(f"y_out{i}") for i in range(2)]
        passed = m.sem("passed")
        block = ctx.enter_context(nc.Block())

        @block.sync
        def _(sp):
            with sp.Fori(0, NT // 2) as i:
                for s in range(2):
                    n = 2 * i + s
                    sp.wait_ge(y_ready, n + 1)
                    sp.dma_start(y_d[bass.ds(n * P, P), :], y[s][:, :]).then_inc(y_out[s], 16)
            for s in range(2):
                sp.wait_ge(y_out[s], 16 * NT // 2)

        @block.gpsimd
        def _(pool):
            with pool.Fori(0, NT // XS) as i:
                for s in range(XS):
                    n = XS * i + s
                    pool.wait_ge(x_in[s], 16 * i)
                    nc.gpsimd.tensor_copy(row_no[s][:, :], table[:, bass.ds(n, 1)]).then_inc(numbered, 1)
                for s in range(XS):
                    n = XS * i + s
                    pool.wait_ge(numbered, n + 1)
                    pool.wait_ge(x_turned, XS * i)
                    pool.sem_inc(passed, 1)
                    nc.gpsimd.indirect_dma_start(out=x[s][:, :], out_offset=None, in_=x_d,
                                                 in_offset=bass.IndirectOffsetOnAxis(ap=row_no[s][:, 0:1], axis=0)
                                                 ).then_inc(x_in[s], 16)

        @block.tensor
        def _(pe):
            def turn_x(n, s):
                pe.wait_ge(x_in[s], 16 * (n // XS + 1))
                pe.wait_ge(xT_ready, n)
                for k in range(KD):
                    mm = nc.tensor.transpose(x_ps[:, k * P:(k + 1) * P], x[s][:, k * P:(k + 1) * P], ident[:, :])
                mm.then_inc(x_turned, 1)

            def up(n, s):
                e = pe.value_load(tile_expert[0:1, bass.ds(n, 1)], min_val=0, max_val=E - 1)
                pe.wait_ge(xT_ready, n + 1)
                if not isinstance(n, int) or n > 1:
                    pe.wait_ge(h_ready, n - 1)
                for i, (k, (xp, wp)) in enumerate((k, t) for k in range(KD) for t in TERMS):
                    mm = nc.tensor.matmul(h_ps[s][:, :], xT[s][xp][:, k * P:(k + 1) * P],
                                          wu_part[wp][:, k, bass.ds(e, 1), :].rearrange("p e f -> p (e f)"),
                                          start=(i == 0), stop=(i == 3 * KD - 1))
                mm.then_inc(h_done, 1)

            def turn_h(n, s):
                pe.wait_ge(h_ready, n + 1)
                for k in range(KF):
                    mm = nc.tensor.transpose(t_ps[s][:, k * P:(k + 1) * P], h[s][:, k * P:(k + 1) * P], ident[:, :])
                mm.then_inc(h_turned, 1)

            def down(n, s):
                e = pe.value_load(tile_expert[0:1, bass.ds(n, 1)], min_val=0, max_val=E - 1)
                pe.wait_ge(hT_ready, n + 1)
                if not isinstance(n, int) or n > 1:
                    pe.wait_ge(y_ready, n - 1)
                for k in range(KF):
                    mm = nc.tensor.matmul(y_ps[s][:, :], hT[s][:, k * P:(k + 1) * P],
                                          wd[:, k, bass.ds(e, 1), :].rearrange("p e f -> p (e f)"),
                                          start=(k == 0), stop=(k == KF - 1))
                mm.then_inc(y_done, 1)

            def one(n, s):
                turn_h(n, s % 2)
                if not (isinstance(n, int) and n + 1 >= NT):
                    up(n + 1, (s + 1) % 2)
                if not (isinstance(n, int) and n + 2 >= NT):
                    turn_x(n + 2, (s + 2) % XS)
                down(n, s % 2)

            pe.wait_ge(w_in, 16 * (KD + KF))
            turn_x(0, 0)
            turn_x(1, 1)
            pe.wait_ge(wu_low, len(wu_pieces))
            up(0, 0)
            one(0, 0)
            one(1, 1)
            one(2, 2)
            one(3, 3)
            with pe.Fori(1, NT // XS - 1) as i:
                for s in range(XS):
                    one(XS * i + s, s)
            for s in range(XS):
                one(NT - XS + s, s)

        @block.scalar
        def _(act):
            act.wait_ge(w_in, 16 * (KD + KF))
            for k, es in wu_pieces:
                nc.scalar.copy(wu_part[0][:, k, es, :], wu[:, k, es, :]).then_inc(wu_high, 1)
            with act.Fori(0, NT // 2) as i:
                for s in range(2):
                    n = 2 * i + s
                    act.wait_ge(h_done, n + 1)
                    act.wait_ge(h_turned, 2 * i)
                    nc.scalar.activation(h[s][:, :], h_ps[s][:, :], ACT.Gelu).then_inc(h_ready, 1)
                    act.wait_ge(h_turned, n + 1)
                    act.wait_ge(y_done, 2 * i)
                    nc.scalar.copy(hT[s][:, :], t_ps[s][:, :]).then_inc(hT_ready, 1)

        @block.vector
        def _(dve):
            def take_x(n, s):
                dve.wait_ge(x_turned, n + 1)
                if not isinstance(n, int) or n > 1:
                    dve.wait_ge(h_done, n - 1)
                nc.vector.tensor_copy(xT[s][0][:, :], x_ps[:, :]).then_inc(xT_high, 1)
                dve.wait_ge(xT_high, n + 1)
                nc.vector.tensor_tensor(xT[s][1][:, :], x_ps[:, :], xT[s][0][:, :].bitcast(F32),
                                        ALU.subtract).then_inc(xT_ready, 1)

            def take_y(n, s):
                dve.wait_ge(y_done, n + 1)
                dve.wait_ge(y_out[s], 16 * (n // 2))
                nc.vector.tensor_copy(y[s][:, :], y_ps[s][:, :]).then_inc(y_ready, 1)

            for i, (k, es) in enumerate(wu_pieces):
                dve.wait_ge(wu_high, i + 1)
                nc.vector.tensor_tensor(wu_part[1][:, k, es, :], wu[:, k, es, :], wu_part[0][:, k, es, :].bitcast(F32),
                                        ALU.subtract).then_inc(wu_low, 1)
            take_x(0, 0)
            take_x(1, 1)
            with dve.Fori(0, NT // 2 - 1) as i:
                for s in range(2):
                    take_x(2 * i + s + 2, s)
                    take_y(2 * i + s, s)
            for s in range(2):
                take_y(NT - 2 + s, s)


def load_expert(sp, e, s, W1, W2, W3, w12, w3, w_in):
    ex = bass.ds(e, 1)
    for a, W in enumerate((W1, W2)):
        sp.dma_start(w12[s][:, a, :, :], W[ex].rearrange("e (k p) f -> p (e k) f", p=P)).then_inc(w_in[s], 16)
    sp.dma_start(w3[s][:, :, :], W3[ex].rearrange("e (k p) f -> p (e k) f", p=P)).then_inc(w_in[s], 16)


def experts_silu(nc, x_d, W1, W2, W3, w12, w3, w_in, ident, table, capacity, y_d):
    NT = table.shape[1]
    F = W1.shape[2]
    KF = F // P
    CT = capacity // P
    HALF = capacity // 2
    AHEAD, RING = 2, 4
    with ExitStack() as ctx:
        m = Mem(nc, ctx, "silu")
        w12_part = [[m.sb(f"w12_part{i}{j}", [P, 2, KD, P], F32R) for j in range(2)] for i in range(RING)]
        w3_part = [m.sb(f"w3_part{j}", [P, KF, D], F32R) for j in range(2)]
        row_no = m.sb("row_no", [P, CT], I32)
        x = [m.sb(f"x{i}", [P, CT, D]) for i in range(2)]
        xT = [[m.sb(f"xT{i}{j}", [P, KD, capacity], F32R) for j in range(2)] for i in range(2)]
        gate = [m.sb(f"gate{i}", [P, HALF]) for i in range(2)]
        h = [m.sb(f"h{i}", [P, HALF]) for i in range(2)]
        h_part = [m.sb(f"h_part{j}", [P, KF, capacity], F32R) for j in range(2)]
        y = [m.sb(f"y{i}", [P, D]) for i in range(2)]
        zero = m.sb("zero", [1, D])
        x_ps = [m.ps(f"x_ps{i}", [P, KD, P]) for i in range(2)]
        h_ps = [[m.ps(f"h_ps{i}{a}", [P, HALF]) for a in range(2)] for i in range(2)]
        y_ps = [m.ps(f"y_ps{i}", [P, D]) for i in range(2)]
        x_turned, x_high, x_low, h_done, gated, h_ready, h_high, h_low, y_done, y_ready, numbered, zeroed = (m.sem(a) for a in (
            "x_turned", "x_high", "x_low", "h_done", "gated", "h_ready", "h_high", "h_low", "y_done", "y_ready",
            "numbered", "zeroed"))
        w12_high, w12_low, w3_high, w3_low = (m.sem(a) for a in ("w12_high", "w12_low", "w3_high", "w3_low"))
        x_in = [m.sem(f"x_in{i}") for i in range(2)]
        y_out, zero_out = [m.sem(f"y_out{i}") for i in range(2)], m.sem("zero_out")
        UNITS = 2 * KF
        passed = m.sem("passed")
        block = ctx.enter_context(nc.Block())

        def experts(eng, work):
            work(0, 0, True)
            with eng.Fori(0, E // 2 - 1) as i:
                work(2 * i + 1, 1, True)
                work(2 * i + 2, 0, True)
            work(E - 1, 1, False)

        def ahead(e, s, f, more):
            if f + AHEAD < KF:
                return e, s, f + AHEAD
            return (e + 1, 1 - s, f + AHEAD - KF) if more else None

        @block.sync
        def _(sp):
            def store(e, s):
                for j in range(CT):
                    sp.wait_ge(y_ready, CT * e + j + 1)
                    b = (s + j) % 2
                    sp.dma_start(y_d[bass.ds((CT * e + j) * P, P), :], y[b][:, :]).then_inc(y_out[b], 16)

            with sp.Fori(0, E // 2 - 1) as i:
                for s in range(2):
                    store(2 * i + s, s)
                    load_expert(sp, 2 * i + s + 2, s, W1, W2, W3, w12, w3, w_in)
            for s in range(2):
                store(E - 2 + s, s)
            for b in range(2):
                sp.wait_ge(y_out[b], 16 * NT // 2)

        @block.gpsimd
        def _(pool):
            nc.gpsimd.memset(zero[:, :], 0.0).then_inc(zeroed, 1)
            pool.wait_ge(zeroed, 1)
            pool.dma_start(y_d[NT * P:NT * P + 1, :], zero[:, :]).then_inc(zero_out, 16)
            with pool.Fori(0, E // 2) as i:
                for s in range(2):
                    e = 2 * i + s
                    pool.wait_ge(x_in[1 - s], 16 * CT * (i + s))
                    nc.gpsimd.tensor_copy(row_no[:, :], table[:, bass.ds(e * CT, CT)]).then_inc(numbered, 1)
                    pool.wait_ge(numbered, e + 1)
                    pool.wait_ge(x_turned, CT * 2 * i)
                    pool.sem_inc(passed, 1)
                    for j in range(CT):
                        nc.gpsimd.indirect_dma_start(out=x[s][:, j, :], out_offset=None, in_=x_d,
                                                     in_offset=bass.IndirectOffsetOnAxis(ap=row_no[:, j:j + 1], axis=0)
                                                     ).then_inc(x_in[s], 16)
            pool.wait_ge(zero_out, 16)

        @block.tensor
        def _(pe):
            def turn(e, s, j):
                if j == 0:
                    pe.wait_ge(x_in[s], 16 * CT * (e // 2 + 1))
                if beyond(e, 0) or j > 1:
                    pe.wait_ge(x_low, CT * e + j - 1)
                for k in range(KD):
                    mm = nc.tensor.transpose(x_ps[(s + j) % 2][:, k, :], x[s][:, j, k * P:(k + 1) * P], ident[:, :])
                mm.then_inc(x_turned, 1)

            def up(e, s, f):
                if f == 0:
                    pe.wait_ge(x_low, CT * (e + 1))
                pe.wait_ge(w12_low, KF * e + f + 1)
                for u in (2 * f, 2 * f + 1):
                    rows = slice(u % 2 * HALF, (u % 2 + 1) * HALF)
                    if beyond(e, 0) or u > 1:
                        pe.wait_ge(h_ready, UNITS * e + u - 1)
                    for a in range(2):
                        for i, (k, (wp, xp)) in enumerate((k, t) for k in range(KD) for t in TERMS):
                            mm = nc.tensor.matmul(h_ps[u % 2][a][:, :], w12_part[f % RING][wp][:, a, k, :],
                                                  xT[s][xp][:, k, rows], start=(i == 0), stop=(i == 3 * KD - 1))
                    mm.then_inc(h_done, 1)

            def down(e, s):
                pe.wait_ge(w3_low, KF * (e + 1))
                pe.wait_ge(h_low, UNITS * (e + 1))
                for j in range(CT):
                    if beyond(e, 0) or j > 1:
                        pe.wait_ge(y_ready, CT * e + j - 1)
                    for i, (f, (hp, wp)) in enumerate((f, t) for f in range(KF) for t in TERMS):
                        mm = nc.tensor.matmul(y_ps[(s + j) % 2][:, :], h_part[hp][:, f, j * P:(j + 1) * P], w3_part[wp][:, f, :],
                                              start=(i == 0), stop=(i == 3 * KF - 1))
                    mm.then_inc(y_done, 1)

            def work(e, s, more):
                for f in range(1, KF):
                    up(e, s, f)
                    if more and f <= CT:
                        turn(e + 1, 1 - s, f - 1)
                if more:
                    up(e + 1, 1 - s, 0)
                down(e, s)

            for j in range(CT):
                turn(0, 0, j)
            up(0, 0, 0)
            experts(pe, work)

        @block.scalar
        def _(act):
            def high_w12(e, s, f):
                if f == 0:
                    act.wait_ge(w_in[s], 48 * (e // 2 + 1))
                if beyond(e, 0) or f >= RING:
                    act.wait_ge(h_done, 2 * (KF * e + f - RING + 1))
                nc.scalar.copy(w12_part[f % RING][0][:, :, :, :], w12[s][:, :, :, f * P:(f + 1) * P]).then_inc(w12_high, 1)

            def high_x(e, s, j):
                if j == 0 and beyond(e, 1):
                    act.wait_ge(h_done, UNITS * (e - 1))
                act.wait_ge(x_turned, CT * e + j + 1)
                nc.scalar.copy(xT[s][0][:, :, j * P:(j + 1) * P], x_ps[(s + j) % 2][:, :, :]).then_inc(x_high, 1)

            def front(e, s, f, more):
                if coming := ahead(e, s, f, more):
                    high_w12(*coming)
                for half in range(2):
                    u = 2 * f + half
                    act.wait_ge(h_done, UNITS * e + u + 1)
                    if beyond(e, 0) or u > 1:
                        act.wait_ge(h_ready, UNITS * e + u - 1)
                    nc.scalar.activation(gate[half][:, :], h_ps[half][0][:, :], ACT.Silu).then_inc(gated, 1)

            def back(e, s, f):
                if f == 0 and beyond(e, 0):
                    act.wait_ge(y_done, CT * e)
                nc.scalar.copy(w3_part[0][:, f, :], w3[s][:, f, :]).then_inc(w3_high, 1)
                for half in range(2):
                    act.wait_ge(h_ready, UNITS * e + 2 * f + half + 1)
                    nc.scalar.copy(h_part[0][:, f, half * HALF:(half + 1) * HALF], h[half][:, :]).then_inc(h_high, 1)

            def work(e, s, more):
                back(e, s, 0)
                for f in range(1, KF):
                    front(e, s, f, more)
                    back(e, s, f)
                    if more and f <= CT:
                        high_x(e + 1, 1 - s, f - 1)
                if more:
                    front(e + 1, 1 - s, 0, True)

            for f in range(AHEAD):
                high_w12(0, 0, f)
            for j in range(CT):
                high_x(0, 0, j)
            front(0, 0, 0, True)
            experts(act, work)

        @block.vector
        def _(dve):
            def low_w12(e, s, f):
                dve.wait_ge(w12_high, KF * e + f + 1)
                high, low = (w12_part[f % RING][j][:, :, :, :] for j in range(2))
                nc.vector.tensor_tensor(low, w12[s][:, :, :, f * P:(f + 1) * P], high.bitcast(F32),
                                        ALU.subtract).then_inc(w12_low, 1)

            def low_x(e, s, j):
                dve.wait_ge(x_high, CT * e + j + 1)
                cols = slice(j * P, (j + 1) * P)
                nc.vector.tensor_tensor(xT[s][1][:, :, cols], x_ps[(s + j) % 2][:, :, :], xT[s][0][:, :, cols].bitcast(F32),
                                        ALU.subtract).then_inc(x_low, 1)

            def front(e, s, f, more):
                if coming := ahead(e, s, f, more):
                    low_w12(*coming)
                for half in range(2):
                    u = 2 * f + half
                    dve.wait_ge(gated, UNITS * e + u + 1)
                    if beyond(e, 0) or u > 1:
                        dve.wait_ge(h_low, UNITS * e + u - 1)
                    nc.vector.tensor_tensor(h[half][:, :], gate[half][:, :], h_ps[half][1][:, :], ALU.mult).then_inc(h_ready, 1)

            def back(e, s, f):
                dve.wait_ge(w3_high, KF * e + f + 1)
                nc.vector.tensor_tensor(w3_part[1][:, f, :], w3[s][:, f, :], w3_part[0][:, f, :].bitcast(F32),
                                        ALU.subtract).then_inc(w3_low, 1)
                for half in range(2):
                    dve.wait_ge(h_high, UNITS * e + 2 * f + half + 1)
                    rows = slice(half * HALF, (half + 1) * HALF)
                    nc.vector.tensor_tensor(h_part[1][:, f, rows], h[half][:, :], h_part[0][:, f, rows].bitcast(F32),
                                            ALU.subtract).then_inc(h_low, 1)

            def work(e, s, more):
                back(e, s, 0)
                for f in range(1, KF):
                    front(e, s, f, more)
                    back(e, s, f)
                    if more and f <= CT:
                        low_x(e + 1, 1 - s, f - 1)
                if more:
                    front(e + 1, 1 - s, 0, True)
                for j in range(CT):
                    b = (s + j) % 2
                    dve.wait_ge(y_done, CT * e + j + 1)
                    if beyond(e, 0) or j > 1:
                        dve.wait_ge(y_out[b], 16 * ((CT * e + j) // 2))
                    nc.vector.tensor_copy(y[b][:, :], y_ps[b][:, :]).then_inc(y_ready, 1)

            for f in range(AHEAD):
                low_w12(0, 0, f)
            for j in range(CT):
                low_x(0, 0, j)
            front(0, 0, 0, True)
            experts(dve, work)


def mix_tokens(nc, part_d, y_d, pos, weight, ident, WkT, WvT, WrT, WoT, decay, first_share, scale, x, nT2):
    with ExitStack() as ctx:
        m = Mem(nc, ctx, "mix")
        w = m.sb("w", [P, 3, KD, D])
        wo = m.sb("wo", [P, KD, D])
        scale_row = m.sb("scale_row", [P, D])
        td, tf, e1, ew, eu = (m.sb(a, [P, KD]) for a in ("td", "tf", "e1", "ew", "eu"))
        base = [m.sb(f"base{i}", [P, GT, D]) for i in range(2)]
        y = [m.sb(f"y{i}", [P, GT, 2, D]) for i in range(2)]
        row_no = [m.sb(f"row_no{i}", [P, 2, GT], I32) for i in range(2)]
        part = [m.sb(f"part{i}", [P, GT, 6]) for i in range(2)]
        mean_var = [m.sb(f"mean_var{i}", [P, GT, 2]) for i in range(2)]
        std, inv, q1, q, root1, inv1, both_inv, total, root2, inv2 = (
            [m.sb(f"{a}{i}", [P, GT]) for i in range(2)]
            for a in ("std", "inv", "q1", "q", "root1", "inv1", "both_inv", "total", "root2", "inv2"))
        x2 = [m.sb(f"x2{i}", [P, GT, D]) for i in range(2)]
        square = [m.sb(f"square{i}", [P, D]) for i in range(2)]
        n1 = [m.sb(f"n1{i}", [P, GT, D]) for i in range(2)]
        n2 = [m.sb(f"n2{i}", [P, GT, D]) for i in range(2)]
        nT = [m.sb(f"nT{i}", [P, KD, GRP]) for i in range(2)]
        eps = m.sb("eps", [P, 2])
        k_sb, r_sb, kv, wkv = ([m.sb(f"{a}{c}", [P, GRP]) for c in range(KD)] for a in ("k_sb", "r_sb", "kv", "wkv"))
        state = [m.sb(f"state{c}", [P, GRP + 1]) for c in range(KD)]
        last = [m.sb(f"last{c}", [P, 1]) for c in range(KD)]
        z = [m.sb(f"z{i}", [P, KD, GRP]) for i in range(2)]
        k_ps, r_ps = m.ps("k_ps", [P, GRP]), m.ps("r_ps", [P, GRP])
        v_ps = [m.ps(f"v_ps{c}", [P, GRP]) for c in range(KD)]
        o_ps = [m.ps(f"o_ps{i}", [P, D]) for i in range(2)]
        turn1_ps, turn2_ps = m.ps("turn1_ps", [P, GRP]), m.ps("turn2_ps", [P, GRP])
        w_in, wo_ready, e1_done, shares_done, k_done, v_done, r_done, k_copied, r_ready = (m.sem(a) for a in (
            "w_in", "wo_ready", "e1_done", "shares_done", "k_done", "v_done", "r_done", "k_copied", "r_ready"))
        carried, kept, kv_done, scanned, wkv_done, z_done, o_done, added = (m.sem(a) for a in (
            "carried", "kept", "kv_done", "scanned", "wkv_done", "z_done", "o_done", "added"))
        first, summed, numbered, passed, eps_set, parted, aggregated, std_done, inv_done, q1_done, q_done = (m.sem(a) for a in (
            "first", "summed", "numbered", "passed", "eps_set", "parted", "aggregated", "std_done", "inv_done", "q1_done", "q_done"))
        normed, root1_done, inv1_done, both_done, n1_done, turned1, copied1 = (m.sem(a) for a in (
            "normed", "root1_done", "inv1_done", "both_done", "n1_done", "turned1", "copied1"))
        squared, root2_done, inv2_done, n2_done, turned2, copied2 = (m.sem(a) for a in (
            "squared", "root2_done", "inv2_done", "n2_done", "turned2", "copied2"))
        paired = m.sem("paired")
        base_in, y_in = ([m.sem(f"{a}{i}") for i in range(2)] for a in ("base_in", "y_in"))
        NW = 16 * (5 + 2 * KD)
        block = ctx.enter_context(nc.Block())

        def tile(a, g, j):
            return a[:, bass.ds(g * GT + j, 1), :].rearrange("p a d -> p (a d)")

        @block.sync
        def _(sp):
            for i, a in enumerate((WkT, WvT, WrT)):
                sp.dma_start(w[:, i], a.rearrange("(k p) n -> p k n", p=P)).then_inc(w_in, 16)
            sp.dma_start(wo[:, :, :], WoT.rearrange("(k p) n -> p k n", p=P)).then_inc(w_in, 16)
            sp.dma_start(scale_row[:, :], row(scale).broadcast_to([P, D])).then_inc(w_in, 16)
            for k in range(KD):
                for a, b in ((td, decay), (tf, first_share)):
                    sp.dma_start(a[:, k:k + 1], b[k * P:(k + 1) * P].rearrange("(p a) -> p a", a=1)).then_inc(w_in, 16)

            def step(g, s):
                if beyond(g, 1):
                    sp.wait_ge(n1_done, GT * (g - 1))
                sp.dma_start(base[s][:, :, :], token_rows(part_d, g)).then_inc(base_in[s], 16)

            skewed(sp, 0, 0, step)

        @block.gpsimd
        def _(pool):
            def step(g, s):
                if exists(g + 2):
                    gather_pairs(nc, pool, g + 2, s, pos, y_d, y, row_no, y_in, numbered, summed, passed)
                if exists(g - 1):
                    for j in range(GT):
                        pool.wait_ge(added, GT * (g - 1) + j + 1)
                        nc.gpsimd.tensor_tensor(tile(x, g - 1, j), tile(x, g - 1, j), x2[1 - s][:, j, :],
                                                ALU.add).then_inc(paired, 1)

            skewed(pool, -2, 1, step)

        @block.tensor
        def _(pe):
            def turn1(g, s):
                pe.wait_ge(n1_done, GT * (g + 1))
                for k in range(KD):
                    pe.wait_ge(copied1, KD * g + k)
                    for j in range(GT):
                        mm = nc.tensor.transpose(turn1_ps[:, j * P:(j + 1) * P], n1[s][:, j, k * P:(k + 1) * P], ident[:, :])
                    mm.then_inc(turned1, 1)

            def turn2(g, s):
                pe.wait_ge(n2_done, GT * (g + 1))
                for k in range(KD):
                    pe.wait_ge(copied2, KD * g + k)
                    for j in range(GT):
                        mm = nc.tensor.transpose(turn2_ps[:, j * P:(j + 1) * P], n2[s][:, j, k * P:(k + 1) * P], ident[:, :])
                    mm.then_inc(turned2, 1)

            def project(g, s):
                pe.wait_ge(copied1, KD * (g + 1))
                for c in range(KD):
                    for i, (bank, done, used) in enumerate(((k_ps, k_done, k_copied), (v_ps[c], v_done, kv_done), (r_ps, r_done, r_ready))):
                        if i != 1:
                            pe.wait_ge(used, KD * g + c)
                        elif beyond(g, 0):
                            pe.wait_ge(used, KD * (g - 1) + c + 1)
                        for k in range(KD):
                            mm = nc.tensor.matmul(bank[:, :], w[:, i, k, c * P:(c + 1) * P], nT[s][:, k, :],
                                                  start=(k == 0), stop=(k == KD - 1))
                        mm.then_inc(done, 1)

            def mix(g, s):
                pe.wait_ge(z_done, KD * (g + 1))
                for j in range(GT):
                    if beyond(g, 0) or j > 1:
                        pe.wait_ge(added, GT * g + j - 1)
                    for k in range(KD):
                        mm = nc.tensor.matmul(o_ps[j % 2][:, :], z[s][:, k, j * P:(j + 1) * P], wo[:, k, :],
                                              start=(k == 0), stop=(k == KD - 1))
                    mm.then_inc(o_done, 1)

            def step(g, s):
                if exists(g + 1):
                    project(g + 1, 1 - s)
                if exists(g + 2):
                    turn1(g + 2, s)
                if exists(g - 1):
                    turn2(g - 1, 1 - s)
                if exists(g):
                    mix(g, s)

            pe.wait_ge(w_in, NW)
            pe.wait_ge(wo_ready, 1)
            skewed(pe, -2, 1, step)

        @block.scalar
        def _(act):
            act.wait_ge(w_in, NW)
            nc.scalar.activation(e1[:, :], td[:, :], ACT.Exp).then_inc(e1_done, 1)
            nc.scalar.activation(eu[:, :], tf[:, :], ACT.Exp)
            act.wait_ge(e1_done, 1)
            nc.scalar.activation(ew[:, :], e1[:, :], ACT.Exp, scale=-1.0).then_inc(shares_done, 1)
            act.wait_ge(eps_set, 1)

            def deviation(g, s):
                act.wait_ge(aggregated, GT * (g + 1))
                nc.scalar.activation(std[s][:, :], mean_var[s][:, :, 1:2].rearrange("p g a -> p (g a)"), ACT.Sqrt,
                                     bias=eps[:, 0:1]).then_inc(std_done, 1)

            def size1(g, s):
                act.wait_ge(q_done, g + 1)
                nc.scalar.activation(root1[s][:, :], q[s][:, :], ACT.Sqrt, bias=eps[:, 1:2]).then_inc(root1_done, 1)

            def squares2(g, s):
                if beyond(g, 1):
                    act.wait_ge(root2_done, g - 1)
                for j in range(GT):
                    act.wait_ge(added, GT * g + j + 1)
                    if beyond(g, 0) or j > 1:
                        act.wait_ge(squared, GT * g + j - 1)
                    nc.scalar.activation(square[j % 2][:, :], x2[s][:, j, :], ACT.Square,
                                         accum_out=total[s][:, j:j + 1]).then_inc(squared, 1)

            def size2(g, s):
                act.wait_ge(squared, GT * (g + 1))
                nc.scalar.activation(root2[s][:, :], total[s][:, :], ACT.Sqrt, bias=eps[:, 1:2],
                                     scale=1.0 / D).then_inc(root2_done, 1)

            def copy1(g, s):
                if beyond(g, 1):
                    act.wait_ge(r_done, KD * (g - 1))
                for k in range(KD):
                    act.wait_ge(turned1, KD * g + k + 1)
                    nc.scalar.copy(nT[s][:, k, :], turn1_ps[:, :]).then_inc(copied1, 1)

            def copy2(g, s):
                for k in range(KD):
                    act.wait_ge(turned2, KD * g + k + 1)
                    nc.scalar.copy(nT2[:, k, bass.ds(g * GRP, GRP)], turn2_ps[:, :]).then_inc(copied2, 1)

            def key(g, c):
                act.wait_ge(k_done, KD * g + c + 1)
                if beyond(g, 0):
                    act.wait_ge(kv_done, KD * (g - 1) + c + 1)
                nc.scalar.copy(k_sb[c][:, :], k_ps[:, :]).then_inc(k_copied, 1)

            def gate(g, c):
                act.wait_ge(r_done, KD * g + c + 1)
                if beyond(g, 0):
                    act.wait_ge(z_done, KD * (g - 1) + c + 1)
                nc.scalar.activation(r_sb[c][:, :], r_ps[:, :], ACT.Sigmoid).then_inc(r_ready, 1)

            def step(g, s):
                if exists(g + 1):
                    key(g + 1, 0)
                if exists(g - 1):
                    size2(g - 1, 1 - s)
                if exists(g + 2):
                    deviation(g + 2, s)
                    size1(g + 2, s)
                if exists(g + 1):
                    gate(g + 1, 0)
                    for c in range(1, KD):
                        key(g + 1, c)
                        gate(g + 1, c)
                if exists(g + 2):
                    copy1(g + 2, s)
                if exists(g - 1):
                    copy2(g - 1, 1 - s)
                if exists(g):
                    squares2(g, s)

            skewed(act, -2, 1, step)

        @block.vector
        def _(dve):
            nc.vector.memset(eps[:, 0:1], LN_EPS)
            nc.vector.memset(eps[:, 1:2], RMS_EPS).then_inc(eps_set, 1)
            for c in range(KD):
                nc.vector.memset(last[c][:, :], 0.0).then_inc(kept, 1)
            dve.wait_ge(w_in, NW)
            nc.vector.tensor_tensor(wo[:, :, :], wo[:, :, :],
                                    scale_row[:, :].rearrange("p (a d) -> p a d", a=1).broadcast_to([P, KD, D]),
                                    ALU.mult).then_inc(wo_ready, 1)
            dve.wait_ge(shares_done, 1)

            def stats(g, s):
                dve.wait_ge(summed, GT * (g + 1))
                for j in range(GT):
                    nc.vector.bn_stats(part[s][:, j, :], base[s][:, j, :]).then_inc(parted, 1)
                dve.wait_ge(parted, GT * (g + 1))
                dve.sem_inc(passed, 1)
                for j in range(GT):
                    nc.vector.bn_aggr(mean_var[s][:, j, :], part[s][:, j, :]).then_inc(aggregated, 1)

            def norms(g, s):
                dve.wait_ge(std_done, g + 1)
                nc.vector.reciprocal(inv[s][:, :], std[s][:, :]).then_inc(inv_done, 1)
                dve.wait_ge(inv_done, g + 1)
                var = mean_var[s][:, :, 1:2].rearrange("p g a -> p (g a)")
                nc.vector.tensor_tensor(q1[s][:, :], var, inv[s][:, :], ALU.mult).then_inc(q1_done, 1)
                dve.wait_ge(q1_done, g + 1)
                nc.vector.tensor_tensor(q[s][:, :], q1[s][:, :], inv[s][:, :], ALU.mult).then_inc(q_done, 1)
                for j in range(GT):
                    nc.vector.tensor_scalar(tile(x, g, j), base[s][:, j, :], mean_var[s][:, j, 0:1],
                                            inv[s][:, j:j + 1], ALU.subtract, ALU.mult).then_inc(normed, 1)
                dve.wait_ge(root1_done, g + 1)
                nc.vector.reciprocal(inv1[s][:, :], root1[s][:, :]).then_inc(inv1_done, 1)
                dve.wait_ge(inv1_done, g + 1)
                nc.vector.tensor_tensor(both_inv[s][:, :], inv1[s][:, :], inv[s][:, :], ALU.mult).then_inc(both_done, 1)
                dve.wait_ge(both_done, g + 1)
                if beyond(g, 1):
                    dve.wait_ge(turned1, KD * (g - 1))
                for j in range(GT):
                    nc.vector.tensor_scalar(n1[s][:, j, :], base[s][:, j, :], mean_var[s][:, j, 0:1],
                                            both_inv[s][:, j:j + 1], ALU.subtract, ALU.mult).then_inc(n1_done, 1)

            def scan(g, s):
                for c in range(KD):
                    n = KD * g + c + 1
                    dve.wait_ge(k_copied, n)
                    dve.wait_ge(v_done, n)
                    nc.vector.tensor_tensor(kv[c][:, :], k_sb[c][:, :], v_ps[c][:, :], ALU.mult).then_inc(kv_done, 1)
                    dve.wait_ge(kept, n)
                    nc.vector.tensor_copy(state[c][:, 0:1], last[c][:, :]).then_inc(carried, 1)
                    dve.wait_ge(kv_done, n)
                    dve.wait_ge(carried, n)
                    nc.vector.tensor_tensor_scan(state[c][:, 1:GRP + 1], ew[:, c:c + 1].broadcast_to([P, GRP]), kv[c][:, :],
                                                 state[c][:, 0:1], ALU.mult, ALU.add).then_inc(scanned, 1)
                for c in range(KD):
                    n = KD * g + c + 1
                    dve.wait_ge(scanned, n)
                    nc.vector.scalar_tensor_tensor(wkv[c][:, :], kv[c][:, :], eu[:, c:c + 1], state[c][:, 0:GRP],
                                                   ALU.mult, ALU.add).then_inc(wkv_done, 1)
                    nc.vector.tensor_copy(last[c][:, :], state[c][:, GRP:GRP + 1]).then_inc(kept, 1)
                if beyond(g, 1):
                    dve.wait_ge(o_done, GT * (g - 1))
                for c in range(KD):
                    n = KD * g + c + 1
                    dve.wait_ge(r_ready, n)
                    dve.wait_ge(wkv_done, n)
                    nc.vector.tensor_tensor(z[s][:, c, :], wkv[c][:, :], r_sb[c][:, :], ALU.mult).then_inc(z_done, 1)

            def add(g, s):
                dve.wait_ge(normed, GT * (g + 1))
                if beyond(g, 1):
                    for used in (squared, paired, n2_done):
                        dve.wait_ge(used, GT * (g - 1))
                for j in range(GT):
                    dve.wait_ge(o_done, GT * g + j + 1)
                    nc.vector.tensor_tensor(x2[s][:, j, :], o_ps[j % 2][:, :], tile(x, g, j), ALU.add).then_inc(added, 1)

            def scale2(g, s):
                dve.wait_ge(root2_done, g + 1)
                nc.vector.reciprocal(inv2[s][:, :], root2[s][:, :]).then_inc(inv2_done, 1)
                dve.wait_ge(inv2_done, g + 1)
                if beyond(g, 1):
                    dve.wait_ge(turned2, KD * (g - 1))
                for j in range(GT):
                    nc.vector.tensor_scalar(n2[s][:, j, :], x2[s][:, j, :], inv2[s][:, j:j + 1], None, ALU.mult).then_inc(n2_done, 1)

            def step(g, s):
                if exists(g + 2):
                    add_pairs(nc, dve, g + 2, s, weight, base, y, base_in, y_in, first, summed)
                    stats(g + 2, s)
                    norms(g + 2, s)
                if exists(g - 1):
                    scale2(g - 1, 1 - s)
                if exists(g + 1):
                    scan(g + 1, 1 - s)
                if exists(g):
                    add(g, s)

            skewed(dve, -2, 1, step)


def mix_channels(nc, nT, x, WfcT, WmlpT, scale, ident, out_d):
    F = WfcT.shape[1]
    KF = F // P
    with ExitStack() as ctx:
        m = Mem(nc, ctx, "mlp")
        wf = m.sb("wf", [P, KD, F])
        wm = m.sb("wm", [P, KF, D])
        scale_row = m.sb("scale_row", [P, D])
        out = [m.sb(f"out{i}", [P, GT, D]) for i in range(2)]
        half = [m.sb(f"half{i}", [P, GRP]) for i in range(2)]
        leaky = [m.sb(f"leaky{i}", [P, GRP]) for i in range(2)]
        wf_part = [m.sb(f"wf_part{j}", [P, KD, F], F32R) for j in range(2)]
        wm_part = [m.sb(f"wm_part{j}", [P, KF, D], F32R) for j in range(2)]
        n_part = [[m.sb(f"n_part{i}{j}", [P, KD, GRP], F32R) for j in range(2)] for i in range(2)]
        h = [m.sb(f"h{i}", [P, GRP]) for i in range(4)]
        h_part = [m.sb(f"h_part{j}", [P, KF, GRP], F32R) for j in range(2)]
        h_ps = [m.ps(f"h_ps{i}", [P, GRP]) for i in range(4)]
        w_high, w_low, n_high, n_low, h_high, h_low = (m.sem(a) for a in (
            "w_high", "w_low", "n_high", "n_low", "h_high", "h_low"))
        h_low_v = m.sem("h_low_v")
        y_ps = [m.ps(f"y_ps{i}", [P, D]) for i in range(2)]
        w_in, wm_ready, h_done, leaked, h_ready, y_done, paired, summed, halved = (m.sem(a) for a in (
            "w_in", "wm_ready", "h_done", "leaked", "h_ready", "y_done", "paired", "summed", "halved"))
        norm = Norm(nc, m, out, summed, out_d, ident, nT)
        block = ctx.enter_context(nc.Block())

        def wait_low(eng, g, f):
            if f % 4 == 3:
                eng.wait_ge(h_low_v, KF // 4 * g + f // 4 + 1)
            else:
                eng.wait_ge(h_low, KF * 3 // 4 * g + f - f // 4 + 1)

        @block.sync
        def _(sp):
            sp.dma_start(wf[:, :, :], WfcT.rearrange("(k p) n -> p k n", p=P)).then_inc(w_in, 16)
            sp.dma_start(wm[:, :, :], WmlpT.rearrange("(k p) n -> p k n", p=P)).then_inc(w_in, 16)
            sp.dma_start(scale_row[:, :], row(scale).broadcast_to([P, D])).then_inc(w_in, 16)

            skewed(sp, 0, 0, lambda g, s: norm.store(sp, g, s))
            norm.finish(sp)

        @block.tensor
        def _(pe):
            def up(g, s, f):
                if f == 0:
                    pe.wait_ge(n_low, g + 1)
                if beyond(g, 0) or f > 3:
                    pe.wait_ge(leaked, KF * g + f - 3)
                for i, (k, (wp, np_)) in enumerate((k, t) for k in range(KD) for t in TERMS):
                    mm = nc.tensor.matmul(h_ps[f % 4][:, :], wf_part[wp][:, k, f * P:(f + 1) * P],
                                          n_part[s][np_][:, k, :], start=(i == 0), stop=(i == 3 * KD - 1))
                mm.then_inc(h_done, 1)

            def down(g, s):
                for f in (KF - 1, KF - 2):
                    wait_low(pe, g, f)
                for j in range(GT):
                    if not isinstance(g, int) or GT * g + j > 1:
                        pe.wait_ge(summed, GT * g + j - 1)
                    for i, (f, (hp, wp)) in enumerate((f, t) for f in range(KF) for t in TERMS):
                        mm = nc.tensor.matmul(y_ps[j % 2][:, :], h_part[hp][:, f, j * P:(j + 1) * P], wm_part[wp][:, f, :],
                                              start=(i == 0), stop=(i == 3 * KF - 1))
                    mm.then_inc(y_done, 1)

            pe.wait_ge(w_low, 2)

            def step(g, s):
                if exists(g):
                    for f in range(1, KF):
                        up(g, s, f)
                if exists(g + 1):
                    up(g + 1, 1 - s, 0)
                if exists(g - 2):
                    norm.turn(pe, g - 2, s)
                if exists(g):
                    down(g, s)

            skewed(pe, -1, 2, step, start=4)

        @block.scalar
        def _(act):
            act.wait_ge(w_in, 48)
            nc.scalar.copy(wf_part[0][:, :, :], wf[:, :, :]).then_inc(w_high, 1)
            act.wait_ge(wm_ready, 1)
            nc.scalar.copy(wm_part[0][:, :, :], wm[:, :, :]).then_inc(w_high, 1)

            def high_n(g, s):
                if beyond(g, 1):
                    act.wait_ge(h_done, KF * (g - 1))
                nc.scalar.copy(n_part[s][0][:, :, :], nT[:, :, bass.ds(g * GRP, GRP)]).then_inc(n_high, 1)

            def halve(g, f):
                act.wait_ge(h_done, KF * g + f + 1)
                if beyond(g, 0) or f > 1:
                    act.wait_ge(leaked, KF * g + f - 1)
                nc.scalar.activation(half[f % 2][:, :], h_ps[f % 4][:, :], ACT.Copy, scale=0.5).then_inc(halved, 1)

            def square(g, f):
                act.wait_ge(leaked, KF * g + f + 1)
                if beyond(g, 0) or f > 3:
                    wait_low(act, *((g, f - 4) if f > 3 else (g - 1, f + 4)))
                nc.scalar.activation(h[f % 4][:, :], leaky[f % 2][:, :], ACT.Square).then_inc(h_ready, 1)

            def step(g, s):
                if exists(g):
                    for f in range(1, KF + 1):
                        if f < KF:
                            halve(g, f)
                        if f > 1:
                            square(g, f - 1)
                if exists(g + 1):
                    halve(g + 1, 0)
                    square(g + 1, 0)
                if exists(g - 1):
                    norm.root(act, g - 1, 1 - s)
                if exists(g + 2):
                    high_n(g + 2, s)
                if exists(g - 2):
                    norm.copy(act, g - 2, s)

            skewed(act, -2, 2, step)

        @block.gpsimd
        def _(pool):
            def step(g, s):
                for f in [f for f in range(KF) if f % 4 != 3]:
                    pool.wait_ge(h_high, KF * g + f + 1)
                    nc.gpsimd.tensor_tensor(h_part[1][:, f, :], h[f % 4][:, :], h_part[0][:, f, :].bitcast(F32),
                                            ALU.subtract).then_inc(h_low, 1)

            skewed(pool, 0, 0, step)

        @block.vector
        def _(dve):
            norm.begin()
            dve.wait_ge(w_in, 48)
            nc.vector.tensor_tensor(wm[:, :, :], wm[:, :, :],
                                    scale_row[:, :].rearrange("p (a d) -> p a d", a=1).broadcast_to([P, KF, D]),
                                    ALU.mult).then_inc(wm_ready, 1)

            for i, (part, whole) in enumerate(((wf_part, wf), (wm_part, wm))):
                dve.wait_ge(w_high, i + 1)
                nc.vector.tensor_tensor(part[1][:, :, :], whole[:, :, :], part[0][:, :, :].bitcast(F32),
                                        ALU.subtract).then_inc(w_low, 1)

            def low_n(g, s):
                dve.wait_ge(n_high, g + 1)
                nc.vector.tensor_tensor(n_part[s][1][:, :, :], nT[:, :, bass.ds(g * GRP, GRP)],
                                        n_part[s][0][:, :, :].bitcast(F32), ALU.subtract).then_inc(n_low, 1)

            def leak(g, f):
                dve.wait_ge(halved, KF * g + f + 1)
                if beyond(g, 0) or f > 1:
                    dve.wait_ge(h_ready, KF * g + f - 1)
                nc.vector.tensor_tensor(leaky[f % 2][:, :], h_ps[f % 4][:, :], half[f % 2][:, :], ALU.max).then_inc(leaked, 1)

            def high_h(g, f):
                dve.wait_ge(h_ready, KF * g + f + 1)
                if f == 0 and beyond(g, 0):
                    dve.wait_ge(y_done, GT * g)
                nc.vector.tensor_copy(h_part[0][:, f, :], h[f % 4][:, :]).then_inc(h_high, 1)
                if f % 4 == 3:
                    dve.wait_ge(h_high, KF * g + f + 1)
                    nc.vector.tensor_tensor(h_part[1][:, f, :], h[f % 4][:, :], h_part[0][:, f, :].bitcast(F32),
                                            ALU.subtract).then_inc(h_low_v, 1)

            def add(g, s):
                if beyond(g, 1):
                    dve.wait_ge(norm.normed, GT * (g - 1))
                for j in range(GT):
                    dve.wait_ge(y_done, GT * g + j + 1)
                    nc.vector.tensor_tensor(out[s][:, j, :], y_ps[j % 2][:, :],
                                            x[:, bass.ds(g * GT + j, 1), :].rearrange("p a d -> p (a d)"),
                                            ALU.add).then_inc(summed, 1)

            def step(g, s):
                if exists(g):
                    high_h(g, 0)
                    for f in range(1, KF + 1):
                        if f < KF:
                            leak(g, f)
                        if f > 1:
                            high_h(g, f - 1)
                if exists(g + 1):
                    leak(g + 1, 0)
                if exists(g - 1):
                    norm.stats(dve, g - 1, 1 - s)
                    norm.apply(dve, g - 1, 1 - s)
                if exists(g + 2):
                    low_n(g + 2, s)
                if exists(g):
                    add(g, s)

            skewed(dve, -2, 1, step)




def network(nc, hidden, hidden_T, Wq, bq, Wk, bk, Wv, bv, gate0, up0, down0, shared1, shared2,
            mixk, mixv, mixr, mixo, decay, first_share, mix_scale, fc, mlp, mlp_scale,
            gate1, gate1_bias, w1, w2, w3, identity, upto_diagonal, out):
    TILES0 = (2 * T + E * (P - 1)) // P
    TILES0 += -TILES0 % 4
    CAPACITY = T * 5 // (4 * E)
    TILES1 = E * CAPACITY // P

    taken.clear()

    def scratch(name, *shape):
        return nc.dram_tensor(name, list(shape), F32).ap()

    rows = [scratch(f"rows{i}", T, D) for i in range(2)]
    part = scratch("part", T, D)
    expert_rows = [scratch("expert_rows0", TILES0 * P, D), scratch("expert_rows1", TILES1 * P + 1, D)]
    with ExitStack() as ctx:
        m = Mem(nc, ctx, "all")
        ident, upto = m.sb("ident", [P, P]), m.sb("upto", [P, P])
        loaded = m.sem("loaded")
        with nc.Block() as block:
            @block.sync
            def _(sp):
                sp.dma_start(ident[:, :], identity).then_inc(loaded, 16)
                sp.dma_start(upto[:, :], upto_diagonal).then_inc(loaded, 16)
                sp.wait_ge(loaded, 32)

        qk = scratch("qk", 2, 2, D, T)
        v = scratch("v", PAIRS, P, TT, 2 * VW)
        context, prob_sums = scratch("context", D, T), scratch("prob_sums", H, T)
        project_qkv(nc, hidden_T, Wq, bq, Wk, bk, Wv, bv, qk, v)
        attend(nc, qk, v, ident, context, prob_sums)

        weight, pos = m.sb("weight", [P, 2, TT]), m.sb("pos", [P, 2, TT], I32)
        table0, table1 = m.sb("table0", [P, TILES0], I32), m.sb("table1", [P, TILES1], I32)
        tile_expert = m.sb("tile_expert", [P, TILES0], I32)
        with ExitStack() as layer:
            m0 = Mem(nc, layer, "layer0")
            wu, wd = m0.sb("wu", [P, KD, E, up0.shape[2]]), m0.sb("wd", [P, up0.shape[2] // P, E, D])
            w_in = m0.sem("w_in")

            def prefetch0(sp):
                for to, of in ((wu, up0), (wd, down0)):
                    for k in range(to.shape[1]):
                        sp.dma_start(to[:, k, :, :], of[:, k * P:(k + 1) * P, :].rearrange("e p f -> p e f")).then_inc(w_in, 16)

            with ExitStack() as turned:
                xT = Mem(nc, turned, "turned0").sb("xT", [P, KD, T])
                merge_heads(nc, hidden, context, prob_sums, ident, rows[0], xT)
                route(nc, "route0", xT, gate0, None, ident, upto, None, weight, pos, table0, tile_expert, prefetch0,
                      (shared1, shared2, rows[0], part))
            experts_gelu(nc, rows[0], wu, wd, w_in, ident, table0, tile_expert, expert_rows[0])
        nc.clear_and_free_semaphores(taken)
        nc.all_engine_barrier()
        taken.clear()

        xT = Mem(nc, ctx, "turned1").sb("xT", [P, KD, T])
        with ExitStack() as layer:
            x = Mem(nc, layer, "layer1").sb("x", [P, TT, D])
            mix_tokens(nc, part, expert_rows[0], pos, weight, ident, mixk, mixv, mixr, mixo, decay, first_share,
                       mix_scale, x, xT)
            mix_channels(nc, xT, x, fc, mlp, mlp_scale, ident, rows[1])
        with ExitStack() as layer:
            m1 = Mem(nc, layer, "experts1")
            w12 = [m1.sb(f"w12{i}", [P, 2, KD, w1.shape[2]]) for i in range(2)]
            w3_in = [m1.sb(f"w3{i}", [P, w1.shape[2] // P, D]) for i in range(2)]
            w_in = [m1.sem(f"w_in{i}") for i in range(2)]

            def prefetch1(sp):
                for e in range(2):
                    load_expert(sp, e, e, w1, w2, w3, w12, w3_in, w_in)

            route(nc, "route1", xT, gate1, gate1_bias, ident, upto, CAPACITY, weight, pos, table1, None, prefetch1)
            experts_silu(nc, rows[1], w1, w2, w3, w12, w3_in, w_in, ident, table1, CAPACITY, expert_rows[1])
        combine(nc, rows[1], expert_rows[1], pos, weight, out)


def kernel(**inputs):
    import numpy as np
    import concourse.bacc as bacc
    from concourse import mybir as _mybir
    from concourse.bass_utils import run_bass_kernel_spmd

    def plain(name):
        return np.ascontiguousarray(inputs[name])

    def turned(name):
        return np.ascontiguousarray(np.asarray(inputs[name]).T)

    hidden = np.ascontiguousarray(np.asarray(inputs["L0_attn_hidden_states"]).reshape(T, D))
    arrays = [hidden, np.ascontiguousarray(hidden.T),
              turned("L0_attn_Wq"), plain("L0_attn_bq"), turned("L0_attn_Wk"), plain("L0_attn_bk"),
              turned("L0_attn_Wv"), plain("L0_attn_bv"),
              plain("L0_ffn_Wg"), plain("L0_ffn_Wu"), plain("L0_ffn_Wd"), plain("L0_ffn_W1"), plain("L0_ffn_W2"),
              turned("L1_attn_Wk"), turned("L1_attn_Wv"), turned("L1_attn_Wr"), turned("L1_attn_Wo"),
              plain("L1_attn_time_decay"), plain("L1_attn_time_first"), plain("L1_attn_mixer_scale"),
              turned("L1_attn_Wfc"), turned("L1_attn_Wmlp"), plain("L1_attn_mlp_scale"),
              plain("L1_ffn_Wg"), plain("L1_ffn_bg"), plain("L1_ffn_W1"), plain("L1_ffn_W2"), plain("L1_ffn_W3"),
              np.eye(P, dtype=np.float32), np.triu(np.ones((P, P), np.float32))]
    nc = bacc.Bacc("TRN2", target_bir_lowering=False, num_devices=1)
    named = {f"in_{i}_dram": a for i, a in enumerate(arrays)}
    args = [nc.dram_tensor(name, a.shape, _mybir.dt.from_np(a.dtype), kind="ExternalInput").ap()
            for name, a in named.items()]
    out = nc.dram_tensor("out_0_dram", (T, D), _mybir.dt.float32, kind="ExternalOutput").ap()
    network(nc, *args, out)
    result = run_bass_kernel_spmd(nc, [named], core_ids=[0])
    return result.results[0]["out_0_dram"].reshape(1, T, D)
```
